# Optimizing a Trainium2 kernel written in Bass

```python
import numpy as np
import jax
import jax.numpy as jnp

def _softmax(x, axis=-1):
    return jax.nn.softmax(x, axis=axis)

def _gelu(x):
    return jax.nn.gelu(x, approximate=True)

def _silu(x):
    return jax.nn.silu(x)

def _sigmoid(x):
    return jax.nn.sigmoid(x)

def _layernorm(x, axis=-1, eps=1e-05):
    m = jnp.mean(x, axis=axis, keepdims=True)
    v = jnp.var(x, axis=axis, keepdims=True)
    return (x - m) / jnp.sqrt(v + eps)

def _scatter_add(tgt, idx, src, axis=0):
    return tgt.at[idx].add(src)

def _segment_sum(src, seg, n):
    return jax.ops.segment_sum(src, seg, n)
kernel_name = 'mk_gps_d4_gnn_r16_392c74'

def setup_inputs(seed: int=0):
    np.random.seed(seed)
    _w = jnp.asarray

    def _rec_inputs():
        import jax
        import jax.numpy as jnp
        _gk = jax.random.key(seed)
        x = -6.415e-05 + 1 * jax.random.normal(jax.random.fold_in(_gk, 1), (625, 512), jnp.float32)
        _s = jax.random.randint(jax.random.fold_in(_gk, 2), (10000,), 0, 625, jnp.int32)
        _d = jax.random.randint(jax.random.fold_in(_gk, 3), (10000,), 0, 625, jnp.int32)
        _loop = jnp.arange(625, dtype=jnp.int32)
        src = jnp.concatenate([_s, _d, _loop])
        dst = jnp.concatenate([_d, _s, _loop])
        _o = jnp.argsort(dst, stable=True)
        src = src[_o]
        dst = dst[_o]
        edge_attr_32 = 6.40344e-05 + 1.00026 * jax.random.normal(jax.random.fold_in(_gk, 12), (20625, 32), jnp.float32)
        edge_attr_64 = 0.000196303 + 1.00016 * jax.random.normal(jax.random.fold_in(_gk, 13), (20625, 64), jnp.float32)
        edge_type_6 = jax.random.randint(jax.random.fold_in(_gk, 15), (20625,), 0, 6, jnp.int32)
        node_vec1 = jax.random.uniform(jax.random.fold_in(_gk, 16), (625, 1), jnp.float32, 0.0, 0.999957)
        return (x, src, dst, edge_attr_32, edge_attr_64, edge_type_6, node_vec1)
    x, src, dst, edge_attr_32, edge_attr_64, edge_type_6, node_vec1 = _rec_inputs()

    def _L0_gnn_setup():
        import jax, jax.numpy as jnp
        import numpy as np
        N, E, DM, H, DFF = (1250, 40000, 512, 8, 128)
        DK = DM // H

        def _layernorm(x, g, b, eps=1e-05):
            mu = jnp.mean(x, axis=-1, keepdims=True)
            var = jnp.mean(jnp.square(x - mu), axis=-1, keepdims=True)
            return (x - mu) * jax.lax.rsqrt(var + eps) * g + b
        key = jax.random.key(seed)
        ks = jax.random.split(key, 12)
        s = 0.02
        h = jax.random.normal(ks[0], (N, DM), dtype=jnp.float32)
        src = jax.random.randint(ks[1], (E,), 0, N, dtype=jnp.int32)
        dst = jnp.sort(jax.random.randint(ks[2], (E,), 0, N, dtype=jnp.int32))
        return {'h': h, 'src': src, 'dst': dst, 'Wq': jax.random.normal(ks[3], (DM, DM), dtype=jnp.float32) * s, 'Wk': jax.random.normal(ks[4], (DM, DM), dtype=jnp.float32) * s, 'Wv': jax.random.normal(ks[5], (DM, DM), dtype=jnp.float32) * s, 'Wo': jax.random.normal(ks[6], (DM, DM), dtype=jnp.float32) * s, 'ln1_g': jnp.ones((DM,), jnp.float32), 'ln1_b': jnp.zeros((DM,), jnp.float32), 'ln2_g': jnp.ones((DM,), jnp.float32), 'ln2_b': jnp.zeros((DM,), jnp.float32), 'W1': jax.random.normal(ks[7], (DM, DFF), dtype=jnp.float32) * s, 'b1': jnp.zeros((DFF,), jnp.float32), 'W2': jax.random.normal(ks[8], (DFF, DM), dtype=jnp.float32) * s, 'b2': jnp.zeros((DM,), jnp.float32)}
    _L0_gnn_all = _L0_gnn_setup()
    _L0_gnn_in = {k: v for k, v in _L0_gnn_all.items() if k in ('Wq', 'Wk', 'Wv', 'Wo', 'ln1_g', 'ln1_b', 'ln2_g', 'ln2_b', 'W1', 'b1', 'W2', 'b2')}
    del _L0_gnn_all

    def _L0_mix_setup():
        import jax, jax.numpy as jnp
        import numpy as np
        B, S, D, H, R, P = (4, 512, 512, 8, 64, 4)
        HD = D // H
        EPS = 1e-06

        def _sketch_p4(z, G1, G2):
            inv_sqrt_r = 1.0 / np.sqrt(R).astype(np.float32)
            half = inv_sqrt_r * (z @ G1 * (z @ G2))
            return half * half
        key = jax.random.key(seed)
        ks = jax.random.split(key, 16)
        lin = lambda k: jax.random.normal(k, (D, D), jnp.float32) * (1.0 / np.sqrt(D))
        g = lambda k: jax.random.normal(k, (HD, R), jnp.float32) * (1.0 / np.sqrt(R))
        return {'x': jax.random.normal(ks[0], (B, S, D), jnp.float32), 'Wq': lin(ks[1]), 'bq': jnp.zeros((D,), jnp.float32), 'Wk': lin(ks[2]), 'bk': jnp.zeros((D,), jnp.float32), 'Wv': lin(ks[3]), 'bv': jnp.zeros((D,), jnp.float32), 'Wp': lin(ks[4]), 'bp': jnp.zeros((D,), jnp.float32), 'gamma_q': jnp.ones((1,), jnp.float32), 'beta_q': jnp.zeros((1,), jnp.float32), 'gamma_k': jnp.ones((1,), jnp.float32), 'beta_k': jnp.zeros((1,), jnp.float32), 'qG1': g(ks[5]), 'qG2': g(ks[6]), 'kG1': g(ks[7]), 'kG2': g(ks[8])}
    _L0_mix_all = _L0_mix_setup()
    _L0_mix_in = {k: v for k, v in _L0_mix_all.items() if k in ('Wq', 'bq', 'Wk', 'bk', 'Wv', 'bv', 'Wp', 'bp', 'gamma_q', 'beta_q', 'gamma_k', 'beta_k', 'qG1', 'qG2', 'kG1', 'kG2')}
    del _L0_mix_all

    def _L0_ffn_setup():
        import jax, jax.numpy as jnp
        import numpy as np
        B, T, D = (4, 128, 512)
        E, H, K = (8, 512, 2)
        key = jax.random.key(seed)
        ks = jax.random.split(key, 8)
        s_in = 1.0 / np.sqrt(D)
        s_h = 1.0 / np.sqrt(H)
        return {'x': jax.random.normal(ks[0], (B, T, D), dtype=jnp.float32), 'Wg': jax.random.uniform(ks[1], (D, E), jnp.float32, -s_in, s_in), 'bg': jax.random.uniform(ks[2], (E,), jnp.float32, -s_in, s_in), 'W1': jax.random.uniform(ks[3], (E, D, H), jnp.float32, -s_in, s_in), 'b1': jax.random.uniform(ks[4], (E, H), jnp.float32, -s_in, s_in), 'W2': jax.random.uniform(ks[5], (E, H, H), jnp.float32, -s_h, s_h), 'b2': jax.random.uniform(ks[6], (E, H), jnp.float32, -s_h, s_h)}
    _L0_ffn_all = _L0_ffn_setup()
    _L0_ffn_in = {k: v for k, v in _L0_ffn_all.items() if k in ('Wg', 'bg', 'W1', 'b1', 'W2', 'b2')}
    del _L0_ffn_all

    def _L1_gnn_setup():
        import jax, jax.numpy as jnp
        import numpy as np
        N_NODES = 40962
        LATENT_DIM = 512
        N_EDGES = 40962
        NUM_BLOCKS = 4
        NUM_HEADS = 4
        NUM_FREQ = 32
        BASE_PERIOD = 16
        NOISE_EMB_DIM = 16
        EPS = 1e-05

        def _cond_layer_norm(x, cond, sw, sb, bw, bb):
            mu = jnp.mean(x, axis=-1, keepdims=True)
            var = jnp.var(x, axis=-1, keepdims=True)
            xn = (x - mu) * jax.lax.rsqrt(var + EPS)
            scale = cond @ sw + sb
            bias = cond @ bw + bb
            return xn * (1.0 + scale) + bias

        def _sparse_attention(x, src, dst, wq, bq, wk, bk, wv, bv, wo, bo):
            N, D = x.shape
            H, Dh = (NUM_HEADS, D // NUM_HEADS)
            q = (x @ wq + bq).reshape(N, H, Dh) * Dh ** (-0.5)
            k = (x @ wk + bk).reshape(N, H, Dh)
            v = (x @ wv + bv).reshape(N, H, Dh)
            scores = jnp.einsum('ehd,ehd->eh', q[src], k[dst])
            smax = jax.ops.segment_max(scores, src, num_segments=N)
            ex = jnp.exp(scores - smax[src])
            denom = jax.ops.segment_sum(ex, src, num_segments=N)
            attn = ex / denom[src]
            out = jax.ops.segment_sum(attn[:, :, None] * v[dst], src, num_segments=N)
            return out.reshape(N, D) @ wo + bo

        def _forward(x, edge_index, noise_levels, f_w1, f_b1, f_w2, f_b2, s1_w, s1_b, b1_w, b1_b, wq, bq, wk, bk, wv, bv, wo, bo, s2_w, s2_b, b2_w, b2_b, m_w1, m_b1, m_w2, m_b2):
            src, dst = (edge_index[0], edge_index[1])
            freqs = jnp.arange(1, NUM_FREQ + 1, dtype=x.dtype) * (2.0 * np.pi / BASE_PERIOD)
            ph = noise_levels * freqs
            emb = jnp.concatenate([jnp.sin(ph), jnp.cos(ph)], axis=-1)
            cond = jax.nn.silu(emb @ f_w1 + f_b1) @ f_w2 + f_b2
            for i in range(NUM_BLOCKS):
                y = _cond_layer_norm(x, cond, s1_w[i], s1_b[i], b1_w[i], b1_b[i])
                y = _sparse_attention(y, src, dst, wq[i], bq[i], wk[i], bk[i], wv[i], bv[i], wo[i], bo[i])
                x = x + y
                y = _cond_layer_norm(x, cond, s2_w[i], s2_b[i], b2_w[i], b2_b[i])
                y = jax.nn.relu(y @ m_w1[i] + m_b1[i]) @ m_w2[i] + m_b2[i]
                x = x + y
            return x
        key = jax.random.key(seed)
        ks = jax.random.split(key, 20)

        def w(k, shape, s=0.02):
            return jax.random.normal(k, shape, dtype=jnp.float32) * s
        D, B, C = (LATENT_DIM, NUM_BLOCKS, NOISE_EMB_DIM)
        z = lambda *s: jnp.zeros(s, jnp.float32)
        return {'latent_mesh_nodes': jax.random.normal(ks[0], (N_NODES, D), dtype=jnp.float32), 'edge_index': jax.random.randint(ks[1], (2, N_EDGES), 0, N_NODES, dtype=jnp.int32), 'noise_levels': jax.random.uniform(ks[2], (N_NODES, 1), dtype=jnp.float32), 'f_w1': w(ks[3], (2 * NUM_FREQ, C)), 'f_b1': z(C), 'f_w2': w(ks[4], (C, C)), 'f_b2': z(C), 's1_w': w(ks[5], (B, C, D)), 's1_b': z(B, D), 'b1_w': w(ks[6], (B, C, D)), 'b1_b': z(B, D), 'wq': w(ks[7], (B, D, D)), 'bq': z(B, D), 'wk': w(ks[8], (B, D, D)), 'bk': z(B, D), 'wv': w(ks[9], (B, D, D)), 'bv': z(B, D), 'wo': w(ks[10], (B, D, D)), 'bo': z(B, D), 's2_w': w(ks[11], (B, C, D)), 's2_b': z(B, D), 'b2_w': w(ks[12], (B, C, D)), 'b2_b': z(B, D), 'm_w1': w(ks[13], (B, D, D)), 'm_b1': z(B, D), 'm_w2': w(ks[14], (B, D, D)), 'm_b2': z(B, D)}
    _L1_gnn_all = _L1_gnn_setup()
    _L1_gnn_in = {k: v for k, v in _L1_gnn_all.items() if k in ('f_w1', 'f_b1', 'f_w2', 'f_b2', 's1_w', 's1_b', 'b1_w', 'b1_b', 'wq', 'bq', 'wk', 'bk', 'wv', 'bv', 'wo', 'bo', 's2_w', 's2_b', 'b2_w', 'b2_b', 'm_w1', 'm_b1', 'm_w2', 'm_b2')}
    del _L1_gnn_all

    def _L1_mix_setup():
        import jax, jax.numpy as jnp
        import numpy as np
        HEADS = 8
        EPS_LN = 1e-05
        EPS_NORM = 1e-08
        key = jax.random.key(seed)
        ks = jax.random.split(key, 3)
        B, N, C = (4, 512, 512)
        x = jax.random.normal(ks[0], (B, N, C), dtype=jnp.float32)
        qkv_w = jax.random.normal(ks[1], (3 * C, C), dtype=jnp.float32) / np.sqrt(C)
        qkv_b = jnp.zeros((3 * C,), dtype=jnp.float32)
        out_w = jax.random.normal(ks[2], (C, C), dtype=jnp.float32) / np.sqrt(C)
        out_b = jnp.zeros((C,), dtype=jnp.float32)
        ln_gamma = jnp.ones((C,), dtype=jnp.float32)
        ln_beta = jnp.zeros((C,), dtype=jnp.float32)
        return {'x': x, 'qkv_w': qkv_w, 'qkv_b': qkv_b, 'out_w': out_w, 'out_b': out_b, 'ln_gamma': ln_gamma, 'ln_beta': ln_beta}
    _L1_mix_all = _L1_mix_setup()
    _L1_mix_in = {k: v for k, v in _L1_mix_all.items() if k in ('qkv_w', 'qkv_b', 'out_w', 'out_b', 'ln_gamma', 'ln_beta')}
    del _L1_mix_all

    def _L1_ffn_setup():
        import jax, jax.numpy as jnp
        import numpy as np
        B, S, D = (2, 128, 512)
        E, H, TOP_K = (8, 1024, 2)
        SCALE = 1.0
        key = jax.random.key(seed)
        ks = jax.random.split(key, 7)
        s = lambda fan_in: 1.0 / np.sqrt(fan_in)
        return {'x': jax.random.normal(ks[0], (B, S, D), dtype=jnp.float32), 'gate_w': jax.random.normal(ks[1], (E, D), dtype=jnp.float32) * s(D), 'w1': jax.random.normal(ks[2], (E, H, D), dtype=jnp.float32) * s(D), 'w2': jax.random.normal(ks[3], (E, D, H), dtype=jnp.float32) * s(H), 'sg_gate': jax.random.normal(ks[4], (H, D), dtype=jnp.float32) * s(D), 'sg_up': jax.random.normal(ks[5], (H, D), dtype=jnp.float32) * s(D), 'sg_down': jax.random.normal(ks[6], (D, H), dtype=jnp.float32) * s(H)}
    _L1_ffn_all = _L1_ffn_setup()
    _L1_ffn_in = {k: v for k, v in _L1_ffn_all.items() if k in ('gate_w', 'w1', 'w2', 'sg_gate', 'sg_up', 'sg_down')}
    del _L1_ffn_all

    def _L2_gnn_setup():
        import jax, jax.numpy as jnp
        import numpy as np
        N_NODES = 3125
        N_EDGES = 25000
        EMBED = 512
        RBF = 64
        ANG = 32
        key = jax.random.key(seed)
        ks = jax.random.split(key, 10)
        x = jax.random.normal(ks[0], (N_NODES, EMBED), dtype=jnp.float32)
        edge_index = jax.random.randint(ks[1], (2, N_EDGES), 0, N_NODES, dtype=jnp.int64)
        rbf_feature = jax.random.normal(ks[2], (N_EDGES, RBF), dtype=jnp.float32)
        angle_feature = jax.random.normal(ks[3], (N_EDGES, ANG), dtype=jnp.float32)
        s_in = 1.0 / np.sqrt(RBF + ANG)
        s_e = 1.0 / np.sqrt(EMBED)
        W_edge = jax.random.uniform(ks[4], (RBF + ANG, EMBED), jnp.float32, -s_in, s_in)
        b_edge = jax.random.uniform(ks[5], (EMBED,), jnp.float32, -s_in, s_in)
        W1 = jax.random.uniform(ks[6], (EMBED, EMBED), jnp.float32, -s_e, s_e)
        b1 = jax.random.uniform(ks[7], (EMBED,), jnp.float32, -s_e, s_e)
        W2 = jax.random.uniform(ks[8], (EMBED, EMBED), jnp.float32, -s_e, s_e)
        b2 = jax.random.uniform(ks[9], (EMBED,), jnp.float32, -s_e, s_e)
        return {'x': x, 'edge_index': edge_index, 'rbf_feature': rbf_feature, 'angle_feature': angle_feature, 'W_edge': W_edge, 'b_edge': b_edge, 'W1': W1, 'b1': b1, 'W2': W2, 'b2': b2}
    _L2_gnn_all = _L2_gnn_setup()
    _L2_gnn_in = {k: v for k, v in _L2_gnn_all.items() if k in ('W_edge', 'b_edge', 'W1', 'b1', 'W2', 'b2')}
    del _L2_gnn_all

    def _L2_mix_setup():
        import jax, jax.numpy as jnp
        import numpy as np
        DIM = 512
        HEADS = 8
        HEAD_DIM = DIM // HEADS
        SCALE = HEAD_DIM ** (-0.5)

        def phi(t):
            return jax.nn.elu(t) + 1.0
        key = jax.random.key(seed)
        k1, k2, k3, k4 = jax.random.split(key, 4)
        B, N, C = (4, 512, DIM)
        x = jax.random.normal(k1, (B, N, C), dtype=jnp.float32)
        w_qkv = jax.random.normal(k2, (3 * C, C), dtype=jnp.float32) * (1.0 / np.sqrt(C))
        w_proj = jax.random.normal(k3, (C, C), dtype=jnp.float32) * (1.0 / np.sqrt(C))
        b_proj = jax.random.normal(k4, (C,), dtype=jnp.float32) * 0.01
        return {'x': x, 'w_qkv': w_qkv, 'w_proj': w_proj, 'b_proj': b_proj}
    _L2_mix_all = _L2_mix_setup()
    _L2_mix_in = {k: v for k, v in _L2_mix_all.items() if k in ('w_qkv', 'w_proj', 'b_proj')}
    del _L2_mix_all

    def _L2_ffn_setup():
        import jax, jax.numpy as jnp
        import numpy as np
        DIM = 512
        FFN_DIM = 1408
        GROUP = 128
        EPS = 1e-05

        def _quantize_weight(w, group_size):
            o, i = w.shape
            wg = w.reshape(o, i // group_size, group_size)
            scale = jnp.mean(jnp.abs(wg), axis=-1, keepdims=True) + EPS
            wq = jnp.clip(jnp.round(wg / scale), -1.0, 1.0) * scale
            return wq.reshape(o, i)

        def _bitlinear(x, w, group_size=GROUP):
            wq = w + jax.lax.stop_gradient(_quantize_weight(w, group_size) - w)
            return jnp.einsum('bsd,fd->bsf', x, wq)
        key = jax.random.key(seed)
        k_x, k_g, k_u, k_d = jax.random.split(key, 4)
        x = jax.random.normal(k_x, (8, 256, DIM), dtype=jnp.float32)
        sd_in = 1.0 / np.sqrt(DIM)
        sd_ffn = 1.0 / np.sqrt(FFN_DIM)
        w_gate = jax.random.normal(k_g, (FFN_DIM, DIM), dtype=jnp.float32) * sd_in
        w_up = jax.random.normal(k_u, (FFN_DIM, DIM), dtype=jnp.float32) * sd_in
        w_down = jax.random.normal(k_d, (DIM, FFN_DIM), dtype=jnp.float32) * sd_ffn
        return {'x': x, 'w_gate': w_gate, 'w_up': w_up, 'w_down': w_down}
    _L2_ffn_all = _L2_ffn_setup()
    _L2_ffn_in = {k: v for k, v in _L2_ffn_all.items() if k in ('w_gate', 'w_up', 'w_down')}
    del _L2_ffn_all

    def _L3_gnn_setup():
        import jax, jax.numpy as jnp
        import numpy as np
        N_NODES = 6250
        N_EDGES = 100000
        HIDDEN = 512
        LOWER = 128
        NUM_RELS = 6

        def _ngcn_layer(h, W, b, edge_src, edge_dst, edge_type, n_nodes):
            t = jnp.einsum('nd,rde->rne', h, W)
            msg = t[edge_type, edge_src]
            agg = jax.ops.segment_sum(msg, edge_dst, num_segments=n_nodes)
            return jax.nn.relu(agg + b)
        key = jax.random.key(seed)
        ks = jax.random.split(key, 16)
        glorot = lambda k, shape: jax.random.normal(k, shape, jnp.float32) * (2.0 / (shape[-2] + shape[-1])) ** 0.5
        return {'h_origin': jax.random.normal(ks[0], (N_NODES, HIDDEN), jnp.float32), 'edge_src': jax.random.randint(ks[1], (N_EDGES,), 0, N_NODES, jnp.int32), 'edge_dst': jax.random.randint(ks[2], (N_EDGES,), 0, N_NODES, jnp.int32), 'edge_type': jax.random.randint(ks[3], (N_EDGES,), 0, NUM_RELS, jnp.int32), 'W_lower': glorot(ks[4], (HIDDEN, LOWER)), 'b_lower': jnp.zeros((LOWER,), jnp.float32), 'W1': glorot(ks[5], (NUM_RELS, LOWER, LOWER)), 'b1': jnp.zeros((LOWER,), jnp.float32), 'W2': glorot(ks[6], (NUM_RELS, LOWER, LOWER)), 'b2': jnp.zeros((LOWER,), jnp.float32), 'W3': glorot(ks[7], (NUM_RELS, LOWER, LOWER)), 'b3': jnp.zeros((LOWER,), jnp.float32), 'W_upper': glorot(ks[8], (LOWER, HIDDEN)), 'b_upper': jnp.zeros((HIDDEN,), jnp.float32), 'W_skip': glorot(ks[9], (HIDDEN, HIDDEN)), 'b_skip': jnp.zeros((HIDDEN,), jnp.float32)}
    _L3_gnn_all = _L3_gnn_setup()
    _L3_gnn_in = {k: v for k, v in _L3_gnn_all.items() if k in ('W_lower', 'b_lower', 'W1', 'b1', 'W2', 'b2', 'W3', 'b3', 'W_upper', 'b_upper', 'W_skip', 'b_skip')}
    del _L3_gnn_all

    def _L3_mix_setup():
        import jax, jax.numpy as jnp
        import numpy as np
        NUM_HEADS = 8
        HEAD_DIM = 64
        EPS = 0.0001

        def _act(x):
            return jnp.where(x > 0, x + 1.0, jnp.exp(x))
        key = jax.random.key(seed)
        k1, k2, k3 = jax.random.split(key, 3)
        b, n, dim = (16, 256, 512)
        inner = NUM_HEADS * HEAD_DIM
        x = jax.random.normal(k1, (b, n, dim), dtype=jnp.float32)
        W_qkv = jax.random.normal(k2, (3 * inner, dim), dtype=jnp.float32) * dim ** (-0.5)
        W_out = jax.random.normal(k3, (dim, inner), dtype=jnp.float32) * inner ** (-0.5)
        b_out = jnp.zeros((dim,), dtype=jnp.float32)
        return {'x': x, 'W_qkv': W_qkv, 'W_out': W_out, 'b_out': b_out}
    _L3_mix_all = _L3_mix_setup()
    _L3_mix_in = {k: v for k, v in _L3_mix_all.items() if k in ('W_qkv', 'W_out', 'b_out')}
    del _L3_mix_all

    def _L3_ffn_setup():
        import jax, jax.numpy as jnp
        import numpy as np
        from jax import lax
        N, M, DIM, HEADS, TOPK = (4, 128, 512, 8, 16)

        def _split_heads(t, h):
            n, m, c = t.shape
            return t.reshape(n, m, h, c // h).transpose(0, 2, 1, 3).reshape(n * h, m, c // h)
        key = jax.random.key(seed)
        ks = jax.random.split(key, 7)
        f = lambda k, s, sc=1.0: jax.random.normal(k, s, dtype=jnp.float32) * sc
        return {'x': f(ks[0], (N, M, DIM)), 'pos_w': f(ks[1], (DIM, 1, 3), 0.1), 'pos_b': f(ks[2], (DIM,), 0.02), 'qkv_w': f(ks[3], (3 * DIM, DIM), 0.02), 'qkv_b': f(ks[4], (3 * DIM,), 0.02), 'wo_w': f(ks[5], (DIM, DIM), 0.02), 'wo_b': f(ks[6], (DIM,), 0.02)}
    _L3_ffn_all = _L3_ffn_setup()
    _L3_ffn_in = {k: v for k, v in _L3_ffn_all.items() if k in ('pos_w', 'pos_b', 'qkv_w', 'qkv_b', 'wo_w', 'wo_b')}
    del _L3_ffn_all
    return {'x': x, 'src': src, 'dst': dst, 'edge_attr_32': edge_attr_32, 'edge_attr_64': edge_attr_64, 'edge_type_6': edge_type_6, 'node_vec1': node_vec1, 'L0_gnn_Wq': _L0_gnn_in['Wq'], 'L0_gnn_Wk': _L0_gnn_in['Wk'], 'L0_gnn_Wv': _L0_gnn_in['Wv'], 'L0_gnn_Wo': _L0_gnn_in['Wo'], 'L0_gnn_ln1_g': _L0_gnn_in['ln1_g'], 'L0_gnn_ln1_b': _L0_gnn_in['ln1_b'], 'L0_gnn_ln2_g': _L0_gnn_in['ln2_g'], 'L0_gnn_ln2_b': _L0_gnn_in['ln2_b'], 'L0_gnn_W1': _L0_gnn_in['W1'], 'L0_gnn_b1': _L0_gnn_in['b1'], 'L0_gnn_W2': _L0_gnn_in['W2'], 'L0_gnn_b2': _L0_gnn_in['b2'], 'L0_mix_Wq': _L0_mix_in['Wq'], 'L0_mix_bq': _L0_mix_in['bq'], 'L0_mix_Wk': _L0_mix_in['Wk'], 'L0_mix_bk': _L0_mix_in['bk'], 'L0_mix_Wv': _L0_mix_in['Wv'], 'L0_mix_bv': _L0_mix_in['bv'], 'L0_mix_Wp': _L0_mix_in['Wp'], 'L0_mix_bp': _L0_mix_in['bp'], 'L0_mix_gamma_q': _L0_mix_in['gamma_q'], 'L0_mix_beta_q': _L0_mix_in['beta_q'], 'L0_mix_gamma_k': _L0_mix_in['gamma_k'], 'L0_mix_beta_k': _L0_mix_in['beta_k'], 'L0_mix_qG1': _L0_mix_in['qG1'], 'L0_mix_qG2': _L0_mix_in['qG2'], 'L0_mix_kG1': _L0_mix_in['kG1'], 'L0_mix_kG2': _L0_mix_in['kG2'], 'L0_ffn_Wg': _L0_ffn_in['Wg'], 'L0_ffn_bg': _L0_ffn_in['bg'], 'L0_ffn_W1': _L0_ffn_in['W1'], 'L0_ffn_b1': _L0_ffn_in['b1'], 'L0_ffn_W2': _L0_ffn_in['W2'], 'L0_ffn_b2': _L0_ffn_in['b2'], 'L1_gnn_f_w1': _L1_gnn_in['f_w1'], 'L1_gnn_f_b1': _L1_gnn_in['f_b1'], 'L1_gnn_f_w2': _L1_gnn_in['f_w2'], 'L1_gnn_f_b2': _L1_gnn_in['f_b2'], 'L1_gnn_s1_w': _L1_gnn_in['s1_w'], 'L1_gnn_s1_b': _L1_gnn_in['s1_b'], 'L1_gnn_b1_w': _L1_gnn_in['b1_w'], 'L1_gnn_b1_b': _L1_gnn_in['b1_b'], 'L1_gnn_wq': _L1_gnn_in['wq'], 'L1_gnn_bq': _L1_gnn_in['bq'], 'L1_gnn_wk': _L1_gnn_in['wk'], 'L1_gnn_bk': _L1_gnn_in['bk'], 'L1_gnn_wv': _L1_gnn_in['wv'], 'L1_gnn_bv': _L1_gnn_in['bv'], 'L1_gnn_wo': _L1_gnn_in['wo'], 'L1_gnn_bo': _L1_gnn_in['bo'], 'L1_gnn_s2_w': _L1_gnn_in['s2_w'], 'L1_gnn_s2_b': _L1_gnn_in['s2_b'], 'L1_gnn_b2_w': _L1_gnn_in['b2_w'], 'L1_gnn_b2_b': _L1_gnn_in['b2_b'], 'L1_gnn_m_w1': _L1_gnn_in['m_w1'], 'L1_gnn_m_b1': _L1_gnn_in['m_b1'], 'L1_gnn_m_w2': _L1_gnn_in['m_w2'], 'L1_gnn_m_b2': _L1_gnn_in['m_b2'], 'L1_mix_qkv_w': _L1_mix_in['qkv_w'], 'L1_mix_qkv_b': _L1_mix_in['qkv_b'], 'L1_mix_out_w': _L1_mix_in['out_w'], 'L1_mix_out_b': _L1_mix_in['out_b'], 'L1_mix_ln_gamma': _L1_mix_in['ln_gamma'], 'L1_mix_ln_beta': _L1_mix_in['ln_beta'], 'L1_ffn_gate_w': _L1_ffn_in['gate_w'], 'L1_ffn_w1': _L1_ffn_in['w1'], 'L1_ffn_w2': _L1_ffn_in['w2'], 'L1_ffn_sg_gate': _L1_ffn_in['sg_gate'], 'L1_ffn_sg_up': _L1_ffn_in['sg_up'], 'L1_ffn_sg_down': _L1_ffn_in['sg_down'], 'L2_gnn_W_edge': _L2_gnn_in['W_edge'], 'L2_gnn_b_edge': _L2_gnn_in['b_edge'], 'L2_gnn_W1': _L2_gnn_in['W1'], 'L2_gnn_b1': _L2_gnn_in['b1'], 'L2_gnn_W2': _L2_gnn_in['W2'], 'L2_gnn_b2': _L2_gnn_in['b2'], 'L2_mix_w_qkv': _L2_mix_in['w_qkv'], 'L2_mix_w_proj': _L2_mix_in['w_proj'], 'L2_mix_b_proj': _L2_mix_in['b_proj'], 'L2_ffn_w_gate': _L2_ffn_in['w_gate'], 'L2_ffn_w_up': _L2_ffn_in['w_up'], 'L2_ffn_w_down': _L2_ffn_in['w_down'], 'L3_gnn_W_lower': _L3_gnn_in['W_lower'], 'L3_gnn_b_lower': _L3_gnn_in['b_lower'], 'L3_gnn_W1': _L3_gnn_in['W1'], 'L3_gnn_b1': _L3_gnn_in['b1'], 'L3_gnn_W2': _L3_gnn_in['W2'], 'L3_gnn_b2': _L3_gnn_in['b2'], 'L3_gnn_W3': _L3_gnn_in['W3'], 'L3_gnn_b3': _L3_gnn_in['b3'], 'L3_gnn_W_upper': _L3_gnn_in['W_upper'], 'L3_gnn_b_upper': _L3_gnn_in['b_upper'], 'L3_gnn_W_skip': _L3_gnn_in['W_skip'], 'L3_gnn_b_skip': _L3_gnn_in['b_skip'], 'L3_mix_W_qkv': _L3_mix_in['W_qkv'], 'L3_mix_W_out': _L3_mix_in['W_out'], 'L3_mix_b_out': _L3_mix_in['b_out'], 'L3_ffn_pos_w': _L3_ffn_in['pos_w'], 'L3_ffn_pos_b': _L3_ffn_in['pos_b'], 'L3_ffn_qkv_w': _L3_ffn_in['qkv_w'], 'L3_ffn_qkv_b': _L3_ffn_in['qkv_b'], 'L3_ffn_wo_w': _L3_ffn_in['wo_w'], 'L3_ffn_wo_b': _L3_ffn_in['wo_b']}

def reference(x, src, dst, edge_attr_32, edge_attr_64, edge_type_6, node_vec1, L0_gnn_Wq, L0_gnn_Wk, L0_gnn_Wv, L0_gnn_Wo, L0_gnn_ln1_g, L0_gnn_ln1_b, L0_gnn_ln2_g, L0_gnn_ln2_b, L0_gnn_W1, L0_gnn_b1, L0_gnn_W2, L0_gnn_b2, L0_mix_Wq, L0_mix_bq, L0_mix_Wk, L0_mix_bk, L0_mix_Wv, L0_mix_bv, L0_mix_Wp, L0_mix_bp, L0_mix_gamma_q, L0_mix_beta_q, L0_mix_gamma_k, L0_mix_beta_k, L0_mix_qG1, L0_mix_qG2, L0_mix_kG1, L0_mix_kG2, L0_ffn_Wg, L0_ffn_bg, L0_ffn_W1, L0_ffn_b1, L0_ffn_W2, L0_ffn_b2, L1_gnn_f_w1, L1_gnn_f_b1, L1_gnn_f_w2, L1_gnn_f_b2, L1_gnn_s1_w, L1_gnn_s1_b, L1_gnn_b1_w, L1_gnn_b1_b, L1_gnn_wq, L1_gnn_bq, L1_gnn_wk, L1_gnn_bk, L1_gnn_wv, L1_gnn_bv, L1_gnn_wo, L1_gnn_bo, L1_gnn_s2_w, L1_gnn_s2_b, L1_gnn_b2_w, L1_gnn_b2_b, L1_gnn_m_w1, L1_gnn_m_b1, L1_gnn_m_w2, L1_gnn_m_b2, L1_mix_qkv_w, L1_mix_qkv_b, L1_mix_out_w, L1_mix_out_b, L1_mix_ln_gamma, L1_mix_ln_beta, L1_ffn_gate_w, L1_ffn_w1, L1_ffn_w2, L1_ffn_sg_gate, L1_ffn_sg_up, L1_ffn_sg_down, L2_gnn_W_edge, L2_gnn_b_edge, L2_gnn_W1, L2_gnn_b1, L2_gnn_W2, L2_gnn_b2, L2_mix_w_qkv, L2_mix_w_proj, L2_mix_b_proj, L2_ffn_w_gate, L2_ffn_w_up, L2_ffn_w_down, L3_gnn_W_lower, L3_gnn_b_lower, L3_gnn_W1, L3_gnn_b1, L3_gnn_W2, L3_gnn_b2, L3_gnn_W3, L3_gnn_b3, L3_gnn_W_upper, L3_gnn_b_upper, L3_gnn_W_skip, L3_gnn_b_skip, L3_mix_W_qkv, L3_mix_W_out, L3_mix_b_out, L3_ffn_pos_w, L3_ffn_pos_b, L3_ffn_qkv_w, L3_ffn_qkv_b, L3_ffn_wo_w, L3_ffn_wo_b):
    import jax
    import jax.numpy as jnp

    def _L0_gnn_ref(h, src, dst, Wq, Wk, Wv, Wo, ln1_g, ln1_b, ln2_g, ln2_b, W1, b1, W2, b2):
        import jax, jax.numpy as jnp
        import numpy as np
        N, E, DM, H, DFF = (1250, 40000, 512, 8, 128)
        DK = DM // H

        def _layernorm(x, g, b, eps=1e-05):
            mu = jnp.mean(x, axis=-1, keepdims=True)
            var = jnp.mean(jnp.square(x - mu), axis=-1, keepdims=True)
            return (x - mu) * jax.lax.rsqrt(var + eps) * g + b
        n = h.shape[0]
        q = (h @ Wq).reshape(n, H, DK)
        k = (h @ Wk).reshape(n, H, DK)
        v = (h @ Wv).reshape(n, H, DK)
        e = jnp.einsum('ehd,ehd->eh', k[src], q[dst]) / np.sqrt(DK).astype(np.float32)
        m = jax.ops.segment_max(e, dst, num_segments=n)
        ex = jnp.exp(e - m[dst])
        z = jax.ops.segment_sum(ex, dst, num_segments=n)
        attn = ex / z[dst]
        a = jax.ops.segment_sum(attn[:, :, None] * v[src], dst, num_segments=n)
        a = a.reshape(n, DM)
        o = a @ Wo
        x = _layernorm(h + o, ln1_g, ln1_b)
        f = jax.nn.relu(x @ W1 + b1) @ W2 + b2
        return _layernorm(x + f, ln2_g, ln2_b)

    def _L0_mix_ref(x, Wq, bq, Wk, bk, Wv, bv, Wp, bp, gamma_q, beta_q, gamma_k, beta_k, qG1, qG2, kG1, kG2):
        import jax, jax.numpy as jnp
        import numpy as np
        B, S, D, H, R, P = (4, 512, 512, 8, 64, 4)
        HD = D // H
        EPS = 1e-06

        def _sketch_p4(z, G1, G2):
            inv_sqrt_r = 1.0 / np.sqrt(R).astype(np.float32)
            half = inv_sqrt_r * (z @ G1 * (z @ G2))
            return half * half
        b, s, d = x.shape
        split = lambda t: t.reshape(b, s, H, HD).transpose(0, 2, 1, 3)
        q = split(x @ Wq + bq)
        k = split(x @ Wk + bk)
        v = split(x @ Wv + bv)
        q = gamma_q * q + beta_q
        k = gamma_k * k + beta_k
        phi_q = _sketch_p4(q, qG1, qG2)
        phi_k = _sketch_p4(k, kG1, kG2)
        kv = jnp.einsum('bhsr,bhsd->bhrd', phi_k, v)
        ksum = phi_k.sum(axis=2)
        num = jnp.einsum('bhqr,bhrd->bhqd', phi_q, kv)
        den = jnp.einsum('bhqr,bhr->bhq', phi_q, ksum) + EPS
        out = num / den[..., None]
        out = out.transpose(0, 2, 1, 3).reshape(b, s, d)
        return out @ Wp + bp

    def _L0_ffn_ref(x, Wg, bg, W1, b1, W2, b2):
        import jax, jax.numpy as jnp
        import numpy as np
        B, T, D = (4, 128, 512)
        E, H, K = (8, 512, 2)
        Bx, Tx, Dx = x.shape
        xf = x.reshape(-1, Dx)
        logits = xf @ Wg + bg
        topk_scores, topk_idx = jax.lax.top_k(logits, K)
        topk_w = jax.nn.softmax(topk_scores, axis=-1)
        h = jax.nn.gelu(jnp.einsum('nd,edh->neh', xf, W1) + b1, approximate=False)
        y = jnp.einsum('neh,ehf->nef', h, W2) + b2
        sel = jnp.take_along_axis(y, topk_idx[:, :, None], axis=1)
        out = jnp.sum(topk_w[:, :, None] * sel, axis=1)
        return out.reshape(Bx, Tx, -1)

    def _L1_gnn_ref(latent_mesh_nodes, edge_index, noise_levels, f_w1, f_b1, f_w2, f_b2, s1_w, s1_b, b1_w, b1_b, wq, bq, wk, bk, wv, bv, wo, bo, s2_w, s2_b, b2_w, b2_b, m_w1, m_b1, m_w2, m_b2):
        import jax, jax.numpy as jnp
        import numpy as np
        N_NODES = 40962
        LATENT_DIM = 512
        N_EDGES = 40962
        NUM_BLOCKS = 4
        NUM_HEADS = 4
        NUM_FREQ = 32
        BASE_PERIOD = 16
        NOISE_EMB_DIM = 16
        EPS = 1e-05

        def _cond_layer_norm(x, cond, sw, sb, bw, bb):
            mu = jnp.mean(x, axis=-1, keepdims=True)
            var = jnp.var(x, axis=-1, keepdims=True)
            xn = (x - mu) * jax.lax.rsqrt(var + EPS)
            scale = cond @ sw + sb
            bias = cond @ bw + bb
            return xn * (1.0 + scale) + bias

        def _sparse_attention(x, src, dst, wq, bq, wk, bk, wv, bv, wo, bo):
            N, D = x.shape
            H, Dh = (NUM_HEADS, D // NUM_HEADS)
            q = (x @ wq + bq).reshape(N, H, Dh) * Dh ** (-0.5)
            k = (x @ wk + bk).reshape(N, H, Dh)
            v = (x @ wv + bv).reshape(N, H, Dh)
            scores = jnp.einsum('ehd,ehd->eh', q[src], k[dst])
            smax = jax.ops.segment_max(scores, src, num_segments=N)
            ex = jnp.exp(scores - smax[src])
            denom = jax.ops.segment_sum(ex, src, num_segments=N)
            attn = ex / denom[src]
            out = jax.ops.segment_sum(attn[:, :, None] * v[dst], src, num_segments=N)
            return out.reshape(N, D) @ wo + bo

        def _forward(x, edge_index, noise_levels, f_w1, f_b1, f_w2, f_b2, s1_w, s1_b, b1_w, b1_b, wq, bq, wk, bk, wv, bv, wo, bo, s2_w, s2_b, b2_w, b2_b, m_w1, m_b1, m_w2, m_b2):
            src, dst = (edge_index[0], edge_index[1])
            freqs = jnp.arange(1, NUM_FREQ + 1, dtype=x.dtype) * (2.0 * np.pi / BASE_PERIOD)
            ph = noise_levels * freqs
            emb = jnp.concatenate([jnp.sin(ph), jnp.cos(ph)], axis=-1)
            cond = jax.nn.silu(emb @ f_w1 + f_b1) @ f_w2 + f_b2
            for i in range(NUM_BLOCKS):
                y = _cond_layer_norm(x, cond, s1_w[i], s1_b[i], b1_w[i], b1_b[i])
                y = _sparse_attention(y, src, dst, wq[i], bq[i], wk[i], bk[i], wv[i], bv[i], wo[i], bo[i])
                x = x + y
                y = _cond_layer_norm(x, cond, s2_w[i], s2_b[i], b2_w[i], b2_b[i])
                y = jax.nn.relu(y @ m_w1[i] + m_b1[i]) @ m_w2[i] + m_b2[i]
                x = x + y
            return x
        return _forward(latent_mesh_nodes, edge_index, noise_levels, f_w1, f_b1, f_w2, f_b2, s1_w, s1_b, b1_w, b1_b, wq, bq, wk, bk, wv, bv, wo, bo, s2_w, s2_b, b2_w, b2_b, m_w1, m_b1, m_w2, m_b2)

    def _L1_mix_ref(x, qkv_w, qkv_b, out_w, out_b, ln_gamma, ln_beta):
        import jax, jax.numpy as jnp
        import numpy as np
        HEADS = 8
        EPS_LN = 1e-05
        EPS_NORM = 1e-08
        B, N, C = x.shape
        h = HEADS
        d = C // h
        residual = x
        mu = jnp.mean(x, axis=-1, keepdims=True)
        var = jnp.var(x, axis=-1, keepdims=True)
        xn = (x - mu) / jnp.sqrt(var + EPS_LN) * ln_gamma + ln_beta
        qkv = xn @ qkv_w.T + qkv_b
        qkv = qkv.reshape(B, N, 3, h, d).transpose(2, 0, 3, 1, 4)
        q, k, v = (qkv[0], qkv[1], qkv[2])
        q = jax.nn.elu(q) + 1.0
        k = jax.nn.elu(k) + 1.0
        kv = jnp.einsum('bhnd,bhne->bhde', k, v)
        k_sum = jnp.sum(k, axis=2)
        out = jnp.einsum('bhnd,bhde->bhne', q, kv)
        normalizer = jnp.einsum('bhnd,bhd->bhn', q, k_sum)
        out = out / (normalizer[..., None] + EPS_NORM)
        out = out.transpose(0, 2, 1, 3).reshape(B, N, C)
        out = out @ out_w.T + out_b
        return out + residual

    def _L1_ffn_ref(x, gate_w, w1, w2, sg_gate, sg_up, sg_down):
        import jax, jax.numpy as jnp
        import numpy as np
        B, S, D = (2, 128, 512)
        E, H, TOP_K = (8, 1024, 2)
        SCALE = 1.0
        b, s_len, d = x.shape
        xf = x.reshape(-1, d)
        n = xf.shape[0]
        logits = xf @ gate_w.T * SCALE
        topk_w, idx = jax.lax.top_k(logits, TOP_K)
        topk_w = jax.nn.softmax(topk_w, axis=-1)
        comb = jnp.zeros((n, E), dtype=xf.dtype).at[jnp.arange(n)[:, None], idx].add(topk_w)
        h = jax.nn.silu(jnp.einsum('td,ehd->teh', xf, w1))
        eo = jnp.einsum('teh,edh->ted', h, w2)
        routed = jnp.einsum('te,ted->td', comb, eo)
        shared = jax.nn.silu(xf @ sg_gate.T) * (xf @ sg_up.T) @ sg_down.T
        return (routed + shared).reshape(b, s_len, d)

    def _L2_gnn_ref(x, edge_index, rbf_feature, angle_feature, W_edge, b_edge, W1, b1, W2, b2):
        import jax, jax.numpy as jnp
        import numpy as np
        N_NODES = 3125
        N_EDGES = 25000
        EMBED = 512
        RBF = 64
        ANG = 32
        row = edge_index[0]
        edge_feat = jnp.concatenate([rbf_feature, angle_feature], axis=-1)
        msg = edge_feat @ W_edge + b_edge
        agg = jax.ops.segment_sum(msg, row, num_segments=x.shape[0])
        h = jax.nn.relu(agg @ W1 + b1)
        return x + h @ W2 + b2

    def _L2_mix_ref(x, w_qkv, w_proj, b_proj):
        import jax, jax.numpy as jnp
        import numpy as np
        DIM = 512
        HEADS = 8
        HEAD_DIM = DIM // HEADS
        SCALE = HEAD_DIM ** (-0.5)

        def phi(t):
            return jax.nn.elu(t) + 1.0
        B, N, C = x.shape
        H, D = (HEADS, C // HEADS)
        qkv = x @ w_qkv.T
        qkv = qkv.reshape(B, N, 3, H, D).transpose(2, 0, 3, 1, 4)
        q, k, v = (qkv[0], qkv[1], qkv[2])
        kv = jnp.einsum('bhnd,bhne->bhde', phi(k), v) * SCALE
        out = jnp.einsum('bhnd,bhde->bhne', phi(q), kv)
        out = out.transpose(0, 2, 1, 3).reshape(B, N, C)
        return out @ w_proj.T + b_proj

    def _L2_ffn_ref(x, w_gate, w_up, w_down):
        import jax, jax.numpy as jnp
        import numpy as np
        DIM = 512
        FFN_DIM = 1408
        GROUP = 128
        EPS = 1e-05

        def _quantize_weight(w, group_size):
            o, i = w.shape
            wg = w.reshape(o, i // group_size, group_size)
            scale = jnp.mean(jnp.abs(wg), axis=-1, keepdims=True) + EPS
            wq = jnp.clip(jnp.round(wg / scale), -1.0, 1.0) * scale
            return wq.reshape(o, i)

        def _bitlinear(x, w, group_size=GROUP):
            wq = w + jax.lax.stop_gradient(_quantize_weight(w, group_size) - w)
            return jnp.einsum('bsd,fd->bsf', x, wq)
        gate = _bitlinear(x, w_gate)
        up = _bitlinear(x, w_up)
        h = jax.nn.silu(gate) * up
        return _bitlinear(h, w_down)

    def _L3_gnn_ref(h_origin, edge_src, edge_dst, edge_type, W_lower, b_lower, W1, b1, W2, b2, W3, b3, W_upper, b_upper, W_skip, b_skip):
        import jax, jax.numpy as jnp
        import numpy as np
        N_NODES = 6250
        N_EDGES = 100000
        HIDDEN = 512
        LOWER = 128
        NUM_RELS = 6

        def _ngcn_layer(h, W, b, edge_src, edge_dst, edge_type, n_nodes):
            t = jnp.einsum('nd,rde->rne', h, W)
            msg = t[edge_type, edge_src]
            agg = jax.ops.segment_sum(msg, edge_dst, num_segments=n_nodes)
            return jax.nn.relu(agg + b)
        n_nodes = h_origin.shape[0]
        h = jax.nn.relu(h_origin @ W_lower + b_lower)
        h = _ngcn_layer(h, W1, b1, edge_src, edge_dst, edge_type, n_nodes)
        h = _ngcn_layer(h, W2, b2, edge_src, edge_dst, edge_type, n_nodes)
        h = _ngcn_layer(h, W3, b3, edge_src, edge_dst, edge_type, n_nodes)
        out = jax.nn.relu(h @ W_upper + b_upper) + jax.nn.relu(h_origin @ W_skip + b_skip)
        return out

    def _L3_mix_ref(x, W_qkv, W_out, b_out):
        import jax, jax.numpy as jnp
        import numpy as np
        NUM_HEADS = 8
        HEAD_DIM = 64
        EPS = 0.0001

        def _act(x):
            return jnp.where(x > 0, x + 1.0, jnp.exp(x))
        b, n, dim = x.shape
        inner = NUM_HEADS * HEAD_DIM
        qkv = x @ W_qkv.T
        q, k, v = jnp.split(qkv, 3, axis=-1)

        def to_heads(t):
            return t.reshape(b, n, NUM_HEADS, HEAD_DIM).transpose(0, 2, 1, 3)
        q, k, v = (to_heads(q), to_heads(k), to_heads(v))
        q = _act(q)
        k = _act(k)
        kv = jnp.einsum('bhnd,bhne->bhde', k, v)
        k_sum = k.sum(axis=-2)
        z = 1.0 / jnp.maximum(jnp.einsum('bhnd,bhd->bhn', q, k_sum), EPS)
        out = jnp.einsum('bhnd,bhde,bhn->bhne', q, kv, z)
        out = out.transpose(0, 2, 1, 3).reshape(b, n, inner)
        return out @ W_out.T + b_out

    def _L3_ffn_ref(x, pos_w, pos_b, qkv_w, qkv_b, wo_w, wo_b):
        import jax, jax.numpy as jnp
        import numpy as np
        from jax import lax
        N, M, DIM, HEADS, TOPK = (4, 128, 512, 8, 16)

        def _split_heads(t, h):
            n, m, c = t.shape
            return t.reshape(n, m, h, c // h).transpose(0, 2, 1, 3).reshape(n * h, m, c // h)
        n, m, c = x.shape
        h = HEADS
        scale = c ** (-0.5)
        pos = lax.conv_general_dilated(x.transpose(0, 2, 1), pos_w, window_strides=(1,), padding=[(1, 1)], feature_group_count=c, dimension_numbers=('NCH', 'OIH', 'NCH'))
        x = x + (pos + pos_b[None, :, None]).transpose(0, 2, 1)
        qkv = x @ qkv_w.T + qkv_b
        q, k, v = jnp.split(qkv, [c, 2 * c], axis=-1)
        q = _split_heads(q, h)
        k = _split_heads(k, h)
        v = _split_heads(v, h)
        qd = lax.stop_gradient(q)
        kd = lax.stop_gradient(k)
        logits = jnp.einsum('bmd,bpd->bmp', qd * scale, kd)
        _, idx = lax.top_k(logits, TOPK)
        gather = jax.vmap(lambda t, i: t[i])
        k_sel = gather(k, idx)
        v_sel = gather(v, idx)
        attn = jax.nn.softmax(jnp.einsum('bmd,bmkd->bmk', q * scale, k_sel), axis=-1)
        out = jnp.einsum('bmk,bmkd->bmd', attn, v_sel)
        d = c // h
        out = out.reshape(n, h, m, d).transpose(0, 2, 1, 3).reshape(n, m, c)
        return out @ wo_w.T + wo_b
    edge_index = jnp.stack([src, dst])
    xn = _layernorm(x, axis=-1)
    x = x + _L0_gnn_ref(xn, src, dst, L0_gnn_Wq, L0_gnn_Wk, L0_gnn_Wv, L0_gnn_Wo, L0_gnn_ln1_g, L0_gnn_ln1_b, L0_gnn_ln2_g, L0_gnn_ln2_b, L0_gnn_W1, L0_gnn_b1, L0_gnn_W2, L0_gnn_b2) + _L0_mix_ref(xn[None], L0_mix_Wq, L0_mix_bq, L0_mix_Wk, L0_mix_bk, L0_mix_Wv, L0_mix_bv, L0_mix_Wp, L0_mix_bp, L0_mix_gamma_q, L0_mix_beta_q, L0_mix_gamma_k, L0_mix_beta_k, L0_mix_qG1, L0_mix_qG2, L0_mix_kG1, L0_mix_kG2)[0]
    x = x + _L0_ffn_ref(_layernorm(x, axis=-1)[None], L0_ffn_Wg, L0_ffn_bg, L0_ffn_W1, L0_ffn_b1, L0_ffn_W2, L0_ffn_b2)[0]
    xn = _layernorm(x, axis=-1)
    x = x + _L1_gnn_ref(xn, edge_index, node_vec1, L1_gnn_f_w1, L1_gnn_f_b1, L1_gnn_f_w2, L1_gnn_f_b2, L1_gnn_s1_w, L1_gnn_s1_b, L1_gnn_b1_w, L1_gnn_b1_b, L1_gnn_wq, L1_gnn_bq, L1_gnn_wk, L1_gnn_bk, L1_gnn_wv, L1_gnn_bv, L1_gnn_wo, L1_gnn_bo, L1_gnn_s2_w, L1_gnn_s2_b, L1_gnn_b2_w, L1_gnn_b2_b, L1_gnn_m_w1, L1_gnn_m_b1, L1_gnn_m_w2, L1_gnn_m_b2) + _L1_mix_ref(xn[None], L1_mix_qkv_w, L1_mix_qkv_b, L1_mix_out_w, L1_mix_out_b, L1_mix_ln_gamma, L1_mix_ln_beta)[0]
    x = x + _L1_ffn_ref(_layernorm(x, axis=-1)[None], L1_ffn_gate_w, L1_ffn_w1, L1_ffn_w2, L1_ffn_sg_gate, L1_ffn_sg_up, L1_ffn_sg_down)[0]
    xn = _layernorm(x, axis=-1)
    x = x + _L2_gnn_ref(xn, edge_index, edge_attr_64, edge_attr_32, L2_gnn_W_edge, L2_gnn_b_edge, L2_gnn_W1, L2_gnn_b1, L2_gnn_W2, L2_gnn_b2) + _L2_mix_ref(xn[None], L2_mix_w_qkv, L2_mix_w_proj, L2_mix_b_proj)[0]
    x = x + _L2_ffn_ref(_layernorm(x, axis=-1)[None], L2_ffn_w_gate, L2_ffn_w_up, L2_ffn_w_down)[0]
    xn = _layernorm(x, axis=-1)
    x = x + _L3_gnn_ref(xn, src, dst, edge_type_6, L3_gnn_W_lower, L3_gnn_b_lower, L3_gnn_W1, L3_gnn_b1, L3_gnn_W2, L3_gnn_b2, L3_gnn_W3, L3_gnn_b3, L3_gnn_W_upper, L3_gnn_b_upper, L3_gnn_W_skip, L3_gnn_b_skip) + _L3_mix_ref(xn[None], L3_mix_W_qkv, L3_mix_W_out, L3_mix_b_out)[0]
    x = x + _L3_ffn_ref(_layernorm(x, axis=-1)[None], L3_ffn_pos_w, L3_ffn_pos_b, L3_ffn_qkv_w, L3_ffn_qkv_b, L3_ffn_wo_w, L3_ffn_wo_b)[0]
    return x

_drawn_inputs = setup_inputs


def setup_inputs(seed=0):
    import zlib

    import numpy as np

    out = dict(_drawn_inputs(seed))
    spreads = {'L0_gnn_ln1_g': (1.0, 0.6),
     'L0_gnn_ln1_b': (0.0, 0.1),
     'L0_gnn_ln2_g': (1.0, 0.2),
     'L0_gnn_ln2_b': (0.0, 0.1),
     'L0_gnn_b1': (0.0, 0.717),
     'L0_gnn_b2': (0.0, 0.1),
     'L0_mix_bq': (0.0, 2.0),
     'L0_mix_bk': (0.0, 2.0),
     'L0_mix_bv': (0.0, 0.1),
     'L0_mix_bp': (0.0, 0.1),
     'L1_gnn_f_b1': (0.0, 0.8),
     'L1_gnn_f_b2': (0.0, 0.8),
     'L1_gnn_s1_b': (0.0, 0.524),
     'L1_gnn_b1_b': (0.0, 0.369),
     'L1_gnn_bq': (0.0, 2.0),
     'L1_gnn_bk': (0.0, 2.0),
     'L1_gnn_bv': (0.0, 0.1),
     'L1_gnn_bo': (0.0, 0.1),
     'L1_gnn_s2_b': (0.0, 0.8),
     'L1_gnn_b2_b': (0.0, 0.65),
     'L1_gnn_m_b1': (0.0, 0.328),
     'L1_gnn_m_b2': (0.0, 0.1),
     'L1_mix_qkv_b': (0.0, 0.1),
     'L1_mix_out_b': (0.0, 0.1),
     'L1_mix_ln_gamma': (1.0, 0.6),
     'L1_mix_ln_beta': (0.0, 0.1),
     'L3_gnn_b_lower': (0.0, 1.21),
     'L3_gnn_b1': (0.0, 2.0),
     'L3_gnn_b2': (0.0, 2.0),
     'L3_gnn_b3': (0.0, 2.0),
     'L3_gnn_b_upper': (0.0, 2.0),
     'L3_gnn_b_skip': (0.0, 2.0),
     'L3_mix_b_out': (0.0, 2.0)}
    factors = {'edge_attr_32': 8.0,
     'edge_attr_64': 8.0,
     'node_vec1': 42.172,
     'L0_gnn_Wq': 48.134,
     'L0_gnn_Wk': 45.351,
     'L0_gnn_W1': 8.626,
     'L0_mix_Wq': 59.96,
     'L0_mix_qG1': 46.04,
     'L0_mix_qG2': 42.624,
     'L0_ffn_bg': 28.31,
     'L0_ffn_b1': 18.686,
     'L1_gnn_f_w1': 37.662,
     'L1_gnn_f_w2': 8.0,
     'L1_gnn_s1_w': 8.0,
     'L1_gnn_b1_w': 8.0,
     'L1_gnn_wq': 8.0,
     'L1_gnn_wk': 8.0,
     'L1_gnn_s2_w': 24.293,
     'L1_gnn_b2_w': 8.0,
     'L2_gnn_W_edge': 8.0,
     'L2_gnn_b_edge': 8.0,
     'L2_gnn_W1': 8.0,
     'L2_gnn_b1': 64.0,
     'L2_gnn_W2': 8.0,
     'L2_gnn_b2': 187.79,
     'L2_mix_b_proj': 200.0,
     'L2_ffn_w_gate': 8.0,
     'L2_ffn_w_up': 8.0,
     'L2_ffn_w_down': 8.0,
     'L3_gnn_W_skip': 64.0,
     'L3_mix_W_qkv': 36.365,
     'L3_mix_W_out': 37.383,
     'L3_ffn_pos_w': 64.0,
     'L3_ffn_pos_b': 64.0,
     'L3_ffn_qkv_w': 64.0,
     'L3_ffn_qkv_b': 64.0,
     'L3_ffn_wo_w': 64.0,
     'L3_ffn_wo_b': 200.0,
     'L0_gnn_Wv': 4.544,
     'L0_gnn_Wo': 4.154,
     'L0_mix_kG1': 4.438,
     'L0_mix_kG2': 4.331,
     'L0_ffn_Wg': 5.357,
     'L0_ffn_W1': 4.904,
     'L0_ffn_b2': 6.188,
     'L1_ffn_gate_w': 3.167,
     'L1_ffn_w1': 3.109,
     'L1_ffn_sg_gate': 3.211}
    for name, (base, spread) in spreads.items():
        noise = np.random.default_rng([zlib.crc32(name.encode()), seed]).standard_normal(out[name].shape)
        drawn = base * np.exp(spread * noise) if base else spread * noise
        out[name] = jnp.asarray(drawn.astype(out[name].dtype))
    for name, factor in factors.items():
        out[name] = (out[name] * factor).astype(out[name].dtype)
    return out
```

```python
from contextlib import ExitStack, contextmanager

import numpy as np

import concourse.bass as bass
from concourse import mybir

ALU = mybir.AluOpType
ACT = mybir.ActivationFunctionType
F32 = mybir.dt.float32
F16 = mybir.dt.float16
BF16 = mybir.dt.bfloat16
I32 = mybir.dt.int32
U32 = mybir.dt.uint32

N = 625
D = 512
R = 125
NT = N // R
KB = D // 128
NP = N + 1
HALF = NP // 2
E = 20625
NCH = E // R
CPI = 5
FPI = 15
EF = 97
NREL = 6
TB = 2560
VS = 520
UC = 2048
RING = 8
NEXP = 8
H1B = 8
FB = 11
NBLK = 4
SPAN = 512 + 114
MASKED = -1.0e30
LEAST = -3.0e38
LN_EPS = 1.0e-5
TAU = 2 * np.pi
TAU_A = 6.28125
TAU_B = float(np.float32(TAU - TAU_A).view(np.int32) // 4096 * 4096 and
              (np.float32(TAU - TAU_A).view(np.int32) // 4096 * 4096).astype(np.int32).view(np.float32))
TAU_C = float(TAU - TAU_A - TAU_B)
ROUND = 1.5 * 2 ** 23

RINGS = {f"unit_full{s}": 16 for s in range(RING)} | {f"unit_free{s}": 1 for s in range(RING)}


def each(name, per, count):
    return {f"{name}{i}": per for i in range(count)}


LOOPS = {
    "relation": dict(onehot_ready=NCH, counts_filled=1, counts_read=NT, counts_added=1,
                     counts_stored=16, dve_step=1) | each("onehot_used", NCH // CPI, CPI),
    "chunk": dict(onehot_ready=CPI) | each("onehot_used", 1, CPI),
    "feature": dict(feat_onehot_ready=FPI) | each("feat_landed", 16, 3)
               | each("feat_used", FPI // CPI, CPI - 1) | each("fe_used", 1, 3),
    "expert0": RINGS | each("filled", 8, 2) | each("drained", 8, 2) | each("bank_filled", 5, 4)
               | each("bank_drained", 5, 4),
    "expert1": {k: 2 * v for k, v in RINGS.items()} | each("filled", 16, 2) | each("drained", 16, 2)
               | each("bank_filled", 5, 4) | each("bank_drained", 5, 4),
    "block": RINGS | each("filled", 31, 2) | each("drained", 31, 2)
             | each("bank_filled", 9, 4) | each("bank_drained", 9, 4)
             | dict(arrived=24, dve_step=40, pool_step=2, var_ready=2, rstd_ready=2,
                    max_ready=20, exp_done=20),
}


class Counts:

    def __init__(self):
        self.k, self.loops, self.slot, self.bank, self.unit = {}, [], 0, 0, 0

    def at(self, sem, k):
        for reg, per in self.loops:
            if per.get(sem.name, 0):
                k = reg * per[sem.name] + k
        return k

    def now(self, sem):
        return self.at(sem, self.k.get(sem.name, 0))

    def next(self, sem, by=1):
        self.k[sem.name] = self.k.get(sem.name, 0) + by
        return self.now(sem)


@contextmanager
def repeat(eng, c, name, times):
    with eng.Fori(0, times) as i:
        began = dict(c.k)
        c.loops.append((i, LOOPS[name]))
        yield i
        for sem, k in list(c.k.items()):
            by = k - began.get(sem, 0)
            if by:
                assert LOOPS[name].get(sem) == by, (name, sem, by, LOOPS[name].get(sem))
                c.k[sem] = k + (times - 1) * by
        c.loops.pop()


def gps_network(nc, t, out, n_units, stop=None):
    rel_dram = nc.dram_tensor("relation_counts", (NREL, R, NT, NP), F32, kind="Internal").ap()

    with ExitStack() as ctx:
        def sb(name, cols, dt=F32):
            return ctx.enter_context(nc.sbuf_tensor(name, [128, cols], dt))

        def sem(name):
            return ctx.enter_context(nc.semaphore(name))

        ring = sb("ring", RING * UC)
        X, XN, G, XT = sb("X", TB), sb("XN", TB), sb("G", TB), sb("XT", TB)
        arena = sb("arena", 4 * TB + NT * VS)
        bias0, bias1 = sb("bias0", NT * NP), sb("bias1", NT * NP)
        P = sb("P", 2 * NP)
        PT = sb("PT", 2 * N)
        AGT = sb("AGT", NP)
        KV = sb("KV", 4 * 130)
        ident, ones = sb("ident", 128), sb("ones", 128)
        iota = sb("iota", NP, F16)
        iota8 = sb("iota8", 8)
        st = sb("st", NT * 6)
        mv = sb("mv", NT * 2)
        rs, hf = sb("rs", NT), sb("hf", NT)
        mx, nm = sb("mx", 4), sb("nm", 4)
        Z, rz = sb("Z", 16), sb("rz", 16)
        top, topi, topf = sb("top", 8 * NT), sb("topi", 8 * NT, U32), sb("topf", 8 * NT)
        wts, comb = sb("wts", 4 * NT), sb("comb", 8 * NT)
        kept = sb("kept", 600)
        emb, cond = sb("emb", NP), sb("cond", NP)

        def rows(buf, cols=D):
            return buf[:, 0:NT * cols].rearrange("p (r d) -> p r d", r=NT)

        def trans(buf, blocks=KB):
            return buf[:, 0:blocks * NP].rearrange("p (k n) -> p k n", k=blocks)

        Q0, K0, V0, A0, Y0 = (arena[:, a:b] for a, b in
                              ((0, TB), (TB, 2 * TB), (2 * TB, 2 * TB + NT * VS),
                               (2 * TB + NT * VS, 3 * TB + NT * VS), (3 * TB + NT * VS, 4 * TB + NT * VS)))
        Xr, XNr, Gr, XTt = rows(X), rows(XN), rows(G), trans(XT)
        QT, KT, YT, Ar = trans(Q0), trans(K0), trans(Y0), rows(A0)
        Kr, V = rows(K0), V0.rearrange("p (r d) -> p r d", r=NT)
        HT = arena[:, 0:FB * NP].rearrange("p (k n) -> p k n", k=FB)
        REL = arena[:, 0:NT * 768].rearrange("p (r d) -> p r d", r=NT)
        TOT = arena[:, 0:NT * NP].rearrange("p (r n) -> p r n", r=NT)
        CNT = arena[:, NT * NP:2 * NT * NP].rearrange("p (r n) -> p r n", r=NT)
        onehots = arena[:, 2 * NT * NP:3 * NT * NP]
        OH = onehots.bitcast(BF16).rearrange("p (b n) -> p b n", b=2 * CPI)
        OHF = onehots.rearrange("p (b n) -> p b n", b=CPI)
        FE = arena[:, 3 * NT * NP:3 * NT * NP + 3 * CPI * EF].rearrange("p (b n) -> p b n", b=3)
        edges_i = G[:, 0:3 * NCH].bitcast(I32)
        edges_f = G[:, 3 * NCH:6 * NCH].rearrange("p (a c) -> p a c", a=3)
        wrel = G[:, 6 * NCH:7 * NCH]
        B0 = bias0[:, :].rearrange("p (r n) -> p r n", r=NT)
        B1 = bias1[:, :].rearrange("p (r n) -> p r n", r=NT)
        Pv = P[:, :].rearrange("p (b n) -> p b n", b=2)
        TMP = Pv
        P2 = G[:, 0:2 * NP].rearrange("p (b n) -> p b n", b=2)
        PTv = PT[:, :].rearrange("p (b j n) -> p b j n", b=2, j=NT)
        KVv = KV[:, :].rearrange("p (j d) -> p j d", j=4)

        PS = ctx.enter_context(nc.psum_tensor("PS", [128, 8, 512], F32))

        consts_landed = sem("consts_landed")
        unit_full = [sem(f"unit_full{s}") for s in range(RING)]
        unit_free = [sem(f"unit_free{s}") for s in range(RING)]
        filled = [sem(f"filled{s}") for s in range(2)]
        drained = [sem(f"drained{s}") for s in range(2)]
        bank_filled = [sem(f"bank_filled{s}") for s in range(4)]
        bank_drained = [sem(f"bank_drained{s}") for s in range(4)]
        arrived = sem("arrived")
        dve_step, act_step, pool_step = sem("dve_step"), sem("act_step"), sem("pool_step")
        var_ready, rstd_ready, rows_ready = sem("var_ready"), sem("rstd_ready"), sem("rows_ready")
        max_ready, exp_done, masked = sem("max_ready"), sem("exp_done"), sem("masked")
        onehot_ready = sem("onehot_ready")
        onehot_used = [sem(f"onehot_used{j}") for j in range(CPI)]
        counts_filled, counts_read = sem("counts_filled"), sem("counts_read")
        counts_added, counts_stored = sem("counts_added"), sem("counts_stored")
        feat_landed = [sem(f"feat_landed{b}") for b in range(3)]
        feat_onehot_ready = sem("feat_onehot_ready")
        feat_used = [sem(f"feat_used{j}") for j in range(CPI)]
        fe_used = [sem(f"fe_used{b}") for b in range(3)]
        elu_neg, elu_exp = sem("elu_neg"), sem("elu_exp")
        z_ready = sem("z_ready")
        abs_ready, scaled, quantised = sem("abs_ready"), sem("scaled"), sem("quantised")
        rel_landed = [sem("rel_landed0"), sem("rel_landed1")]
        rel_used = [sem("rel_used0"), sem("rel_used1")]
        passed = sem("passed")
        out_stored = sem("out_stored")
        CONSTS = 16 * 7

        def anchor(e):
            e.sem_inc(passed, 1)

        def meet(e, c):
            if c.loops:
                anchor(e)
            e.drain().then_inc(arrived, 1)
            e.wait_ge(arrived, c.next(arrived, 4))
            anchor(e)

        def slot_ap(s, p=128):
            return PS[0:p, 2 * s:2 * s + 2, 0:HALF]

        def take_slot(pe, c):
            s = c.slot % 2
            c.slot += 1
            pe.wait_ge(drained[s], c.now(filled[s]))
            c.next(filled[s])
            c.next(drained[s])
            return s

        def take_bank(pe, c):
            b = c.bank % 4
            c.bank += 1
            pe.wait_ge(bank_drained[b], c.now(bank_filled[b]))
            c.next(bank_filled[b])
            c.next(bank_drained[b])
            return b

        def await_slot(e, c):
            s = c.slot % 2
            c.slot += 1
            e.wait_ge(filled[s], c.next(filled[s]))
            c.next(drained[s])
            return s

        def await_bank(e, c):
            b = c.bank % 4
            c.bank += 1
            e.wait_ge(bank_filled[b], c.next(bank_filled[b]))
            c.next(bank_drained[b])
            return b

        def pass_slots(c, n):
            for _ in range(n):
                c.next(filled[c.slot % 2])
                c.next(drained[c.slot % 2])
                c.slot += 1

        def pass_banks(c, n):
            for _ in range(n):
                c.next(bank_filled[c.bank % 4])
                c.next(bank_drained[c.bank % 4])
                c.bank += 1

        def unit(e, c):
            s = c.unit % RING
            c.unit += 1
            e.wait_ge(unit_full[s], c.next(unit_full[s], 16))
            return s

        def pass_units(c, n):
            for _ in range(n):
                c.next(unit_full[c.unit % RING], 16)
                c.unit += 1

        def U(s, a=0, b=UC, p=128):
            return ring[0:p, s * UC + a:s * UC + b]

        def release(e, s):
            e.sem_inc(unit_free[s], 1)

        def pe_project_T(pe, c, s, src, ncols, outs, first=0, nk=KB, wo=0):
            for o in range(outs):
                b = take_slot(pe, c)
                for k in range(nk):
                    w = U(s, wo + k * ncols + o * 128, wo + k * ncols + o * 128 + 128)
                    for h in range(2):
                        mm = pe.matmul(PS[:, 2 * b + h, 0:HALF], w, src[:, k, h * HALF:(h + 1) * HALF],
                                       start=(k == 0), stop=(k == nk - 1))
                mm.then_inc(filled[b], 1)

        def pe_project_rows(pe, c, units, src, nk=KB, wo=0, tiles=NT):
            for r in range(tiles):
                b = take_bank(pe, c)
                blocks = [(s, k) for s, n in units for k in range(n)]
                for i, (s, k) in enumerate(blocks):
                    mm = pe.matmul(PS[0:R, 4 + b, :], src[:, i, r * R:(r + 1) * R],
                                   U(s, wo + k * D, wo + (k + 1) * D),
                                   start=(i == 0), stop=(i == len(blocks) - 1))
                mm.then_inc(bank_filled[b], 1)

        def pe_transpose_rows(pe, c, src, signalled=True):
            for r in range(NT):
                if signalled:
                    pe.wait_ge(rows_ready, c.next(rows_ready))
                b = take_bank(pe, c)
                for k in range(KB):
                    mm = pe.transpose(PS[:, 4 + b, k * R:(k + 1) * R], src[0:R, r, k * 128:(k + 1) * 128],
                                      ident[0:R, 0:R])
                mm.then_inc(bank_filled[b], 1)

        def pe_attend(pe, c, heads, dh, chosen):
            total = NT * heads
            where = {}

            def score(i):
                r, h = divmod(i, heads)
                p, k = h * dh % 128, h * dh // 128
                b = take_slot(pe, c)
                for half in range(2):
                    mm = pe.matmul(PS[0:R, 2 * b + half, 0:HALF], QT[p:p + dh, k, r * R:(r + 1) * R],
                                   KT[p:p + dh, k, half * HALF:(half + 1) * HALF], start=True, stop=True)
                mm.then_inc(filled[b], 1)

            def turn(i):
                pe.wait_ge(chosen, c.next(chosen))
                b = take_slot(pe, c)
                for j in range(NT):
                    mm = pe.transpose(PS[0:R, 2 * b + j // 3, j % 3 * R:(j % 3 + 1) * R],
                                      Pv[0:R, i % 2, j * R:(j + 1) * R], ident[0:R, 0:R])
                mm.then_inc(filled[b], 1)
                return b, c.now(filled[b])

            score(0)
            for i in range(total):
                r, h = divmod(i, heads)
                if i + 1 < total:
                    score(i + 1)
                b, k = turn(i)
                if h == 0:
                    where[r] = take_bank(pe, c)
                pe.wait_ge(drained[b], k)
                for j in range(NT):
                    mm = pe.matmul(PS[0:R, 4 + where[r], h * dh:(h + 1) * dh], PTv[0:R, i % 2, j, :],
                                   V[0:R, j, h * dh:(h + 1) * dh], start=(j == 0), stop=(j == NT - 1))
                if h == heads - 1:
                    mm.then_inc(bank_filled[where[r]], 1)

        def pe_linear_attend(pe, c, krows):
            for j in range(4):
                b = take_bank(pe, c)
                for r in range(NT):
                    mm = pe.matmul(PS[:, 4 + b, 0:130], krows[0:R, r, j * 128:(j + 1) * 128],
                                   V[0:R, r, j * 130:(j + 1) * 130], start=(r == 0), stop=(r == NT - 1))
                mm.then_inc(bank_filled[b], 1)
            for b in range(4):
                pe.wait_ge(bank_drained[b], c.now(bank_drained[b]))
            for r in range(NT):
                b = take_slot(pe, c)
                for j in range(4):
                    mm = pe.matmul(PS[0:R, 2 * b + j // 2, j % 2 * 130:(j % 2 + 1) * 130],
                                   QT[:, j, r * R:(r + 1) * R], KVv[:, j, :], start=True, stop=True)
                mm.then_inc(filled[b], 1)

        def act_drain_T(act, c, dst, func, outs, bias=None, scale=None, freed=None, func_per=None):
            for o in range(outs):
                s = await_slot(act, c)
                if freed is not None and o == outs - 1:
                    release(act, freed)
                more = {}
                if bias is not None:
                    more["bias"] = bias(o)
                if scale is not None:
                    more["scale"] = scale
                act.activation(dst(o), slot_ap(s), func, **more).then_inc(drained[s], 1)

        def halves(t):
            return lambda o: t[:, o, :].rearrange("p (h n) -> p h n", h=2)

        def act_drain_transposed(act, c, dst, bias=None):
            for r in range(NT):
                b = await_bank(act, c)
                src = PS[:, 4 + b, 0:KB * R].rearrange("p (k n) -> p k n", k=KB)
                if bias is None:
                    act.activation(dst[:, :, r * R:(r + 1) * R], src, ACT.Copy).then_inc(bank_drained[b], 1)
                else:
                    for k in range(KB):
                        ins = act.activation(dst[:, k, r * R:(r + 1) * R], src[:, k, :], ACT.Identity, bias=bias(k))
                    ins.then_inc(bank_drained[b], 1)

        def act_attend(act, c, heads, summed):
            total = NT * heads

            def exps(i):
                r, h = divmod(i, heads)
                act.wait_ge(max_ready, c.next(max_ready))
                cols = NP if summed else N
                more = dict(accum_out=Z[0:R, r % 2 * 8 + h:r % 2 * 8 + h + 1]) if summed else {}
                act.activation(Pv[0:R, i % 2, 0:cols], Pv[0:R, i % 2, 0:cols], ACT.Exp, bias=nm[0:R, i % 4:i % 4 + 1],
                               **more).then_inc(exp_done, 1)
                c.next(exp_done)

            pass_slots(c, 1)
            exps(0)
            for i in range(total):
                if i + 1 < total:
                    pass_slots(c, 1)
                s = await_slot(act, c)
                act.activation(PTv[0:R, i % 2, 0:3, :], PS[0:R, 2 * s, 0:3 * R].rearrange("p (j n) -> p j n", j=3),
                               ACT.Copy)
                act.activation(PTv[0:R, i % 2, 3:5, :], PS[0:R, 2 * s + 1, 0:2 * R].rearrange("p (j n) -> p j n", j=2),
                               ACT.Copy).then_inc(drained[s], 1)
                if i + 1 < total:
                    exps(i + 1)

        def act_linear_attend(act, c, scale):
            for j in range(4):
                b = await_bank(act, c)
                act.activation(KVv[0:64, j, 0:65], PS[0:64, 4 + b, 0:65], ACT.Copy, scale=scale)
                act.activation(KVv[64:128, j, 65:130], PS[64:128, 4 + b, 65:130], ACT.Copy,
                               scale=scale).then_inc(bank_drained[b], 1)
            pass_slots(c, NT)

        def dve_norm(v, c, src, dst, gain=None, shift=None, cond=False, signal=None):
            for r in range(NT):
                v.bn_stats(st[0:R, 6 * r:6 * r + 6], src[0:R, r, :]).then_inc(dve_step, 1)
                k = c.next(dve_step)
            v.wait_ge(dve_step, k)
            anchor(v)
            for r in range(NT):
                ins = v.bn_aggr(mv[0:R, 2 * r:2 * r + 2], st[0:R, 6 * r:6 * r + 6])
            ins.then_inc(var_ready, 1)
            c.next(var_ready)
            v.wait_ge(rstd_ready, c.next(rstd_ready))
            for r in range(NT):
                ins = v.tensor_scalar(dst[0:R, r, :], src[0:R, r, :], mv[0:R, 2 * r:2 * r + 1], rs[0:R, r:r + 1],
                                      ALU.subtract, ALU.mult)
                if gain is None and not cond:
                    ins.then_inc(rows_ready, 1)
                    k = c.next(rows_ready)
                else:
                    ins.then_inc(dve_step, 1)
                    k = c.next(dve_step)
            if gain is not None:
                v.wait_ge(dve_step, k)
                for r in range(NT):
                    v.tensor_tensor(dst[0:R, r, :], dst[0:R, r, :], gain, ALU.mult).then_inc(dve_step, 1)
                    k = c.next(dve_step)
                v.wait_ge(dve_step, k)
                for r in range(NT):
                    v.tensor_tensor(dst[0:R, r, :], dst[0:R, r, :], shift, ALU.add).then_inc(signal, 1)
                    c.next(signal)
            if cond:
                for r in range(NT):
                    s = await_slot(v, c)
                    if r == 0:
                        v.wait_ge(dve_step, k)
                    v.scalar_tensor_tensor(out=dst[0:R, r, :], in0=PS[0:R, 2 * s, :], scalar=1.0,
                                           in1=dst[0:R, r, :], op0=ALU.add, op1=ALU.mult).then_inc(dve_step, 1)
                    v.wait_ge(dve_step, c.next(dve_step))
                    v.tensor_tensor(dst[0:R, r, :], PS[0:R, 2 * s + 1, :], dst[0:R, r, :],
                                    ALU.add).then_inc(drained[s], 1)

        def pool_rstd(g, c):
            g.wait_ge(var_ready, c.next(var_ready))
            anchor(g)
            g.tensor_scalar(rs[0:R, :], mv[0:R, :].rearrange("p (r a) -> p r a", a=2)[:, :, 1], LN_EPS, None,
                            ALU.add).then_inc(pool_step, 1)
            g.wait_ge(pool_step, c.next(pool_step))
            g.tensor_tensor(rs[0:R, :], rs[0:R, :], hf[0:R, :], ALU.pow).then_inc(rstd_ready, 1)
            c.next(rstd_ready)

        def pool_add_row(g, dst, row):
            for r in range(NT):
                g.tensor_tensor(dst[0:R, r, :], dst[0:R, r, :], row, ALU.add)

        def dve_drain_rows(v, c, dst, row=None, freed=()):
            for r in range(NT):
                b = await_bank(v, c)
                if r == NT - 1:
                    for s in freed:
                        release(v, s)
                p = PS[0:R, 4 + b, :]
                if row is None:
                    ins = v.tensor_copy(dst(r), p)
                else:
                    ins = v.tensor_tensor(dst(r), p, row(r), ALU.add)
                ins.then_inc(bank_drained[b], 1)

        def tile_of(buf):
            return lambda r: buf[0:R, r, :]

        def await_own_banks(e, c):
            for b in range(4):
                e.wait_ge(bank_drained[b], c.now(bank_drained[b]))

        def await_own_slots(e, c):
            for s in range(2):
                e.wait_ge(drained[s], c.now(drained[s]))

        def dve_values(v, c, freed, bias=None):
            for r in range(NT):
                b = await_bank(v, c)
                if r == NT - 1:
                    release(v, freed)
                dst = V[0:R, r, :].rearrange("p (h d) -> p h d", d=65)[:, :, 0:64]
                src = PS[0:R, 4 + b, :].rearrange("p (h d) -> p h d", d=64)
                if bias is None:
                    ins = v.tensor_copy(dst, src)
                else:
                    ins = v.tensor_tensor(dst, src, bias.rearrange("p (h d) -> p h d", d=64), ALU.add)
                ins.then_inc(bank_drained[b], 1)

        def dve_accumulate(v, c, dst, freed, row=None):
            row = row or dst
            dve_drain_rows(v, c, tile_of(dst), row=tile_of(row), freed=freed)

        def dve_attend(v, c, heads, dh, bias, scale):
            total = NT * heads

            def score(i):
                r, h = divmod(i, heads)
                s = await_slot(v, c)
                anchor(v)
                v.tensor_tensor_reduce(Pv[0:R, i % 2, :].rearrange("p (h n) -> p h n", h=2), slot_ap(s, R),
                                       bias[0:R, r, :].rearrange("p (h n) -> p h n", h=2), scale, LEAST,
                                       ALU.add, ALU.max, mx[0:R, i % 4:i % 4 + 1]).then_inc(drained[s], 1)
                v.wait_ge(drained[s], c.now(drained[s]))
                v.tensor_scalar(nm[0:R, i % 4:i % 4 + 1], mx[0:R, i % 4:i % 4 + 1], -1.0, None,
                                ALU.mult).then_inc(max_ready, 1)
                c.next(max_ready)
                c.next(exp_done)

            score(0)
            for i in range(total):
                if i + 1 < total:
                    score(i + 1)
                pass_slots(c, 1)
                if i % heads == heads - 1:
                    norm_heads(v, c, i // heads, heads, dh)

        def norm_heads(v, c, r, heads, dh):
            b = await_bank(v, c)
            z0 = r % 2 * 8
            z = Z[0:R, z0:z0 + heads]
            v.tensor_scalar(rz[0:R, z0:z0 + heads], z, 1.0e-30, None, ALU.max).then_inc(dve_step, 1)
            v.wait_ge(dve_step, c.next(dve_step))
            v.reciprocal(rz[0:R, z0:z0 + heads], rz[0:R, z0:z0 + heads]).then_inc(dve_step, 1)
            v.wait_ge(dve_step, c.next(dve_step))
            v.tensor_tensor(Ar[0:R, r, :].rearrange("p (h d) -> p h d", d=dh),
                            PS[0:R, 4 + b, :].rearrange("p (h d) -> p h d", d=dh),
                            rz[0:R, z0:z0 + heads].unsqueeze(2).to_broadcast([R, heads, dh]),
                            ALU.mult).then_inc(bank_drained[b], 1)

        def dve_linear_attend(v, c, guard):
            pass_banks(c, 4)
            for r in range(NT):
                s = await_slot(v, c)
                z0 = r % 2 * 8
                pairs = [PS[0:R, 2 * s + b, 0:260].rearrange("p (h d) -> p h d", d=65) for b in range(2)]
                if guard is not None:
                    op, amount = guard
                    for b in range(2):
                        v.tensor_scalar(rz[0:R, z0 + 4 * b:z0 + 4 * b + 4], pairs[b][:, :, 64], amount, None,
                                        op).then_inc(dve_step, 1)
                        c.next(dve_step)
                    v.wait_ge(dve_step, c.now(dve_step))
                    v.reciprocal(rz[0:R, z0:z0 + 8], rz[0:R, z0:z0 + 8]).then_inc(dve_step, 1)
                    v.wait_ge(dve_step, c.next(dve_step))
                for b in range(2):
                    dst = Ar[0:R, r, b * 256:(b + 1) * 256].rearrange("p (h d) -> p h d", d=64)
                    if guard is None:
                        ins = v.tensor_copy(dst, pairs[b][:, :, 0:64])
                    else:
                        ins = v.tensor_tensor(dst, pairs[b][:, :, 0:64],
                                              rz[0:R, z0 + 4 * b:z0 + 4 * b + 4].unsqueeze(2).to_broadcast([R, 4, 64]),
                                              ALU.mult)
                ins.then_inc(drained[s], 1)

        def dve_elu(v, c, buf, tmp, p):
            v.tensor_scalar(tmp, buf, 0.0, None, ALU.min).then_inc(elu_neg, 1)
            c.next(elu_neg)
            v.wait_ge(elu_exp, c.next(elu_exp))
            v.scalar_tensor_tensor(out=buf, in0=buf, scalar=0.0, in1=tmp, op0=ALU.max, op1=ALU.add)

        def act_elu(act, c, tmp):
            act.wait_ge(elu_neg, c.next(elu_neg))
            act.activation(tmp, tmp, ACT.Exp).then_inc(elu_exp, 1)
            c.next(elu_exp)

        def dve_gate(v, c, row=None):
            b = await_bank(v, c)
            lg = Z[0:R, 0:8]
            logits = P[0:R, 0:8 * NT]
            cp = PS[0:R, 4 + b, 0:8 * NT]
            if row is None:
                v.tensor_copy(logits, cp).then_inc(bank_drained[b], 1)
            else:
                v.tensor_tensor(logits.rearrange("p (r e) -> p r e", e=8), cp.rearrange("p (r e) -> p r e", e=8),
                                row.unsqueeze(1).to_broadcast([R, NT, 8]), ALU.add).then_inc(bank_drained[b], 1)
            v.wait_ge(bank_drained[b], c.now(bank_drained[b]))
            for r in range(NT):
                v.max(top[0:R, 8 * r:8 * r + 8], logits[:, 8 * r:8 * r + 8]).then_inc(dve_step, 1)
                c.next(dve_step)
            v.wait_ge(dve_step, c.now(dve_step))
            for r in range(NT):
                ins = v.max_index(topi[0:R, 8 * r:8 * r + 8], top[0:R, 8 * r:8 * r + 8], logits[:, 8 * r:8 * r + 8])
            topv = top[0:R, :].rearrange("p (r e) -> p r e", e=8)
            w = wts[0:R, :].rearrange("p (a r) -> p a r", a=4)
            v.tensor_tensor(w[:, 0, :], topv[:, :, 1], topv[:, :, 0], ALU.subtract).then_inc(elu_neg, 1)
            c.next(elu_neg)
            v.wait_ge(elu_neg, c.now(elu_neg))
            v.tensor_copy(topf[0:R, :], topi[0:R, :]).then_inc(dve_step, 1)
            c.next(dve_step)
            v.wait_ge(elu_exp, c.next(elu_exp))
            v.tensor_scalar(w[:, 1, :], w[:, 0, :], 1.0, None, ALU.add).then_inc(dve_step, 1)
            v.wait_ge(dve_step, c.next(dve_step))
            v.reciprocal(w[:, 2, :], w[:, 1, :]).then_inc(dve_step, 1)
            v.wait_ge(dve_step, c.next(dve_step))
            v.tensor_tensor(w[:, 3, :], w[:, 0, :], w[:, 2, :], ALU.mult).then_inc(dve_step, 1)
            v.wait_ge(dve_step, c.next(dve_step))
            for r in range(NT):
                v.tensor_scalar(comb[0:R, 8 * r:8 * r + 8], iota8[0:R, :], topf[0:R, 8 * r:8 * r + 1],
                                w[:, 2, r:r + 1], ALU.is_equal, ALU.mult).then_inc(dve_step, 1)
                v.tensor_scalar(P[0:R, 64 + 8 * r:72 + 8 * r], iota8[0:R, :], topf[0:R, 8 * r + 1:8 * r + 2],
                                w[:, 3, r:r + 1], ALU.is_equal, ALU.mult).then_inc(dve_step, 1)
                c.next(dve_step, 2)
            v.wait_ge(dve_step, c.now(dve_step))
            v.tensor_tensor(comb[0:R, 0:8 * NT], comb[0:R, 0:8 * NT], P[0:R, 64:64 + 8 * NT], ALU.add)

        def act_gate(act, c):
            act.wait_ge(elu_neg, c.next(elu_neg))
            act.activation(wts[0:R, 0:NT], wts[0:R, 0:NT], ACT.Exp).then_inc(elu_exp, 1)
            c.next(elu_exp)

        def pe_gate(pe, c, s):
            b = take_bank(pe, c)
            for r in range(NT):
                for k in range(KB):
                    mm = pe.matmul(PS[0:R, 4 + b, 8 * r:8 * r + 8], XTt[:, k, r * R:(r + 1) * R],
                                   U(s, 8 * k, 8 * k + 8), start=(k == 0), stop=(k == KB - 1))
            mm.then_inc(bank_filled[b], 1)

        def dve_expert(v, c, weight, freed):
            for r in range(NT):
                p = (c.bank - 5) % 4
                b = await_bank(v, c)
                if r == NT - 1:
                    for s in freed:
                        release(v, s)
                if r == 0:
                    for q in range(4):
                        k = c.k.get(bank_drained[q].name, 0) - (q == b)
                        v.wait_ge(bank_drained[q], c.at(bank_drained[q], k))
                anchor(v)
                v.scalar_tensor_tensor(out=Xr[0:R, r, :], in0=PS[0:R, 4 + b, :], scalar=weight(r),
                                       in1=Xr[0:R, r, :], op0=ALU.mult, op1=ALU.add).then_inc(bank_drained[b], 1)

        def dve_gated(v, c, blocks, freed):
            for o in blocks:
                g = c.slot % 2
                pass_slots(c, 1)
                v.wait_ge(drained[g], c.now(drained[g]))
                s = await_slot(v, c)
                if o == blocks[-1]:
                    for f in freed:
                        release(v, f)
                v.tensor_tensor(halves(HT)(o), slot_ap(s), halves(HT)(o), ALU.mult).then_inc(drained[s], 1)

        def dve_embedding(v, c, s):
            def settle(ins):
                ins.then_inc(dve_step, 1)
                v.wait_ge(dve_step, c.next(dve_step))

            e, turns = emb[0:64, :], TMP[0:64, 0, :]
            shift = U(s, 35, 36, 64)
            settle(v.memset(emb[0:64, N:NP], 0.0))
            settle(v.tensor_scalar(e, e, U(s, 34, 35, 64), None, ALU.mult))
            settle(v.tensor_scalar(turns, e, shift, 1.0 / TAU, ALU.add, ALU.mult))
            settle(v.tensor_scalar(turns, turns, ROUND, None, ALU.add))
            settle(v.tensor_scalar(turns, turns, -ROUND, None, ALU.add))
            for part in (TAU_A, TAU_B, TAU_C):
                settle(v.scalar_tensor_tensor(out=e, in0=turns, scalar=-part, in1=e, op0=ALU.mult, op1=ALU.add))
            settle(v.tensor_scalar(e, e, shift, 3.1415925, ALU.add, ALU.min))
            v.tensor_scalar(e, e, -3.1415925, None, ALU.max).then_inc(elu_neg, 1)
            c.next(elu_neg)

        def dve_attend_top(v, c, heads, dh, scale):
            total = NT * heads

            def settle(ins):
                ins.then_inc(dve_step, 1)
                v.wait_ge(dve_step, c.next(dve_step))

            def score(i):
                s = await_slot(v, c)
                p, q, m = Pv[0:R, i % 2, :], P2[0:R, i % 2, 0:N], top[0:R, 0:8]
                v.tensor_scalar(p.rearrange("p (h n) -> p h n", h=2), slot_ap(s, R), scale, None,
                                ALU.mult).then_inc(drained[s], 1)
                v.wait_ge(drained[s], c.now(drained[s]))
                settle(v.max(m, p[:, 0:N]))
                settle(v.match_replace(q, m, p[:, 0:N], LEAST))
                v.tensor_scalar(nm[0:R, i % 4:i % 4 + 1], m[:, 0:1], -1.0, None, ALU.mult).then_inc(max_ready, 1)
                settle(v.max(top[0:R, 8:16], q))
                settle(v.match_replace(q, top[0:R, 8:16], q, LEAST))

            def select(i):
                r, h = divmod(i, heads)
                v.wait_ge(exp_done, c.next(exp_done))
                v.scalar_tensor_tensor(out=Pv[0:R, i % 2, 0:N], in0=P2[0:R, i % 2, 0:N], scalar=0.5 * LEAST,
                                       in1=Pv[0:R, i % 2, 0:N], op0=ALU.is_lt, op1=ALU.mult,
                                       accum_out=Z[0:R, r % 2 * 8 + h:r % 2 * 8 + h + 1]).then_inc(masked, 1)
                c.next(masked)

            score(0)
            for i in range(total):
                if i + 1 < total:
                    score(i + 1)
                select(i)
                pass_slots(c, 1)
                if i % heads == heads - 1:
                    v.wait_ge(masked, c.now(masked))
                    norm_heads(v, c, i // heads, heads, dh)

        def pool_quantise(g, c):
            i = 0
            us = [x % RING for x in range(c.unit - 9, c.unit)]
            for u, s in enumerate(us):
                for k in range(KB if u < 8 else 3):
                    i += 1
                    g.wait_ge(scaled, i)
                    at = i % 2 * 512
                    g.tensor_tensor(U(s, k * D, (k + 1) * D), SG[:, at:at + 512], QZ[:, at:at + 512],
                                    ALU.mult).then_inc(quantised, 1)

        def chunk_column(q, i, j):
            return bass.ds(i * CPI + j, 1)

        combv = comb[:, 0:8 * NT].rearrange("p (r e) -> p r e", e=8)
        AB, SG = G[:, 0:1024], G[:, 1024:2048]
        SC, QZ = A0[:, 0:1024], A0[:, 1024:2048]
        rel_seen = [0, 0]
        stages = ["edges", "l0a", "l0f", "l1a", "l1f", "l2a", "l2f", "l3a", "l3f"]

        def on(stage):
            return stop is None or stages.index(stage) <= stages.index(stop)

        block = ctx.enter_context(nc.Block())

        @block.sync
        def _(sp):
            for dst, src in ((ident[:, :], t["ident"]), (iota[0:R, :], t["iota"]), (iota8[:, :], t["iota8"]),
                             (edges_i[0:R, :], t["edges"]), (Xr[0:R, :, :], t["x"].rearrange("(r p) d -> p r d", p=R)),
                             (emb[0:64, 0:N], t["noise"]), (kept[0:R, 590:590 + NREL], t["relations"])):
                sp.dma_start(dst, src).then_inc(consts_landed, 16)
            for s in range(min(RING, n_units)):
                sp.dma_start(U(s), t["units"][s]).then_inc(unit_full[s], 16)
            if n_units >= 2 * RING:
              with sp.Fori(1, n_units // RING) as i:
                for s in range(RING):
                      sp.wait_ge(unit_free[s], i)
                      sp.dma_start(U(s), t["units"][i * RING + s]).then_inc(unit_full[s], 16)
            for s in range(n_units % RING if n_units >= RING else 0):
                sp.wait_ge(unit_free[s], n_units // RING)
                sp.dma_start(U(s), t["units"][n_units // RING * RING + s]).then_inc(unit_full[s], 16)
            sp.wait_ge(out_stored, 16)

        @block.gpsimd
        def _(g):
            c = Counts()
            for buf in (XT, arena, P, PT, KV, AGT):
                g.memset(buf[:, :], 0.0)
            g.memset(ones[:, :], 1.0)
            g.memset(cond[:, :], 1.0)
            g.memset(hf[:, :], -0.5)
            g.wait_ge(consts_landed, CONSTS)
            meet(g, c)
            meet(g, c)
            meet(g, c)
            g.memset(B0[0:R, :, N:NP], MASKED)
            meet(g, c)
            meet(g, c)

            def ones_column():
                g.memset(V[0:R, :, :].rearrange("p r (h d) -> p (r h) d", d=65)[:, :, 64:65], 1.0)

            def settle(ins):
                ins.then_inc(pool_step, 1)
                g.wait_ge(pool_step, c.next(pool_step))

            def add_rows(dst, row):
                for r in range(NT):
                    ins = g.tensor_tensor(dst[0:R, r, :], dst[0:R, r, :], row(r), ALU.add)
                settle(ins)

            def linear_mix(more=()):
                ones_column()
                for row in more:
                    add_rows(Xr, row)
                meet(g, c)
                meet(g, c)
                meet(g, c)
                meet(g, c)

            if on("l0a"):
                pool_rstd(g, c)
                meet(g, c)
                pass_units(c, 2)
                meet(g, c)
                meet(g, c)
                pool_rstd(g, c)
                pool_rstd(g, c)
                meet(g, c)
                pass_units(c, 4)
                s = unit(g, c)
                meet(g, c)
                linear_mix([lambda r: U(s, 512, 1024, R)])
                pass_units(c, 4)
            if on("l0f"):
                pool_rstd(g, c)
                meet(g, c)
                meet(g, c)
                pass_units(c, 17)
                meet(g, c)
                meet(g, c)
            if on("l1a"):
                pool_rstd(g, c)
                meet(g, c)
                pass_units(c, 1)
                meet(g, c)
                with repeat(g, c, "block", NBLK):
                    s = unit(g, c)
                    pass_units(c, 7)
                    pool_rstd(g, c)
                    meet(g, c)
                    meet(g, c)
                    for r in range(NT):
                        g.tensor_tensor(Gr[0:R, r, :], Gr[0:R, r, :], U(s, 0, 512, R), ALU.add)
                    meet(g, c)
                    pool_rstd(g, c)
                    meet(g, c)
                    for r in range(NT):
                        g.tensor_tensor(Gr[0:R, r, :], Gr[0:R, r, :], U(s, 512, 1024, R), ALU.add)
                    meet(g, c)
                    meet(g, c)
                meet(g, c)
                pool_rstd(g, c)
                pass_units(c, 1)
                s = unit(g, c)
                pass_units(c, 4)
                linear_mix([lambda r: U(s, 0, 512, R), lambda r: XNr[0:R, r, :]])
            if on("l1f"):
                pool_rstd(g, c)
                meet(g, c)
                meet(g, c)
                pass_units(c, 39)
                meet(g, c)
            if on("l2a"):
                pool_rstd(g, c)
                meet(g, c)
                s = unit(g, c)
                for row in (lambda r: XNr[0:R, r, :], lambda r: U(s, 512, 1024, R), lambda r: U(s, 1024, 1536, R)):
                    add_rows(Xr, row)
                meet(g, c)
                meet(g, c)
                pass_units(c, 6)
                linear_mix()
            if on("l2f"):
                pool_rstd(g, c)
                meet(g, c)
                pass_units(c, 9)
                pool_quantise(g, c)
                meet(g, c)
            if on("l3a"):
                pool_rstd(g, c)
                meet(g, c)
                pass_units(c, 2)
                s = unit(g, c)
                pass_units(c, 5)
                add_rows(Xr, lambda r: U(s, 512, 1024, R))
                meet(g, c)
                meet(g, c)
                linear_mix()
            if on("l3f"):
                pool_rstd(g, c)
                s = unit(g, c)
                pass_units(c, 4)
                meet(g, c)
                add_rows(Xr, lambda r: U(s, 0, 512, R))
                meet(g, c)
                meet(g, c)
                meet(g, c)
                meet(g, c)

        @block.tensor
        def _(pe):
            c = Counts()
            pe.wait_ge(consts_landed, CONSTS)
            meet(pe, c)
            zeros = XT[:, :].bitcast(BF16)

            with repeat(pe, c, "relation", NREL):
                pe.wait_ge(counts_read, c.now(counts_read))
                c.next(counts_read, NT)
                for b in range(7):
                    pe.matmul(PS[0:R, b, :], zeros[0:R, 0:R], zeros[0:R, 0:512], start=True, stop=True)
                anchor(pe)
                with repeat(pe, c, "chunk", NCH // CPI):
                    for j in range(CPI):
                        pe.wait_ge(onehot_ready, c.next(onehot_ready))
                        for q in range(NT):
                            w = OH[0:R, 2 * j, q * R:(q + 1) * R]
                            pe.matmul(PS[0:R, q, :], w, OH[0:R, 2 * j + 1, 0:512], start=False, stop=False,
                                      skip_group_check=True)
                            mm = pe.matmul(PS[0:R, 5 + q // 4, q % 4 * 114:q % 4 * 114 + 114], w,
                                           OH[0:R, 2 * j + 1, 512:NP], start=False, stop=False,
                                           skip_group_check=True)
                        mm.then_inc(onehot_used[j], 1)
                        c.next(onehot_used[j])
                pe.drain().then_inc(counts_filled, 1)
                c.next(counts_filled)
            meet(pe, c)

            for h in range(2):
                pe.matmul(PS[0:EF, h, 0:HALF], XT[:, 0:EF], XT[:, 0:HALF], start=True, stop=True)
            with repeat(pe, c, "feature", NCH // FPI):
                for b in range(3):
                    pe.wait_ge(feat_landed[b], c.next(feat_landed[b], 16))
                    for j in range(CPI):
                        pe.wait_ge(feat_onehot_ready, c.next(feat_onehot_ready))
                        for h in range(2):
                            mm = pe.matmul(PS[0:EF, h, 0:HALF], FE[0:R, b, j * EF:(j + 1) * EF],
                                           OHF[0:R, j, h * HALF:(h + 1) * HALF], start=False, stop=False,
                                           skip_group_check=True)
                        used = feat_used[j] if j < CPI - 1 else fe_used[b]
                        mm.then_inc(used, 1)
                        c.next(used)
            meet(pe, c)
            meet(pe, c)
            for r in range(NT):
                b = take_slot(pe, c)
                for j in range(NT):
                    mm = pe.transpose(PS[0:R, 2 * b + j // 3, j % 3 * R:(j % 3 + 1) * R],
                                      CNT[0:R, j, r * R:(r + 1) * R], ident[0:R, 0:R])
                mm.then_inc(filled[b], 1)
            meet(pe, c)

            def norm_T(src=XNr):
                pe_transpose_rows(pe, c, src)

            def linear_mix(krows):
                meet(pe, c)
                pe_linear_attend(pe, c, krows)
                meet(pe, c)
                pe_transpose_rows(pe, c, Ar, signalled=False)
                await_own_banks(pe, c)
                s = unit(pe, c)
                pe_project_rows(pe, c, [(s, KB)], YT)
                meet(pe, c)

            def qkv(src, krow):
                s = unit(pe, c)
                pe_project_T(pe, c, s, src, D, KB)
                s = unit(pe, c)
                if krow:
                    pe_project_rows(pe, c, [(s, KB)], src)
                else:
                    pe_project_T(pe, c, s, src, D, KB)
                s = unit(pe, c)
                pe_project_rows(pe, c, [(s, KB)], src)
                meet(pe, c)

            if on("l0a"):
                norm_T()
                meet(pe, c)
                sa, sbb = unit(pe, c), unit(pe, c)
                qkv(XTt, False)
                pe_attend(pe, c, 8, 64, exp_done)
                meet(pe, c)
                pe_transpose_rows(pe, c, Ar, signalled=False)
                await_own_banks(pe, c)
                s = unit(pe, c)
                pe_project_rows(pe, c, [(s, KB)], YT)
                pe_transpose_rows(pe, c, Ar)
                await_own_banks(pe, c)
                pe_project_T(pe, c, sbb, YT, 128, 1, wo=516)
                await_own_slots(pe, c)
                pe_project_rows(pe, c, [(sbb, 1)], KT, wo=1028)
                meet(pe, c)
                release(pe, sa)
                release(pe, sbb)
                sc = unit(pe, c)
                meet(pe, c)
                qkv(XTt, False)
                for j in range(KB):
                    for g in range(2):
                        b = take_slot(pe, c)
                        for h in range(2):
                            mm = pe.matmul(PS[:, 2 * b + h, 0:HALF], U(sc, 1036 + 128 * g, 1164 + 128 * g),
                                           QT[:, j, h * HALF:(h + 1) * HALF], start=True, stop=True)
                        mm.then_inc(filled[b], 1)
                for r in range(NT):
                    for g in range(2, 4):
                        b = take_bank(pe, c)
                        for j in range(KB):
                            mm = pe.matmul(PS[0:R, 4 + b, j * 128:(j + 1) * 128], KT[:, j, r * R:(r + 1) * R],
                                           U(sc, 1036 + 128 * g, 1164 + 128 * g), start=True, stop=True)
                        mm.then_inc(bank_filled[b], 1)
                linear_mix(Gr)
                release(pe, sc)
            if on("l0f"):
                norm_T()
                meet(pe, c)
                sd = unit(pe, c)
                pe_gate(pe, c, sd)
                meet(pe, c)
                b = take_slot(pe, c)
                for r in range(NT):
                    mm = pe.matmul(PS[0:8, 2 * b + r // 3, r % 3 * R:(r % 3 + 1) * R], combv[0:R, r, :],
                                   ident[0:R, 0:R], start=True, stop=True)
                mm.then_inc(filled[b], 1)
                await_own_slots(pe, c)
                for r in range(NT):
                    b = take_bank(pe, c)
                    pe.matmul(PS[0:R, 4 + b, :], Pv[0:8, 0, r * R:(r + 1) * R], U(sd, 72, 584, 8),
                              start=True, stop=True).then_inc(bank_filled[b], 1)
                meet(pe, c)
                release(pe, sd)
                with repeat(pe, c, "expert0", 2):
                    for e in range(4):
                        s = unit(pe, c)
                        pe_project_T(pe, c, s, XTt, D, KB)
                        await_own_slots(pe, c)
                        s = unit(pe, c)
                        pe_project_rows(pe, c, [(s, KB)], HT)
                meet(pe, c)
            if on("l1a"):
                norm_T()
                meet(pe, c)
                se = unit(pe, c)
                pe.wait_ge(z_ready, c.next(z_ready))
                b = take_slot(pe, c)
                for h in range(2):
                    mm = pe.matmul(PS[0:16, 2 * b + h, 0:HALF], U(se, 0, 16, 64), emb[0:64, h * HALF:(h + 1) * HALF],
                                   start=True, stop=True)
                mm.then_inc(filled[b], 1)
                await_own_slots(pe, c)
                b = take_slot(pe, c)
                for h in range(2):
                    mm = pe.matmul(PS[0:16, 2 * b + h, 0:HALF], U(se, 16, 32, 16), Pv[0:16, 0, h * HALF:(h + 1) * HALF],
                                   start=True, stop=True)
                mm.then_inc(filled[b], 1)
                meet(pe, c)
                release(pe, se)
                with repeat(pe, c, "block", NBLK):
                    sf, sg = unit(pe, c), unit(pe, c)

                    def condition(a):
                        for r in range(NT):
                            b = take_slot(pe, c)
                            for h in range(2):
                                mm = pe.matmul(PS[0:R, 2 * b + h, :], cond[0:17, r * R:(r + 1) * R],
                                               U(sg, (a + h) * D, (a + h + 1) * D, 17), start=True, stop=True)
                            mm.then_inc(filled[b], 1)
                        meet(pe, c)
                        pe_transpose_rows(pe, c, Ar, signalled=False)
                        await_own_banks(pe, c)

                    condition(0)
                    qkv(YT, False)
                    pe_attend(pe, c, 4, 128, exp_done)
                    meet(pe, c)
                    pe_transpose_rows(pe, c, Ar, signalled=False)
                    await_own_banks(pe, c)
                    s = unit(pe, c)
                    pe_project_rows(pe, c, [(s, KB)], YT)
                    condition(2)
                    s = unit(pe, c)
                    pe_project_T(pe, c, s, YT, D, KB)
                    meet(pe, c)
                    s = unit(pe, c)
                    pe_project_rows(pe, c, [(s, KB)], QT)
                    b = take_bank(pe, c)
                    pe.sem_inc(bank_filled[b], 1)
                    meet(pe, c)
                    release(pe, sf)
                    release(pe, sg)
                meet(pe, c)
                norm_T(Ar)
                await_own_banks(pe, c)
                sg, sh = unit(pe, c), unit(pe, c)
                qkv(YT, True)
                linear_mix(Kr)
                release(pe, sg)
                release(pe, sh)
            if on("l1f"):
                norm_T()
                meet(pe, c)
                si = unit(pe, c)
                pe_gate(pe, c, si)
                meet(pe, c)
                release(pe, si)
                with repeat(pe, c, "expert1", 2):
                    for e in range(4):
                        for half in range(2):
                            s = unit(pe, c)
                            pe_project_T(pe, c, s, XTt, D, KB)
                        await_own_slots(pe, c)
                        s, s2 = unit(pe, c), unit(pe, c)
                        pe_project_rows(pe, c, [(s, KB), (s2, KB)], HT)
                for half in range(2):
                    s, s2 = unit(pe, c), unit(pe, c)
                    for o in range(KB):
                        pe_project_T(pe, c, s, XTt, D, 1, wo=o * 128)
                        pe_project_T(pe, c, s2, XTt, D, 1, wo=o * 128)
                await_own_slots(pe, c)
                s, s2 = unit(pe, c), unit(pe, c)
                pe_project_rows(pe, c, [(s, KB), (s2, KB)], HT)
                meet(pe, c)
            if on("l2a"):
                norm_T()
                meet(pe, c)
                sj = unit(pe, c)
                meet(pe, c)
                for o in range(KB):
                    b = take_slot(pe, c)
                    for h in range(2):
                        mm = pe.matmul(PS[:, 2 * b + h, 0:HALF], U(sj, o * 128, o * 128 + 128, EF),
                                       AGT[0:EF, h * HALF:(h + 1) * HALF], start=True, stop=True)
                    mm.then_inc(filled[b], 1)
                await_own_slots(pe, c)
                s = unit(pe, c)
                pe_project_T(pe, c, s, YT, D, KB)
                await_own_slots(pe, c)
                s = unit(pe, c)
                pe_project_rows(pe, c, [(s, KB)], QT)
                meet(pe, c)
                release(pe, sj)
                qkv(XTt, True)
                linear_mix(Kr)
            if on("l2f"):
                norm_T()
                meet(pe, c)
                us = []

                def column_sums(u, blocks=KB):
                    us.append(unit(pe, c))
                    for k in range(blocks):
                        pe.wait_ge(abs_ready, c.next(abs_ready))
                        b = take_bank(pe, c)
                        pe.matmul(PS[:, 4 + b, :], ones[:, :], AB[:, c.k[abs_ready.name] % 2 * 512 + 0:
                                  c.k[abs_ready.name] % 2 * 512 + 512], start=True, stop=True).then_inc(bank_filled[b], 1)

                column_sums(0)
                for u in range(6):
                    if u < 5:
                        column_sums(u + 1)
                    else:
                        column_sums(6)
                        column_sums(7)
                        column_sums(8, 3)
                    pe.wait_ge(quantised, 4 * (u + 1))
                    for o in range(2 if u < 5 else 1):
                        pe_project_T(pe, c, us[u], XTt, D, 1, wo=o * 128)
                        pe_project_T(pe, c, us[u], XTt, D, 1, wo=256 + o * 128)
                pe.wait_ge(quantised, 35)
                await_own_slots(pe, c)
                pe_project_rows(pe, c, [(us[6], KB), (us[7], KB), (us[8], 3)], HT)
                meet(pe, c)
            if on("l3a"):
                norm_T()
                meet(pe, c)
                sa, sbb, sc = unit(pe, c), unit(pe, c), unit(pe, c)
                meet(pe, c)
                pe_project_T(pe, c, sa, XTt, 128, 1)
                for l in range(3):
                    await_own_slots(pe, c)
                    su, at = ((sa, 512), (sa, 1280), (sbb, 0))[l]
                    for j in range(NT):
                        b = take_slot(pe, c)
                        for h in range(2):
                            mm = pe.matmul(PS[0:R, 2 * b + h, 0:384], YT[:, 0, j * R:(j + 1) * R],
                                           U(su, at + 384 * h, at + 384 * h + 384), start=True, stop=True)
                        mm.then_inc(filled[b], 1)
                    await_own_slots(pe, c)
                    b = take_slot(pe, c)
                    for q in range(NREL):
                        pe.wait_ge(rel_landed[q % 2], c.next(rel_landed[q % 2], 16))
                        for j in range(NT):
                            for h in range(2):
                                mm = pe.matmul(PS[:, 2 * b + h, 0:HALF], REL[0:R, j, q * 128:(q + 1) * 128],
                                               (B0, B1)[q % 2][0:R, j, h * HALF:(h + 1) * HALF],
                                               start=(q == 0 and j == 0), stop=(q == NREL - 1 and j == NT - 1))
                        mm.then_inc(rel_used[q % 2] if q < NREL - 1 else filled[b], 1)
                await_own_slots(pe, c)
                pe_project_rows(pe, c, [(sbb, 1)], YT, nk=1, wo=768)
                s = unit(pe, c)
                pe_project_rows(pe, c, [(s, KB)], XTt)
                meet(pe, c)
                release(pe, sa)
                release(pe, sbb)
                release(pe, sc)
                qkv(XTt, True)
                linear_mix(Kr)
            if on("l3f"):
                norm_T()
                sd = unit(pe, c)
                meet(pe, c)
                meet(pe, c)
                qkv(YT, False)
                pe_attend(pe, c, 8, 64, masked)
                meet(pe, c)
                pe_transpose_rows(pe, c, Ar, signalled=False)
                await_own_banks(pe, c)
                s = unit(pe, c)
                pe_project_rows(pe, c, [(s, KB)], YT)
                meet(pe, c)

        @block.scalar
        def _(act):
            c = Counts()
            act.wait_ge(consts_landed, CONSTS)
            meet(act, c)
            with repeat(act, c, "relation", NREL) as q:
                act.wait_ge(counts_stored, c.now(counts_stored))
                act.wait_ge(counts_added, c.now(counts_added))
                act.wait_ge(counts_filled, c.next(counts_filled))
                c.next(counts_added)
                for j in range(NT):
                    act.activation(CNT[0:R, j, 0:512], PS[0:R, j, :], ACT.Copy)
                    act.activation(CNT[0:R, j, 512:NP], PS[0:R, 5 + j // 4, j % 4 * 114:j % 4 * 114 + 114],
                                   ACT.Copy).then_inc(counts_read, 1)
                    c.next(counts_read)
                act.wait_ge(counts_read, c.now(counts_read))
                act.dma_start(rel_dram[q], CNT[0:R, :, :]).then_inc(counts_stored, 16)
                c.next(counts_stored, 16)
            meet(act, c)
            with repeat(act, c, "feature", NCH // FPI) as i:
                for b in range(3):
                    act.wait_ge(fe_used[b], c.now(fe_used[b]))
                    c.next(fe_used[b])
                    act.dma_start(FE[0:R, b, :], t["feats"][i * 3 + b]).then_inc(feat_landed[b], 16)
                    c.next(feat_landed[b], 16)
            meet(act, c)
            act.wait_ge(counts_stored, 16 * NREL)
            act.activation(AGT[0:EF, :].rearrange("p (h n) -> p h n", h=2), PS[0:EF, 0:2, 0:HALF], ACT.Copy)
            act.wait_ge(elu_neg, c.next(elu_neg))
            act.activation(CNT[0:R, :, :], CNT[0:R, :, :], ACT.Ln).then_inc(elu_exp, 1)
            c.next(elu_exp)
            meet(act, c)
            for r in range(NT):
                s = await_slot(act, c)
                act.activation(B0[0:R, r, 0:3 * R], PS[0:R, 2 * s, 0:3 * R], ACT.Copy)
                act.activation(B0[0:R, r, 3 * R:N], PS[0:R, 2 * s + 1, 0:2 * R], ACT.Copy).then_inc(drained[s], 1)
            meet(act, c)

            def norm_T(dst=XTt):
                act_drain_transposed(act, c, dst)

            def column(s, at):
                return lambda o: U(s, at + o, at + o + 1)

            def qkv(krow, qbias=None, kbias=None, scale=(None, None)):
                f = ACT.Copy if qbias is None else ACT.Identity
                s = unit(act, c)
                act_drain_T(act, c, halves(QT), f, KB, bias=qbias, scale=scale[0], freed=s)
                s = unit(act, c)
                if krow:
                    pass_banks(c, NT)
                else:
                    act_drain_T(act, c, halves(KT), f, KB, bias=kbias, scale=scale[1], freed=s)
                pass_units(c, 1)
                pass_banks(c, NT)
                meet(act, c)

            def linear_mix(scale=1.0):
                meet(act, c)
                act_linear_attend(act, c, scale)
                meet(act, c)
                act_drain_transposed(act, c, YT)
                pass_units(c, 1)
                pass_banks(c, NT)
                meet(act, c)

            def elu_maps():
                act_elu(act, c, Y0[:, 0:KB * NP])
                act_elu(act, c, A0[0:R, 0:NT * D])

            if on("l0a"):
                norm_T()
                meet(act, c)
                sa, sbb = unit(act, c), unit(act, c)
                qkv(False)
                act_attend(act, c, 8, True)
                pass_banks(c, NT)
                meet(act, c)
                act_drain_transposed(act, c, YT)
                pass_units(c, 1)
                pass_banks(c, NT)
                act_drain_transposed(act, c, YT)
                act_drain_T(act, c, halves(KT), ACT.Relu, 1, bias=column(sbb, 512))
                pass_banks(c, NT)
                meet(act, c)
                sc = unit(act, c)
                meet(act, c)
                qkv(False, qbias=lambda o: wts[:, o:o + 1], kbias=lambda o: wts[:, 4 + o:5 + o],
                    scale=(U(sc, 1032, 1033), U(sc, 1034, 1035)))
                for j in range(KB):
                    s = await_slot(act, c)
                    act.activation(TMP[:, j % 2, :].rearrange("p (h n) -> p h n", h=2), slot_ap(s),
                                   ACT.Copy).then_inc(drained[s], 1)
                    pass_slots(c, 1)
                    act.wait_ge(drained[1 - s], c.now(drained[1 - s]))
                    act.activation(QT[:, j, :], YT[:, j, :], ACT.Square, scale=0.125)
                for r in range(NT):
                    b = await_bank(act, c)
                    act.activation(TMP[0:R, r % 2, 0:D], PS[0:R, 4 + b, :], ACT.Copy).then_inc(bank_drained[b], 1)
                    pass_banks(c, 1)
                    act.wait_ge(bank_drained[(b + 1) % 4], c.now(bank_drained[(b + 1) % 4]))
                    act.activation(Gr[0:R, r, :], Ar[0:R, r, :], ACT.Square, scale=0.125)
                linear_mix()
            if on("l0f"):
                norm_T()
                meet(act, c)
                sd = unit(act, c)
                pass_banks(c, 1)
                act.activation(kept[:, 0:32], U(sd, 40, 72), ACT.Copy)
                act_gate(act, c)
                meet(act, c)
                s = await_slot(act, c)
                act.activation(Pv[0:8, 0, 0:3 * R], PS[0:8, 2 * s, 0:3 * R], ACT.Copy)
                act.activation(Pv[0:8, 0, 3 * R:N], PS[0:8, 2 * s + 1, 0:2 * R], ACT.Copy).then_inc(drained[s], 1)
                pass_banks(c, NT)
                meet(act, c)
                with repeat(act, c, "expert0", 2) as i:
                    for e in range(4):
                        s = unit(act, c)
                        act_drain_T(act, c, halves(HT), ACT.Gelu, KB, freed=s,
                                    bias=lambda o: kept[:, bass.ds(i * 16 + (e * 4 + o), 1)])
                        pass_units(c, 1)
                        pass_banks(c, NT)
                meet(act, c)
            if on("l1a"):
                norm_T()
                meet(act, c)
                se = unit(act, c)
                act.wait_ge(elu_neg, c.next(elu_neg))
                act.activation(emb[0:64, :], emb[0:64, :], ACT.Sin).then_inc(z_ready, 1)
                c.next(z_ready)
                s = await_slot(act, c)
                act.activation(Pv[0:16, 0, :].rearrange("p (h n) -> p h n", h=2), slot_ap(s, 16), ACT.Silu,
                               bias=U(se, 32, 33, 16)).then_inc(drained[s], 1)
                s = await_slot(act, c)
                act.activation(cond[0:16, :].rearrange("p (h n) -> p h n", h=2), slot_ap(s, 16), ACT.Identity,
                               bias=U(se, 33, 34, 16)).then_inc(drained[s], 1)
                meet(act, c)
                with repeat(act, c, "block", NBLK):
                    sf, sg = unit(act, c), unit(act, c)
                    pass_slots(c, NT)
                    meet(act, c)
                    act_drain_transposed(act, c, YT)
                    qkv(False, qbias=column(sf, 1536), kbias=column(sf, 1540))
                    act_attend(act, c, 4, True)
                    pass_banks(c, NT)
                    meet(act, c)
                    act_drain_transposed(act, c, YT)
                    pass_units(c, 1)
                    pass_banks(c, NT)
                    pass_slots(c, NT)
                    meet(act, c)
                    act_drain_transposed(act, c, YT)
                    s = unit(act, c)
                    act_drain_T(act, c, halves(QT), ACT.Relu, KB, bias=column(sf, 1544), freed=s)
                    meet(act, c)
                    pass_units(c, 1)
                    pass_banks(c, NT)
                    b = await_bank(act, c)
                    act.sem_inc(bank_drained[b], 1)
                    meet(act, c)
                meet(act, c)
                act_drain_transposed(act, c, YT)
                sg, sh = unit(act, c), unit(act, c)
                qkv(True, qbias=column(sh, 512))
                elu_maps()
                linear_mix()
            if on("l1f"):
                norm_T()
                meet(act, c)
                pass_units(c, 1)
                pass_banks(c, 1)
                act_gate(act, c)
                meet(act, c)
                with repeat(act, c, "expert1", 2):
                    for e in range(4):
                        for half in range(2):
                            s = unit(act, c)
                            act_drain_T(act, c, lambda o: halves(HT)(4 * half + o), ACT.Silu, KB, freed=s)
                        pass_units(c, 2)
                        pass_banks(c, NT)
                for o in range(2 * KB):
                    s = await_slot(act, c)
                    act.activation(halves(HT)(o), slot_ap(s), ACT.Silu).then_inc(drained[s], 1)
                    pass_slots(c, 1)
                pass_units(c, 6)
                pass_banks(c, NT)
                meet(act, c)
            if on("l2a"):
                norm_T()
                meet(act, c)
                sj = unit(act, c)
                meet(act, c)
                act_drain_T(act, c, halves(YT), ACT.Copy, KB)
                s = unit(act, c)
                act_drain_T(act, c, halves(QT), ACT.Relu, KB, bias=column(sj, 1536), freed=s)
                pass_units(c, 1)
                pass_banks(c, NT)
                meet(act, c)
                qkv(True)
                elu_maps()
                linear_mix(0.125)
            if on("l2f"):
                norm_T()
                meet(act, c)

                def magnitudes(blocks=KB):
                    s = unit(act, c)
                    for k in range(blocks):
                        i = c.k.get(abs_ready.name, 0)
                        if i >= 2:
                            act.wait_ge(quantised, i - 1)
                        w, at = U(s, k * D, (k + 1) * D), (i + 1) % 2 * 512
                        act.activation(SG[:, at:at + 512], w, ACT.Sign)
                        act.activation(AB[:, at:at + 512], w, ACT.Abs).then_inc(abs_ready, 1)
                        c.next(abs_ready)
                        pass_banks(c, 1)

                magnitudes()
                for u in range(6):
                    if u < 5:
                        magnitudes()
                    else:
                        magnitudes()
                        magnitudes()
                        magnitudes(3)
                    for o in range(2 if u < 5 else 1):
                        s = await_slot(act, c)
                        act.activation(halves(HT)(2 * u + o), slot_ap(s), ACT.Silu).then_inc(drained[s], 1)
                        pass_slots(c, 1)
                pass_banks(c, NT)
                meet(act, c)
            if on("l3a"):
                norm_T()
                meet(act, c)
                sa, sbb, sc = unit(act, c), unit(act, c), unit(act, c)
                meet(act, c)
                act_drain_T(act, c, halves(YT), ACT.Relu, 1, bias=column(sbb, 1792))
                for l in range(3):
                    for q in range(NREL):
                        if q >= 2:
                            act.wait_ge(rel_used[q % 2], rel_seen[q % 2])
                        elif l > 0 and q == 0:
                            act.wait_ge(rel_used[0], rel_seen[0])
                        elif l > 0:
                            act.wait_ge(drained[0], c.now(drained[0]))
                            act.wait_ge(drained[1], c.now(drained[1]))
                        act.dma_start((B0, B1)[q % 2][0:R, :, :], rel_dram[q]).then_inc(rel_landed[q % 2], 16)
                        if q < NREL - 1:
                            rel_seen[q % 2] += 1
                        if q == 1:
                            for j in range(NT):
                                s = await_slot(act, c)
                                act.activation(REL[0:R, j, :].rearrange("p (h n) -> p h n", h=2),
                                               PS[0:R, 2 * s:2 * s + 2, 0:384], ACT.Copy).then_inc(drained[s], 1)
                    act_drain_T(act, c, halves(YT), ACT.Relu, 1, bias=column(sbb, 1793 + l))
                pass_banks(c, NT)
                pass_units(c, 1)
                pass_banks(c, NT)
                meet(act, c)
                qkv(True)
                elu_maps()
                linear_mix()
            if on("l3f"):
                norm_T()
                sd = unit(act, c)
                meet(act, c)
                meet(act, c)
                qkv(False, qbias=column(sd, 528), kbias=column(sd, 532))
                act_attend(act, c, 8, False)
                pass_banks(c, NT)
                meet(act, c)
                act_drain_transposed(act, c, YT, bias=column(sd, 536))
                pass_units(c, 1)
                pass_banks(c, NT)
                meet(act, c)
            act.dma_start(out.rearrange("(r p) d -> p r d", p=R), Xr[0:R, :, :]).then_inc(out_stored, 16)
            act.wait_ge(out_stored, 16)

        @block.vector
        def _(v):
            c = Counts()
            v.wait_ge(consts_landed, CONSTS)
            for a in range(3):
                v.tensor_copy(edges_f[0:R, a, :], edges_i[0:R, a * NCH:(a + 1) * NCH])
            meet(v, c)
            with repeat(v, c, "relation", NREL) as q:
                v.tensor_scalar(wrel[0:R, :], edges_f[0:R, 2, :], kept[0:R, bass.ds(590 + q, 1)], None,
                                ALU.is_equal).then_inc(dve_step, 1)
                v.wait_ge(dve_step, c.next(dve_step))
                anchor(v)
                with repeat(v, c, "chunk", NCH // CPI) as i:
                    for j in range(CPI):
                        v.wait_ge(onehot_used[j], c.now(onehot_used[j]))
                        c.next(onehot_used[j])
                        anchor(v)
                        col = chunk_column(q, i, j)
                        v.tensor_scalar(OH[0:R, 2 * j, :], iota[0:R, :], edges_f[0:R, 0, col], wrel[0:R, col],
                                        ALU.is_equal, ALU.mult)
                        v.tensor_scalar(OH[0:R, 2 * j + 1, :], iota[0:R, :], edges_f[0:R, 1, col], None,
                                        ALU.is_equal).then_inc(onehot_ready, 1)
                        c.next(onehot_ready)
                v.wait_ge(counts_read, c.next(counts_read, NT))
                v.tensor_tensor(TOT[0:R, :, :], TOT[0:R, :, :], CNT[0:R, :, :], ALU.add).then_inc(counts_added, 1)
                v.wait_ge(counts_added, c.next(counts_added))
            anchor(v)
            meet(v, c)
            with repeat(v, c, "feature", NCH // FPI) as i:
                for b in range(3):
                    for j in range(CPI):
                        if j < CPI - 1:
                            v.wait_ge(feat_used[j], c.now(feat_used[j]))
                            c.next(feat_used[j])
                        else:
                            p = fe_used[(b - 1) % 3]
                            v.wait_ge(p, c.at(p, c.k.get(p.name, 0)))
                            c.next(fe_used[b])
                        anchor(v)
                        v.tensor_scalar(OHF[0:R, j, :], iota[0:R, :], edges_f[0:R, 0, bass.ds(i * FPI + (b * CPI + j), 1)],
                                        None, ALU.is_equal).then_inc(feat_onehot_ready, 1)
                        c.next(feat_onehot_ready)
            meet(v, c)
            v.tensor_scalar(CNT[0:R, :, :], TOT[0:R, :, :], 1.0, None, ALU.max).then_inc(elu_neg, 1)
            c.next(elu_neg)
            v.tensor_scalar(TOT[0:R, :, :], TOT[0:R, :, :], 1.0, -MASKED, ALU.min, ALU.mult).then_inc(dve_step, 1)
            v.wait_ge(dve_step, c.next(dve_step))
            v.tensor_scalar(TOT[0:R, :, :], TOT[0:R, :, :], MASKED, None, ALU.add).then_inc(dve_step, 1)
            v.wait_ge(dve_step, c.next(dve_step))
            v.wait_ge(elu_exp, c.next(elu_exp))
            v.scalar_tensor_tensor(out=B1[0:R, :, :], in0=CNT[0:R, :, :], scalar=float(np.sqrt(128.0)),
                                   in1=TOT[0:R, :, :], op0=ALU.mult, op1=ALU.add)
            v.scalar_tensor_tensor(out=CNT[0:R, :, :], in0=CNT[0:R, :, :], scalar=8.0,
                                   in1=TOT[0:R, :, :], op0=ALU.mult, op1=ALU.add)
            meet(v, c)
            pass_slots(c, NT)
            meet(v, c)

            def norm_X():
                dve_norm(v, c, Xr, XNr)
                pass_banks(c, NT)

            def qkv_tail(krow, kbias=None, vbias=None, values=True):
                pass_units(c, 1)
                pass_slots(c, KB)
                s = unit(v, c)
                if krow:
                    row = None if kbias is None else (lambda r: kbias)
                    dve_drain_rows(v, c, lambda r: Kr[0:R, r, :], row=row, freed=(s,))
                else:
                    pass_slots(c, KB)
                s = unit(v, c)
                if values:
                    dve_values(v, c, s, bias=vbias)
                else:
                    row = None if vbias is None else (lambda r: vbias)
                    dve_drain_rows(v, c, lambda r: V[0:R, r, 0:D], row=row, freed=(s,))
                meet(v, c)

            def linear_mix(guard):
                meet(v, c)
                dve_linear_attend(v, c, guard)
                meet(v, c)
                pass_banks(c, NT)
                s = unit(v, c)
                dve_accumulate(v, c, Xr, (s,))
                meet(v, c)

            def elu_maps():
                dve_elu(v, c, Q0[:, 0:KB * NP], Y0[:, 0:KB * NP], 128)
                dve_elu(v, c, K0[0:R, 0:NT * D], A0[0:R, 0:NT * D], R)

            if on("l0a"):
                norm_X()
                meet(v, c)
                sa, sbb = unit(v, c), unit(v, c)
                qkv_tail(False, values=False)
                dve_attend(v, c, 8, 64, B0, 0.125)
                meet(v, c)
                pass_banks(c, NT)
                s = unit(v, c)
                dve_accumulate(v, c, Ar, (s,), row=XNr)
                await_own_banks(v, c)
                dve_norm(v, c, Ar, Ar, gain=U(sa, 0, 512, R), shift=U(sa, 512, 1024, R), signal=rows_ready)
                pass_banks(c, NT)
                pass_slots(c, 1)
                dve_accumulate(v, c, Ar, ())
                await_own_banks(v, c)
                for r in range(NT):
                    v.tensor_tensor(Ar[0:R, r, :], Ar[0:R, r, :], U(sbb, 0, 512, R), ALU.add).then_inc(dve_step, 1)
                    c.next(dve_step)
                v.wait_ge(dve_step, c.now(dve_step))
                dve_norm(v, c, Ar, Ar, gain=U(sa, 1024, 1536, R), shift=U(sa, 1536, 2048, R), signal=dve_step)
                v.wait_ge(dve_step, c.now(dve_step))
                for r in range(NT):
                    v.tensor_tensor(Xr[0:R, r, :], Xr[0:R, r, :], Ar[0:R, r, :], ALU.add)
                meet(v, c)
                sc = unit(v, c)
                for a in range(2):
                    v.tensor_scalar(wts[:, 4 * a:4 * a + 4], U(sc, 1024 + 4 * a, 1028 + 4 * a),
                                    U(sc, 1032 + 2 * a, 1033 + 2 * a), U(sc, 1033 + 2 * a, 1034 + 2 * a),
                                    ALU.mult, ALU.add)
                meet(v, c)
                qkv_tail(False, vbias=U(sc, 0, 512, R))
                for j in range(KB):
                    b = c.slot % 2
                    pass_slots(c, 1)
                    v.wait_ge(drained[b], c.now(drained[b]))
                    s = await_slot(v, c)
                    v.tensor_tensor(halves(YT)(j), slot_ap(s), TMP[:, j % 2, :].rearrange("p (h n) -> p h n", h=2),
                                    ALU.mult).then_inc(drained[s], 1)
                for r in range(NT):
                    b = c.bank % 4
                    pass_banks(c, 1)
                    v.wait_ge(bank_drained[b], c.now(bank_drained[b]))
                    b = await_bank(v, c)
                    v.tensor_tensor(Ar[0:R, r, :], PS[0:R, 4 + b, :], TMP[0:R, r % 2, 0:D],
                                    ALU.mult).then_inc(bank_drained[b], 1)
                linear_mix((ALU.add, 1.0e-6))
            if on("l0f"):
                norm_X()
                meet(v, c)
                sd = unit(v, c)
                dve_gate(v, c, row=U(sd, 32, 40, R))
                meet(v, c)
                pass_slots(c, 1)
                dve_accumulate(v, c, Xr, ())
                meet(v, c)
                with repeat(v, c, "expert0", 2) as i:
                    for e in range(4):
                        pass_units(c, 1)
                        pass_slots(c, KB)
                        s = unit(v, c)
                        dve_expert(v, c, lambda r: combv[0:R, r, bass.ds(i * 4 + e, 1)], (s,))
                meet(v, c)
            if on("l1a"):
                norm_X()
                meet(v, c)
                se = unit(v, c)
                dve_embedding(v, c, se)
                for r in range(NT):
                    v.tensor_copy(Gr[0:R, r, :], XNr[0:R, r, :])
                pass_slots(c, 2)
                meet(v, c)
                with repeat(v, c, "block", NBLK):
                    sf, sg = unit(v, c), unit(v, c)
                    dve_norm(v, c, Gr, Ar, cond=True)
                    meet(v, c)
                    pass_banks(c, NT)
                    qkv_tail(False, vbias=U(sf, 1024, 1536, R), values=False)
                    dve_attend(v, c, 4, 128, B1, 128.0 ** -0.5)
                    meet(v, c)
                    pass_banks(c, NT)
                    s = unit(v, c)
                    dve_accumulate(v, c, Gr, (s,))
                    await_own_banks(v, c)
                    dve_norm(v, c, Gr, Ar, cond=True)
                    meet(v, c)
                    pass_banks(c, NT)
                    pass_units(c, 1)
                    pass_slots(c, KB)
                    meet(v, c)
                    s = unit(v, c)
                    dve_accumulate(v, c, Gr, (s,))
                    pass_banks(c, 1)
                    meet(v, c)
                for r in range(NT):
                    v.tensor_tensor(Xr[0:R, r, :], Xr[0:R, r, :], Gr[0:R, r, :], ALU.add)
                meet(v, c)
                sg, sh = unit(v, c), unit(v, c)
                dve_norm(v, c, XNr, Ar, gain=U(sg, 0, 512, R), shift=U(sg, 512, 1024, R), signal=rows_ready)
                pass_banks(c, NT)
                qkv_tail(True, kbias=U(sg, 1024, 1536, R), vbias=U(sg, 1536, 2048, R))
                elu_maps()
                linear_mix((ALU.add, 1.0e-8))
            if on("l1f"):
                norm_X()
                meet(v, c)
                pass_units(c, 1)
                dve_gate(v, c)
                meet(v, c)
                with repeat(v, c, "expert1", 2) as i:
                    for e in range(4):
                        pass_units(c, 2)
                        pass_slots(c, 2 * KB)
                        s, s2 = unit(v, c), unit(v, c)
                        dve_expert(v, c, lambda r: combv[0:R, r, bass.ds(i * 4 + e, 1)], (s, s2))
                for half in range(2):
                    s, s2 = unit(v, c), unit(v, c)
                    dve_gated(v, c, range(4 * half, 4 * half + 4), (s, s2))
                s, s2 = unit(v, c), unit(v, c)
                dve_accumulate(v, c, Xr, (s, s2))
                meet(v, c)
            if on("l2a"):
                norm_X()
                meet(v, c)
                pass_units(c, 1)
                meet(v, c)
                pass_slots(c, 2 * KB)
                pass_units(c, 1)
                s = unit(v, c)
                dve_accumulate(v, c, Xr, (s,))
                meet(v, c)
                qkv_tail(True)
                elu_maps()
                linear_mix(None)
            if on("l2f"):
                norm_X()
                meet(v, c)
                us = []

                def scales(blocks=KB):
                    us.append(unit(v, c))
                    for k in range(blocks):
                        b = await_bank(v, c)
                        i = c.k.get(abs_ready.name, 0)
                        at = (i + 1) % 2 * 512
                        c.next(abs_ready)
                        if i >= 2:
                            v.wait_ge(quantised, i - 1)
                        sc, q = SC[:, at:at + 512], QZ[:, at:at + 512]
                        v.tensor_scalar(sc, PS[:, 4 + b, :], 1.0 / 128, 1.0e-5, ALU.mult, ALU.add).then_inc(bank_drained[b], 1)
                        v.wait_ge(bank_drained[b], c.now(bank_drained[b]))
                        v.scalar_tensor_tensor(out=q, in0=sc, scalar=0.5, in1=AB[:, at:at + 512], op0=ALU.mult,
                                               op1=ALU.is_lt).then_inc(dve_step, 1)
                        v.wait_ge(dve_step, c.next(dve_step))
                        v.tensor_tensor(q, q, sc, ALU.mult).then_inc(scaled, 1)

                scales()
                for u in range(6):
                    if u < 5:
                        scales()
                    else:
                        scales()
                        scales()
                        scales(3)
                    dve_gated(v, c, range(2 * u, 2 * u + (2 if u < 5 else 1)), (us[u],))
                dve_accumulate(v, c, Xr, (us[6], us[7], us[8]))
                meet(v, c)
            if on("l3a"):
                norm_X()
                meet(v, c)
                sa, sbb, sc = unit(v, c), unit(v, c), unit(v, c)
                meet(v, c)
                pass_slots(c, 1 + 3 * (NT + 1))
                for row, free in ((U(sbb, 1280, 1792, R), False), (U(sc, 0, 512, R), True)):
                    s = unit(v, c) if free else None
                    for r in range(NT):
                        b = await_bank(v, c)
                        if free and r == NT - 1:
                            release(v, s)
                        tmp = P[0:R, r % 2 * 512:r % 2 * 512 + 512]
                        v.tensor_tensor(tmp, PS[0:R, 4 + b, :], row, ALU.add).then_inc(bank_drained[b], 1)
                        v.wait_ge(bank_drained[b], c.now(bank_drained[b]))
                        v.scalar_tensor_tensor(out=Xr[0:R, r, :], in0=tmp, scalar=0.0, in1=Xr[0:R, r, :],
                                               op0=ALU.max, op1=ALU.add).then_inc(dve_step, 1)
                        c.next(dve_step)
                    v.wait_ge(dve_step, c.now(dve_step))
                meet(v, c)
                qkv_tail(True)
                elu_maps()
                linear_mix((ALU.max, 1.0e-4))
            if on("l3f"):
                norm_X()
                sd = unit(v, c)
                meet(v, c)
                for k in range(KB):
                    y, x = YT[:, k, 0:N], XTt[:, k, 0:N]
                    w = [U(sd, 512 + 3 * k + j, 513 + 3 * k + j) for j in range(3)]

                    def settle(ins):
                        ins.then_inc(dve_step, 1)
                        v.wait_ge(dve_step, c.next(dve_step))

                    settle(v.tensor_scalar(y, x, w[1], U(sd, 524 + k, 525 + k), ALU.mult, ALU.add))
                    settle(v.scalar_tensor_tensor(out=y[:, 1:N], in0=x[:, 0:N - 1], scalar=w[0], in1=y[:, 1:N],
                                                  op0=ALU.mult, op1=ALU.add))
                    settle(v.scalar_tensor_tensor(out=y[:, 0:N - 1], in0=x[:, 1:N], scalar=w[2], in1=y[:, 0:N - 1],
                                                  op0=ALU.mult, op1=ALU.add))
                    v.tensor_tensor(y, y, x, ALU.add)
                meet(v, c)
                qkv_tail(False, values=False)
                dve_attend_top(v, c, 8, 64, 512.0 ** -0.5)
                meet(v, c)
                pass_banks(c, NT)
                s = unit(v, c)
                dve_accumulate(v, c, Xr, (s,))
                meet(v, c)


UNITS = {"edges": 0, "l0a": 11, "l0f": 17, "l1a": 39, "l1f": 39, "l2a": 7, "l2f": 9, "l3a": 8, "l3f": 5}


def blocks_of(w, k=None):
    w = np.asarray(w)
    return w.reshape(-1, 128, w.shape[1]).transpose(1, 0, 2).reshape(128, -1)


def columns_of(b):
    return np.asarray(b).reshape(-1, 128).T


def row_of(b):
    return np.broadcast_to(np.asarray(b).reshape(1, -1), (128, np.asarray(b).size))


def below(*parts):
    parts = [np.asarray(p) for p in parts]
    u = np.zeros((128, parts[0].shape[1]), np.float32)
    at = 0
    for p in parts:
        u[at:at + len(p)] = p
        at += len(p)
    return u


def diagonal(g):
    u = np.zeros((128, 128), np.float32)
    u[0:64, 0:64] = g
    u[64:128, 64:128] = g
    return u


def units_of(a):
    out = []

    def put(*parts):
        u = np.zeros((128, UC), np.float32)
        at = 0
        for p in parts:
            u[:, at:at + p.shape[1]] = p
            at += p.shape[1]
        assert at <= UC
        out.append(u)

    def mats(*ws):
        for w in ws:
            put(blocks_of(w))

    g = lambda layer: (lambda n: np.asarray(a[f"{layer}_{n}"]))
    w = g("L0_gnn")
    put(row_of(w("ln1_g")), row_of(w("ln1_b")), row_of(w("ln2_g")), row_of(w("ln2_b")))
    put(row_of(w("b2")), columns_of(w("b1")), np.zeros((128, 3), np.float32), blocks_of(w("W1")), blocks_of(w("W2")))
    mats(w("Wq"), w("Wk"), w("Wv"), w("Wo"))
    w = g("L0_mix")
    put(row_of(w("bv")), row_of(w("bp")), columns_of(w("bq")), columns_of(w("bk")), row_of(w("gamma_q")),
        row_of(w("beta_q")), row_of(w("gamma_k")), row_of(w("beta_k")),
        diagonal(w("qG1")), diagonal(w("qG2")), diagonal(w("kG1")), diagonal(w("kG2")))
    mats(w("Wq"), w("Wk"), w("Wv"), w("Wp"))
    w = g("L0_ffn")
    put(blocks_of(w("Wg")), row_of(w("bg")), columns_of(w("b1")), below(w("b2")))
    for e in range(NEXP):
        mats(w("W1")[e], w("W2")[e])
    w = g("L1_gnn")
    freqs = np.arange(1, 33, dtype=np.float32) * np.float32(2.0 * np.pi / 16)
    turn = np.zeros((64, 1), np.float32)
    turn[32:] = np.float32(np.pi / 2)
    put(below(w("f_w1")), below(w("f_w2")), below(w("f_b1")[:, None]), below(w("f_b2")[:, None]),
        below(freqs[:, None], freqs[:, None]), below(turn))
    for i in range(NBLK):
        put(row_of(w("bo")[i]), row_of(w("m_b2")[i]), row_of(w("bv")[i]), columns_of(w("bq")[i]),
            columns_of(w("bk")[i]), columns_of(w("m_b1")[i]))
        put(*[below(w(f"{n}_w")[i], w(f"{n}_b")[i][None]) for n in ("s1", "b1", "s2", "b2")])
        mats(*[w(n)[i] for n in ("wq", "wk", "wv", "wo", "m_w1", "m_w2")])
    w = g("L1_mix")
    qkv, b = w("qkv_w").T, w("qkv_b")
    put(row_of(w("ln_gamma")), row_of(w("ln_beta")), row_of(b[D:2 * D]), row_of(b[2 * D:]))
    put(row_of(w("out_b")), columns_of(b[0:D]))
    mats(qkv[:, 0:D], qkv[:, D:2 * D], qkv[:, 2 * D:], w("out_w").T)
    w = g("L1_ffn")
    put(blocks_of(w("gate_w").T))
    for e in range(NEXP):
        w1, w2 = w("w1")[e].T, w("w2")[e].T
        mats(w1[:, 0:D], w1[:, D:], w2[0:D], w2[D:])
    for h in range(2):
        mats(w("sg_gate").T[:, h * D:(h + 1) * D], w("sg_up").T[:, h * D:(h + 1) * D])
    mats(w("sg_down").T[0:D], w("sg_down").T[D:])
    w = g("L2_gnn")
    put(below(w("W_edge"), w("b_edge")[None]), row_of(w("b2")), row_of(a["L2_mix_b_proj"]), columns_of(w("b1")))
    mats(w("W1"), w("W2"))
    w = g("L2_mix")
    qkv = w("w_qkv").T
    mats(qkv[:, 0:D], qkv[:, D:2 * D], qkv[:, 2 * D:], w("w_proj").T)
    w = g("L2_ffn")
    wg, wu, wd = w("w_gate").T, w("w_up").T, w("w_down").T
    for u in range(6):
        m = np.zeros((D, 512), np.float32)
        n = 256 if u < 5 else 128
        m[:, 0:n] = wg[:, u * 256:u * 256 + n]
        m[:, 256:256 + n] = wu[:, u * 256:u * 256 + n]
        mats(m)
    mats(wd[0:D], wd[D:2 * D], wd[2 * D:])
    w = g("L3_gnn")
    rel = lambda n: w(n).transpose(1, 0, 2).reshape(128, NREL * 128)
    put(blocks_of(w("W_lower")), rel("W1"), rel("W2"))
    put(rel("W3"), w("W_upper"), row_of(w("b_upper")), *[columns_of(w(n)) for n in ("b_lower", "b1", "b2", "b3")])
    put(row_of(w("b_skip")), row_of(a["L3_mix_b_out"]))
    mats(w("W_skip"))
    w = g("L3_mix")
    qkv = w("W_qkv").T
    mats(qkv[:, 0:D], qkv[:, D:2 * D], qkv[:, 2 * D:], w("W_out").T)
    w = g("L3_ffn")
    b = w("qkv_b")
    put(row_of(w("wo_b")), w("pos_w").reshape(KB, 128, 3).transpose(1, 0, 2).reshape(128, 3 * KB),
        columns_of(w("pos_b")), columns_of(b[0:D]), columns_of(b[D:2 * D]), columns_of(b[2 * D:]))
    qkv = w("qkv_w").T
    mats(qkv[:, 0:D], qkv[:, D:2 * D], qkv[:, 2 * D:], w("wo_w").T)
    assert len(out) == sum(UNITS.values())
    return np.stack(out)


def arrays_of(a):
    ids = np.stack([np.asarray(a[n]).reshape(NCH, R).T for n in ("src", "dst", "edge_type_6")], 1)
    feats = np.ones((E, EF), np.float32)
    feats[:, 0:64] = np.asarray(a["edge_attr_64"])
    feats[:, 64:96] = np.asarray(a["edge_attr_32"])
    return {
        "x": np.asarray(a["x"]),
        "edges": np.ascontiguousarray(ids.reshape(R, 3 * NCH)),
        "feats": np.ascontiguousarray(feats.reshape(NCH // CPI, CPI, R, EF).transpose(0, 2, 1, 3)
                                      .reshape(NCH // CPI, R, CPI * EF)),
        "noise": np.ascontiguousarray(np.broadcast_to(np.asarray(a["node_vec1"]).reshape(1, N), (64, N))),
        "units": units_of(a),
        "ident": np.eye(128, dtype=np.float32),
        "iota": np.ascontiguousarray(np.broadcast_to(np.arange(NP, dtype=np.float16), (R, NP))),
        "iota8": np.ascontiguousarray(np.broadcast_to(np.arange(8, dtype=np.float32), (128, 8))),
        "relations": np.ascontiguousarray(np.broadcast_to(np.arange(NREL, dtype=np.float32), (R, NREL))),
    }


def kernel(**inputs):
    import concourse.bacc as bacc
    from concourse.bass_utils import run_bass_kernel_spmd

    arrays = arrays_of(inputs)
    nc = bacc.Bacc("TRN2", target_bir_lowering=False, num_devices=1)
    t = {n: nc.dram_tensor(f"in_{n}", x.shape, mybir.dt.from_np(x.dtype), kind="ExternalInput").ap()
         for n, x in arrays.items()}
    out = nc.dram_tensor("out", (N, D), F32, kind="ExternalOutput").ap()
    gps_network(nc, t, out, sum(UNITS.values()))
    r = run_bass_kernel_spmd(nc, [{f"in_{n}": x for n, x in arrays.items()}], core_ids=[0])
    return r.results[0]["out"]
```

```python
from contextlib import ExitStack, contextmanager

import numpy as np

import concourse.bass as bass
from concourse import mybir

ALU = mybir.AluOpType
ACT = mybir.ActivationFunctionType
AX = mybir.AxisListType
F32 = mybir.dt.float32
F16 = mybir.dt.float16
BF16 = mybir.dt.bfloat16
I32 = mybir.dt.int32
U32 = mybir.dt.uint32

N = 625
D = 512
R = 125
NT = N // R
KB = D // 128
NP = N + 1
HALF = NP // 2
E = 20625
NCH = E // R
CPI = 5
FPI = 15
EF = 97
NREL = 6
WD = 32
NW = -(-N // WD)
WC = NREL * WD
WS = NT * WC
GC = 3
NG = NCH // GC
GW = 5
FAR = 64
TB = 2560
VS = 520
UC = 2048
RING = 8
NEXP = 8
SUMS = 35
FB = 11
NBLK = 4
MASKED = -1.0e30
LEAST = -3.0e38
LN_EPS = 1.0e-5
TAU = 2 * np.pi
TAU_A = 6.28125
TAU_B = round((TAU - TAU_A) * 2 ** 20) / 2 ** 20
TAU_C = float(TAU - TAU_A - TAU_B)
ROUND = 1.5 * 2 ** 23

RINGS = {f"unit_full{s}": 16 for s in range(RING)} | {f"unit_free{s}": 1 for s in range(RING)}


def each(name, per, count):
    return {f"{name}{i}": per for i in range(count)}


LOOPS = {
    "window": each("window_filled", 1, 2) | each("window_read", 1, 2) | each("window_stored", 16, 2)
              | each("window_added", 1, 2) | dict(key_ready=2, pool_step=2 * (NREL - 2)),
    "feature": dict(feat_onehot_ready=FPI, feat_first=3, feat_left=3, feat_second=3, feat_split=3) | each("feat_landed", 16, 3)
               | each("feat_used", FPI // CPI, CPI - 1) | each("fe_used", 1, 3),
    "expert0": RINGS | each("filled", 8, 2) | each("drained", 8, 2) | each("bank_filled", 5, 4)
               | each("bank_drained", 5, 4),
    "expert1": {k: 2 * v for k, v in RINGS.items()} | each("filled", 16, 2) | each("drained", 16, 2)
               | each("bank_filled", 5, 4) | each("bank_drained", 5, 4),
    "block": RINGS | each("filled", 31, 2) | each("drained", 31, 2)
             | each("bank_filled", 9, 4) | each("bank_drained", 9, 4)
             | dict(arrived=24, dve_step=40, pool_step=2, var_ready=2, rstd_ready=2,
                    max_ready=20, exp_done=20),
}


class Counts:

    def __init__(self):
        self.k, self.loops, self.slot, self.bank, self.unit = {}, [], 0, 0, 0

    def at(self, sem, k):
        for reg, per in self.loops:
            if per.get(sem.name, 0):
                k = reg * per[sem.name] + k
        return k

    def now(self, sem):
        return self.at(sem, self.k.get(sem.name, 0))

    def next(self, sem, by=1):
        self.k[sem.name] = self.k.get(sem.name, 0) + by
        return self.now(sem)


@contextmanager
def repeat(eng, c, name, times):
    with eng.Fori(0, times) as i:
        began = dict(c.k)
        c.loops.append((i, LOOPS[name]))
        yield i
        for sem, k in list(c.k.items()):
            by = k - began.get(sem, 0)
            if by:
                assert LOOPS[name].get(sem) == by, (name, sem, by, LOOPS[name].get(sem))
                c.k[sem] = k + (times - 1) * by
        c.loops.pop()


def gps_network(nc, t, out, n_units):
    rel_dram = nc.dram_tensor("relation_counts", (NW, R, WS), F32, kind="Internal").ap()

    with ExitStack() as ctx:
        def sb(name, cols, dt=F32):
            return ctx.enter_context(nc.sbuf_tensor(name, [128, cols], dt))

        def sem(name):
            return ctx.enter_context(nc.semaphore(name))

        ring = sb("ring", RING * UC)
        X, XN, G, XT = sb("X", TB), sb("XN", TB), sb("G", TB), sb("XT", TB)
        arena = sb("arena", 4 * TB + NT * VS)
        biases = sb("biases", 2 * NT * NP)
        P = sb("P", 2 * NP)
        PT = sb("PT", 2 * N)
        AGT = sb("AGT", NP)
        KV = sb("KV", 4 * 130)
        ident, ones = sb("ident", 128), sb("ones", 128)
        iota = sb("iota", NP, F16)
        iota8 = sb("iota8", 8)
        spans = sb("spans", 3 * NW)
        ranges = sb("ranges", 3 * NW, I32)
        found = sb("found", 160)
        st = sb("st", NT * 6)
        mv = sb("mv", NT * 2)
        rs, hf = sb("rs", NT), sb("hf", NT)
        mx, nm = sb("mx", 4), sb("nm", 4)
        Z, rz = sb("Z", 16), sb("rz", 16)
        top, topi, topf = sb("top", 8 * NT), sb("topi", 8 * NT, U32), sb("topf", 8 * NT)
        wts, comb = sb("wts", 4 * NT), sb("comb", 8 * NT)
        kept = sb("kept", 600)
        emb, cond = sb("emb", NP), sb("cond", NP)

        def rows(buf, cols=D):
            return buf[:, 0:NT * cols].rearrange("p (r d) -> p r d", r=NT)

        def trans(buf, blocks=KB):
            return buf[:, 0:blocks * NP].rearrange("p (k n) -> p k n", k=blocks)

        Q0, K0, V0, A0, Y0 = (arena[:, a:b] for a, b in
                              ((0, TB), (TB, 2 * TB), (2 * TB, 2 * TB + NT * VS),
                               (2 * TB + NT * VS, 3 * TB + NT * VS), (3 * TB + NT * VS, 4 * TB + NT * VS)))
        Xr, XNr, Gr, XTt = rows(X), rows(XN), rows(G), trans(XT)
        QT, KT, YT, Ar = trans(Q0), trans(K0), trans(Y0), rows(A0)
        Kr, V = rows(K0), V0.rearrange("p (r d) -> p r d", r=NT)
        HT = arena[:, 0:FB * NP].rearrange("p (k n) -> p k n", k=FB)
        REL = arena[:, 0:NT * 768].rearrange("p (r d) -> p r d", r=NT)
        TOTW = arena[:, 0:NT * NW * WD].rearrange("p (r n) -> p r n", r=NT)
        TOT = TOTW[:, :, 0:NP]
        CNT = arena[:, NT * NW * WD:NT * NW * WD + NT * NP].rearrange("p (r n) -> p r n", r=NT)
        onehots = arena[:, 2 * NT * NW * WD:2 * NT * NW * WD + NT * NP]
        OH = onehots[:, 0:GC * NP // 2].bitcast(BF16).rearrange("p (b n) -> p b n", b=GC)
        OK = onehots[:, GC * NP // 2:GC * (NP + WC) // 2].bitcast(BF16).rearrange("p (b n) -> p b n", b=GC)
        OHF = onehots[:, 0:CPI * NP // 2].bitcast(BF16).rearrange("p (b n) -> p b n", b=CPI)
        at = 2 * NT * NW * WD + CPI * NP // 2
        parts = arena[:, at:at + (3 * CPI * 3 * EF + 1) // 2 + 1].bitcast(BF16)[:, 0:3 * CPI * 3 * EF]
        FP = parts.rearrange("p (b j a e) -> p b j a e", b=3, j=CPI, a=3)
        at += (3 * CPI * 3 * EF + 1) // 2 + 1
        FE = arena[:, at:at + 3 * CPI * EF].rearrange("p (b n) -> p b n", b=3)
        rest = arena[:, at + 3 * CPI * EF:at + 4 * CPI * EF]
        left_over = rest[0:R, :].rearrange("p (j e) -> p j e", j=CPI)
        edges_i = G[:, 0:3 * NCH].bitcast(I32)
        edges_f = G[:, 3 * NCH:6 * NCH].rearrange("p (a c) -> p a c", a=3)
        wkey = G[:, 6 * NCH:8 * NCH].rearrange("p (b c) -> p b c", b=2)
        stage = biases[:, 0:2 * WS].rearrange("p (b q t d) -> p b q t d", b=2, q=NT, t=NREL)
        B0 = biases[:, 0:NT * NP].rearrange("p (r n) -> p r n", r=NT)
        B1 = biases[:, NT * NP:2 * NT * NP].rearrange("p (r n) -> p r n", r=NT)
        loads = [arena[:, NT * 768:NT * 768 + GW * WS], biases[:, 0:GW * WS]]
        CR = [l.rearrange("p (w q t d) -> p w q t d", w=GW, q=NT, t=NREL) for l in loads]
        Pv = P[:, :].rearrange("p (b n) -> p b n", b=2)
        TMP = Pv
        P3 = biases[:, 0:3 * NP].rearrange("p (b n) -> p b n", b=3)
        left = G[:, 0:3 * NP].rearrange("p (b n) -> p b n", b=3)
        PTv = PT[:, :].rearrange("p (b j n) -> p b j n", b=2, j=NT)
        KVv = KV[:, :].rearrange("p (j d) -> p j d", j=4)

        PS = ctx.enter_context(nc.psum_tensor("PS", [128, 8, 512], F32))

        consts_landed = sem("consts_landed")
        unit_full = [sem(f"unit_full{s}") for s in range(RING)]
        unit_free = [sem(f"unit_free{s}") for s in range(RING)]
        filled = [sem(f"filled{s}") for s in range(2)]
        drained = [sem(f"drained{s}") for s in range(2)]
        bank_filled = [sem(f"bank_filled{s}") for s in range(4)]
        bank_drained = [sem(f"bank_drained{s}") for s in range(4)]
        arrived = sem("arrived")
        dve_step, pool_step = sem("dve_step"), sem("pool_step")
        var_ready, rstd_ready, rows_ready = sem("var_ready"), sem("rstd_ready"), sem("rows_ready")
        max_ready, exp_done, masked = sem("max_ready"), sem("exp_done"), sem("masked")
        spans_ready, spans_turned = sem("spans_ready"), sem("spans_turned")
        key_ready = sem("key_ready")
        onehot_ready = sem("onehot_ready")
        onehot_used = [sem(f"onehot_used{j}") for j in range(GC)]
        window_filled = [sem(f"window_filled{b}") for b in range(2)]
        window_read = [sem(f"window_read{b}") for b in range(2)]
        window_stored = [sem(f"window_stored{b}") for b in range(2)]
        window_added = [sem(f"window_added{b}") for b in range(2)]
        feat_landed = [sem(f"feat_landed{b}") for b in range(3)]
        feat_first, feat_left, feat_second, feat_split = (
            sem(name) for name in ("feat_first", "feat_left", "feat_second", "feat_split"))
        feat_onehot_ready = sem("feat_onehot_ready")
        feat_used = [sem(f"feat_used{j}") for j in range(CPI)]
        fe_used = [sem(f"fe_used{b}") for b in range(3)]
        elu_neg, elu_exp = sem("elu_neg"), sem("elu_exp")
        z_ready = sem("z_ready")
        abs_ready, scaled, quantised = sem("abs_ready"), sem("scaled"), sem("quantised")
        rel_landed = [sem("rel_landed0"), sem("rel_landed1")]
        passed = sem("passed")
        out_stored = sem("out_stored")
        CONSTS = 16 * 7

        def anchor(e):
            e.sem_inc(passed, 1)

        def meet(e, c):
            if c.loops:
                anchor(e)
            e.drain().then_inc(arrived, 1)
            e.wait_ge(arrived, c.next(arrived, 4))
            anchor(e)

        def slot_ap(s, p=128):
            return PS[0:p, 2 * s:2 * s + 2, 0:HALF]

        def scores_ap(s):
            return PS[0:R, 2 * s:2 * s + 2, :].rearrange("p b n -> p (b n)")[:, 0:N]

        def take_slot(pe, c):
            s = c.slot % 2
            c.slot += 1
            pe.wait_ge(drained[s], c.now(filled[s]))
            c.next(filled[s])
            c.next(drained[s])
            return s

        def take_bank(pe, c):
            b = c.bank % 4
            c.bank += 1
            pe.wait_ge(bank_drained[b], c.now(bank_filled[b]))
            c.next(bank_filled[b])
            c.next(bank_drained[b])
            return b

        def await_slot(e, c):
            s = c.slot % 2
            c.slot += 1
            e.wait_ge(filled[s], c.next(filled[s]))
            c.next(drained[s])
            return s

        def await_bank(e, c):
            b = c.bank % 4
            c.bank += 1
            e.wait_ge(bank_filled[b], c.next(bank_filled[b]))
            c.next(bank_drained[b])
            return b

        def pass_slots(c, n):
            for _ in range(n):
                c.next(filled[c.slot % 2])
                c.next(drained[c.slot % 2])
                c.slot += 1

        def pass_banks(c, n):
            for _ in range(n):
                c.next(bank_filled[c.bank % 4])
                c.next(bank_drained[c.bank % 4])
                c.bank += 1

        def unit(e, c):
            s = c.unit % RING
            c.unit += 1
            e.wait_ge(unit_full[s], c.next(unit_full[s], 16))
            return s

        def pass_units(c, n):
            for _ in range(n):
                c.next(unit_full[c.unit % RING], 16)
                c.unit += 1

        def U(s, a=0, b=UC, p=128):
            return ring[0:p, s * UC + a:s * UC + b]

        def release(e, s):
            e.sem_inc(unit_free[s], 1)

        def pe_project_T(pe, c, s, src, ncols, outs, first=0, nk=KB, wo=0):
            for o in range(outs):
                b = take_slot(pe, c)
                for k in range(nk):
                    w = U(s, wo + k * ncols + o * 128, wo + k * ncols + o * 128 + 128)
                    for h in range(2):
                        mm = pe.matmul(PS[:, 2 * b + h, 0:HALF], w, src[:, k, h * HALF:(h + 1) * HALF],
                                       start=(k == 0), stop=(k == nk - 1))
                mm.then_inc(filled[b], 1)

        def pe_project_rows(pe, c, units, src, nk=KB, wo=0, tiles=NT):
            for r in range(tiles):
                b = take_bank(pe, c)
                blocks = [(s, k) for s, n in units for k in range(n)]
                for i, (s, k) in enumerate(blocks):
                    mm = pe.matmul(PS[0:R, 4 + b, :], src[:, i, r * R:(r + 1) * R],
                                   U(s, wo + k * D, wo + (k + 1) * D),
                                   start=(i == 0), stop=(i == len(blocks) - 1))
                mm.then_inc(bank_filled[b], 1)

        def pe_transpose_rows(pe, c, src, signalled=True):
            for r in range(NT):
                if signalled:
                    pe.wait_ge(rows_ready, c.next(rows_ready))
                b = take_bank(pe, c)
                for k in range(KB):
                    mm = pe.transpose(PS[:, 4 + b, k * R:(k + 1) * R], src[0:R, r, k * 128:(k + 1) * 128],
                                      ident[0:R, 0:R])
                mm.then_inc(bank_filled[b], 1)

        def pe_attend(pe, c, heads, dh):
            total = NT * heads
            where = {}

            def score(i):
                r, h = divmod(i, heads)
                p, k = h * dh % 128, h * dh // 128
                b = take_slot(pe, c)
                for half in range(2):
                    mm = pe.matmul(PS[0:R, 2 * b + half, 0:HALF], QT[p:p + dh, k, r * R:(r + 1) * R],
                                   KT[p:p + dh, k, half * HALF:(half + 1) * HALF], start=True, stop=True)
                mm.then_inc(filled[b], 1)

            def turn(i):
                pe.wait_ge(exp_done, c.next(exp_done))
                b = take_slot(pe, c)
                for j in range(NT):
                    mm = pe.transpose(PS[0:R, 2 * b + j // 3, j % 3 * R:(j % 3 + 1) * R],
                                      Pv[0:R, i % 2, j * R:(j + 1) * R], ident[0:R, 0:R])
                mm.then_inc(filled[b], 1)
                return b, c.now(filled[b])

            score(0)
            score(1)
            for i in range(total):
                r, h = divmod(i, heads)
                b, k = turn(i)
                if i + 2 < total:
                    score(i + 2)
                if h == 0:
                    where[r] = take_bank(pe, c)
                pe.wait_ge(drained[b], k)
                for j in range(NT):
                    mm = pe.matmul(PS[0:R, 4 + where[r], h * dh:(h + 1) * dh], PTv[0:R, i % 2, j, :],
                                   V[0:R, j, h * dh:(h + 1) * dh], start=(j == 0), stop=(j == NT - 1))
                if h == heads - 1:
                    mm.then_inc(bank_filled[where[r]], 1)

        def top_order(total):
            for i in range(-2, total):
                if i + 2 < total:
                    yield "scores", i + 2
                if i >= 0:
                    yield "turned", i

        def pe_attend_top(pe, c, heads, dh):
            for what, i in top_order(NT * heads):
                r, h = divmod(i, heads)
                if what == "scores":
                    p, k = h * dh % 128, h * dh // 128
                    b = take_slot(pe, c)
                    for half, (lo, hi) in enumerate(((0, 512), (512, N))):
                        mm = pe.matmul(PS[0:R, 2 * b + half, 0:hi - lo], QT[p:p + dh, k, r * R:(r + 1) * R],
                                       KT[p:p + dh, k, lo:hi], start=True, stop=True)
                    mm.then_inc(filled[b], 1)
                    continue
                if h == 0:
                    where = take_bank(pe, c)
                pe.wait_ge(masked, c.next(masked))
                b = take_slot(pe, c)
                for j in range(NT):
                    mm = pe.transpose(PS[0:R, 2 * b + j // 3, j % 3 * R:(j % 3 + 1) * R],
                                      P3[0:R, i % 3, j * R:(j + 1) * R], ident[0:R, 0:R])
                mm.then_inc(filled[b], 1)
                pe.wait_ge(drained[b], c.now(filled[b]))
                for j in range(NT):
                    mm = pe.matmul(PS[0:R, 4 + where, h * dh:(h + 1) * dh], PTv[0:R, i % 2, j, :],
                                   V[0:R, j, h * dh:(h + 1) * dh], start=(j == 0), stop=(j == NT - 1))
                if h == heads - 1:
                    mm.then_inc(bank_filled[where], 1)

        def pe_linear_attend(pe, c, krows):
            for j in range(4):
                b = take_bank(pe, c)
                for r in range(NT):
                    mm = pe.matmul(PS[:, 4 + b, 0:130], krows[0:R, r, j * 128:(j + 1) * 128],
                                   V[0:R, r, j * 130:(j + 1) * 130], start=(r == 0), stop=(r == NT - 1))
                mm.then_inc(bank_filled[b], 1)
            for b in range(4):
                pe.wait_ge(bank_drained[b], c.now(bank_drained[b]))
            for r in range(NT):
                b = take_slot(pe, c)
                for j in range(4):
                    mm = pe.matmul(PS[0:R, 2 * b + j // 2, j % 2 * 130:(j % 2 + 1) * 130],
                                   QT[:, j, r * R:(r + 1) * R], KVv[:, j, :], start=True, stop=True)
                mm.then_inc(filled[b], 1)

        def act_drain_T(act, c, dst, func, outs, bias=None, scale=None, freed=None):
            for o in range(outs):
                s = await_slot(act, c)
                if freed is not None and o == outs - 1:
                    release(act, freed)
                more = {}
                if bias is not None:
                    more["bias"] = bias(o)
                if scale is not None:
                    more["scale"] = scale
                act.activation(dst(o), slot_ap(s), func, **more).then_inc(drained[s], 1)

        def halves(t):
            return lambda o: t[:, o, :].rearrange("p (h n) -> p h n", h=2)

        def act_drain_transposed(act, c, dst, bias=None):
            for r in range(NT):
                b = await_bank(act, c)
                src = PS[:, 4 + b, 0:KB * R].rearrange("p (k n) -> p k n", k=KB)
                if bias is None:
                    act.activation(dst[:, :, r * R:(r + 1) * R], src, ACT.Copy).then_inc(bank_drained[b], 1)
                else:
                    for k in range(KB):
                        ins = act.activation(dst[:, k, r * R:(r + 1) * R], src[:, k, :], ACT.Identity, bias=bias(k))
                    ins.then_inc(bank_drained[b], 1)

        def act_attend(act, c, heads):
            total = NT * heads

            def exps(i):
                r, h = divmod(i, heads)
                act.wait_ge(max_ready, c.next(max_ready))
                act.activation(Pv[0:R, i % 2, :], Pv[0:R, i % 2, :], ACT.Exp, bias=nm[0:R, i % 4:i % 4 + 1],
                               accum_out=Z[0:R, r % 2 * 8 + h:r % 2 * 8 + h + 1]).then_inc(exp_done, 1)
                c.next(exp_done)

            pass_slots(c, 2)
            exps(0)
            exps(1)
            for i in range(total):
                s = await_slot(act, c)
                act.activation(PTv[0:R, i % 2, 0:3, :], PS[0:R, 2 * s, 0:3 * R].rearrange("p (j n) -> p j n", j=3),
                               ACT.Copy)
                act.activation(PTv[0:R, i % 2, 3:5, :], PS[0:R, 2 * s + 1, 0:2 * R].rearrange("p (j n) -> p j n", j=2),
                               ACT.Copy).then_inc(drained[s], 1)
                if i + 2 < total:
                    pass_slots(c, 1)
                    exps(i + 2)

        def act_attend_top(act, c, heads, scale):
            ahead = []

            def exps():
                i, s = ahead.pop(0)
                act.wait_ge(max_ready, c.next(max_ready))
                act.activation(P3[0:R, i % 3, 0:N], scores_ap(s), ACT.Exp, bias=nm[0:R, i % 4:i % 4 + 1],
                               scale=scale).then_inc(drained[s], 1)

            for what, i in top_order(NT * heads):
                if what == "scores":
                    s = c.slot % 2
                    pass_slots(c, 1)
                    ahead.append((i, s))
                    if i < 2:
                        exps()
                    continue
                s = await_slot(act, c)
                act.activation(PTv[0:R, i % 2, 0:3, :], PS[0:R, 2 * s, 0:3 * R].rearrange("p (j n) -> p j n", j=3),
                               ACT.Copy)
                act.activation(PTv[0:R, i % 2, 3:5, :], PS[0:R, 2 * s + 1, 0:2 * R].rearrange("p (j n) -> p j n", j=2),
                               ACT.Copy).then_inc(drained[s], 1)
                if ahead:
                    exps()

        def act_linear_attend(act, c, scale):
            for j in range(4):
                b = await_bank(act, c)
                act.activation(KVv[0:64, j, 0:65], PS[0:64, 4 + b, 0:65], ACT.Copy, scale=scale)
                act.activation(KVv[64:128, j, 65:130], PS[64:128, 4 + b, 65:130], ACT.Copy,
                               scale=scale).then_inc(bank_drained[b], 1)
            pass_slots(c, NT)

        def dve_norm(v, c, src, dst, gain=None, shift=None, cond=False, signal=None, stats=True):
            for r in range(NT if stats else 0):
                v.bn_stats(st[0:R, 6 * r:6 * r + 6], src[0:R, r, :]).then_inc(dve_step, 1)
                c.next(dve_step)
            v.wait_ge(dve_step, c.now(dve_step))
            anchor(v)
            for r in range(NT):
                ins = v.bn_aggr(mv[0:R, 2 * r:2 * r + 2], st[0:R, 6 * r:6 * r + 6])
            ins.then_inc(var_ready, 1)
            c.next(var_ready)
            v.wait_ge(rstd_ready, c.next(rstd_ready))
            for r in range(NT):
                ins = v.tensor_scalar(dst[0:R, r, :], src[0:R, r, :], mv[0:R, 2 * r:2 * r + 1], rs[0:R, r:r + 1],
                                      ALU.subtract, ALU.mult)
                if gain is None and not cond:
                    ins.then_inc(rows_ready, 1)
                    k = c.next(rows_ready)
                else:
                    ins.then_inc(dve_step, 1)
                    k = c.next(dve_step)
            if gain is not None:
                v.wait_ge(dve_step, k)
                for r in range(NT):
                    v.tensor_tensor(dst[0:R, r, :], dst[0:R, r, :], gain, ALU.mult).then_inc(dve_step, 1)
                    k = c.next(dve_step)
                v.wait_ge(dve_step, k)
                for r in range(NT):
                    v.tensor_tensor(dst[0:R, r, :], dst[0:R, r, :], shift, ALU.add).then_inc(signal, 1)
                    c.next(signal)
            if cond:
                for r in range(NT):
                    s = await_slot(v, c)
                    if r == 0:
                        v.wait_ge(dve_step, k)
                    v.scalar_tensor_tensor(out=dst[0:R, r, :], in0=PS[0:R, 2 * s, :], scalar=1.0,
                                           in1=dst[0:R, r, :], op0=ALU.add, op1=ALU.mult).then_inc(dve_step, 1)
                    v.wait_ge(dve_step, c.next(dve_step))
                    v.tensor_tensor(dst[0:R, r, :], PS[0:R, 2 * s + 1, :], dst[0:R, r, :],
                                    ALU.add).then_inc(drained[s], 1)

        def pool_rstd(g, c):
            g.wait_ge(var_ready, c.next(var_ready))
            anchor(g)
            g.tensor_scalar(rs[0:R, :], mv[0:R, :].rearrange("p (r a) -> p r a", a=2)[:, :, 1], LN_EPS, None,
                            ALU.add).then_inc(pool_step, 1)
            g.wait_ge(pool_step, c.next(pool_step))
            g.tensor_tensor(rs[0:R, :], rs[0:R, :], hf[0:R, :], ALU.pow).then_inc(rstd_ready, 1)
            c.next(rstd_ready)

        def dve_drain_rows(v, c, dst, row=None, freed=()):
            for r in range(NT):
                b = await_bank(v, c)
                if r == NT - 1:
                    for s in freed:
                        release(v, s)
                p = PS[0:R, 4 + b, :]
                if row is None:
                    ins = v.tensor_copy(dst(r), p)
                else:
                    ins = v.tensor_tensor(dst(r), p, row(r), ALU.add)
                ins.then_inc(bank_drained[b], 1)

        def tile_of(buf):
            return lambda r: buf[0:R, r, :]

        def await_own_banks(e, c):
            for b in range(4):
                e.wait_ge(bank_drained[b], c.now(bank_drained[b]))

        def await_own_slots(e, c):
            for s in range(2):
                e.wait_ge(drained[s], c.now(drained[s]))

        def dve_values(v, c, freed, bias=None):
            for r in range(NT):
                b = await_bank(v, c)
                if r == NT - 1:
                    release(v, freed)
                dst = V[0:R, r, :].rearrange("p (h d) -> p h d", d=65)[:, :, 0:64]
                src = PS[0:R, 4 + b, :].rearrange("p (h d) -> p h d", d=64)
                if bias is None:
                    ins = v.tensor_copy(dst, src)
                else:
                    ins = v.tensor_tensor(dst, src, bias.rearrange("p (h d) -> p h d", d=64), ALU.add)
                ins.then_inc(bank_drained[b], 1)

        def dve_accumulate(v, c, dst, freed, row=None, stats=False):
            row = row or dst
            if not stats:
                dve_drain_rows(v, c, tile_of(dst), row=tile_of(row), freed=freed)
                return
            for r in range(NT + 1):
                if r < NT:
                    b = await_bank(v, c)
                    if r == NT - 1:
                        for s in freed:
                            release(v, s)
                    v.tensor_tensor(dst[0:R, r, :], PS[0:R, 4 + b, :], row[0:R, r, :],
                                    ALU.add).then_inc(bank_drained[b], 1)
                if r > 0:
                    v.wait_ge(*written)
                    anchor(v)
                    v.bn_stats(st[0:R, 6 * (r - 1):6 * r], dst[0:R, r - 1, :]).then_inc(dve_step, 1)
                    c.next(dve_step)
                if r < NT:
                    written = bank_drained[b], c.now(bank_drained[b])

        def dve_attend(v, c, heads, dh, bias, scale):
            total = NT * heads

            def score(i):
                r, h = divmod(i, heads)
                s = await_slot(v, c)
                anchor(v)
                v.tensor_tensor_reduce(Pv[0:R, i % 2, :].rearrange("p (h n) -> p h n", h=2), slot_ap(s, R),
                                       bias[0:R, r, :].rearrange("p (h n) -> p h n", h=2), scale, LEAST,
                                       ALU.add, ALU.max, mx[0:R, i % 4:i % 4 + 1]).then_inc(drained[s], 1)
                v.wait_ge(drained[s], c.now(drained[s]))
                v.tensor_scalar(nm[0:R, i % 4:i % 4 + 1], mx[0:R, i % 4:i % 4 + 1], -1.0, None,
                                ALU.mult).then_inc(max_ready, 1)
                c.next(max_ready)
                c.next(exp_done)

            score(0)
            score(1)
            for i in range(total):
                pass_slots(c, 1)
                if i + 2 < total:
                    score(i + 2)
                if i % heads == 0 and i > 0:
                    norm_heads(v, c, i // heads - 1, heads, dh)
            norm_heads(v, c, NT - 1, heads, dh)

        def norm_heads(v, c, r, heads, dh):
            b = await_bank(v, c)
            z0 = r % 2 * 8
            z = Z[0:R, z0:z0 + heads]
            v.tensor_scalar(rz[0:R, z0:z0 + heads], z, 1.0e-30, None, ALU.max).then_inc(dve_step, 1)
            v.wait_ge(dve_step, c.next(dve_step))
            v.reciprocal(rz[0:R, z0:z0 + heads], rz[0:R, z0:z0 + heads]).then_inc(dve_step, 1)
            v.wait_ge(dve_step, c.next(dve_step))
            v.tensor_tensor(Ar[0:R, r, :].rearrange("p (h d) -> p h d", d=dh),
                            PS[0:R, 4 + b, :].rearrange("p (h d) -> p h d", d=dh),
                            rz[0:R, z0:z0 + heads].unsqueeze(2).to_broadcast([R, heads, dh]),
                            ALU.mult).then_inc(bank_drained[b], 1)

        def dve_linear_attend(v, c, guard):
            pass_banks(c, 4)
            for r in range(NT):
                s = await_slot(v, c)
                z0 = r % 2 * 8
                pairs = [PS[0:R, 2 * s + b, 0:260].rearrange("p (h d) -> p h d", d=65) for b in range(2)]
                if guard is not None:
                    op, amount = guard
                    for b in range(2):
                        v.tensor_scalar(rz[0:R, z0 + 4 * b:z0 + 4 * b + 4], pairs[b][:, :, 64], amount, None,
                                        op).then_inc(dve_step, 1)
                        c.next(dve_step)
                    v.wait_ge(dve_step, c.now(dve_step))
                    v.reciprocal(rz[0:R, z0:z0 + 8], rz[0:R, z0:z0 + 8]).then_inc(dve_step, 1)
                    v.wait_ge(dve_step, c.next(dve_step))
                for b in range(2):
                    dst = Ar[0:R, r, b * 256:(b + 1) * 256].rearrange("p (h d) -> p h d", d=64)
                    if guard is None:
                        ins = v.tensor_copy(dst, pairs[b][:, :, 0:64])
                    else:
                        ins = v.tensor_tensor(dst, pairs[b][:, :, 0:64],
                                              rz[0:R, z0 + 4 * b:z0 + 4 * b + 4].unsqueeze(2).to_broadcast([R, 4, 64]),
                                              ALU.mult)
                ins.then_inc(drained[s], 1)

        def dve_elu(v, c, buf, tmp, p):
            v.tensor_scalar(tmp, buf, 0.0, None, ALU.min).then_inc(elu_neg, 1)
            c.next(elu_neg)
            v.wait_ge(elu_exp, c.next(elu_exp))
            v.scalar_tensor_tensor(out=buf, in0=buf, scalar=0.0, in1=tmp, op0=ALU.max, op1=ALU.add)

        def act_elu(act, c, tmp):
            act.wait_ge(elu_neg, c.next(elu_neg))
            act.activation(tmp, tmp, ACT.Exp).then_inc(elu_exp, 1)
            c.next(elu_exp)

        def dve_gate(v, c, row=None):
            b = await_bank(v, c)
            logits = P[0:R, 0:8 * NT]
            cp = PS[0:R, 4 + b, 0:8 * NT]
            if row is None:
                v.tensor_copy(logits, cp).then_inc(bank_drained[b], 1)
            else:
                v.tensor_tensor(logits.rearrange("p (r e) -> p r e", e=8), cp.rearrange("p (r e) -> p r e", e=8),
                                row.unsqueeze(1).to_broadcast([R, NT, 8]), ALU.add).then_inc(bank_drained[b], 1)
            v.wait_ge(bank_drained[b], c.now(bank_drained[b]))
            for r in range(NT):
                v.max(top[0:R, 8 * r:8 * r + 8], logits[:, 8 * r:8 * r + 8]).then_inc(dve_step, 1)
                c.next(dve_step)
            v.wait_ge(dve_step, c.now(dve_step))
            for r in range(NT):
                ins = v.max_index(topi[0:R, 8 * r:8 * r + 8], top[0:R, 8 * r:8 * r + 8], logits[:, 8 * r:8 * r + 8])
            topv = top[0:R, :].rearrange("p (r e) -> p r e", e=8)
            w = wts[0:R, :].rearrange("p (a r) -> p a r", a=4)
            v.tensor_tensor(w[:, 0, :], topv[:, :, 1], topv[:, :, 0], ALU.subtract).then_inc(elu_neg, 1)
            c.next(elu_neg)
            v.wait_ge(elu_neg, c.now(elu_neg))
            v.tensor_copy(topf[0:R, :], topi[0:R, :]).then_inc(dve_step, 1)
            c.next(dve_step)
            v.wait_ge(elu_exp, c.next(elu_exp))
            v.tensor_scalar(w[:, 1, :], w[:, 0, :], 1.0, None, ALU.add).then_inc(dve_step, 1)
            v.wait_ge(dve_step, c.next(dve_step))
            v.reciprocal(w[:, 2, :], w[:, 1, :]).then_inc(dve_step, 1)
            v.wait_ge(dve_step, c.next(dve_step))
            v.tensor_tensor(w[:, 3, :], w[:, 0, :], w[:, 2, :], ALU.mult).then_inc(dve_step, 1)
            v.wait_ge(dve_step, c.next(dve_step))
            for r in range(NT):
                v.tensor_scalar(comb[0:R, 8 * r:8 * r + 8], iota8[0:R, :], topf[0:R, 8 * r:8 * r + 1],
                                w[:, 2, r:r + 1], ALU.is_equal, ALU.mult).then_inc(dve_step, 1)
                v.tensor_scalar(P[0:R, 64 + 8 * r:72 + 8 * r], iota8[0:R, :], topf[0:R, 8 * r + 1:8 * r + 2],
                                w[:, 3, r:r + 1], ALU.is_equal, ALU.mult).then_inc(dve_step, 1)
                c.next(dve_step, 2)
            v.wait_ge(dve_step, c.now(dve_step))
            v.tensor_tensor(comb[0:R, 0:8 * NT], comb[0:R, 0:8 * NT], P[0:R, 64:64 + 8 * NT], ALU.add)

        def act_gate(act, c):
            act.wait_ge(elu_neg, c.next(elu_neg))
            act.activation(wts[0:R, 0:NT], wts[0:R, 0:NT], ACT.Exp).then_inc(elu_exp, 1)
            c.next(elu_exp)

        def pe_gate(pe, c, s):
            b = take_bank(pe, c)
            for r in range(NT):
                for k in range(KB):
                    mm = pe.matmul(PS[0:R, 4 + b, 8 * r:8 * r + 8], XTt[:, k, r * R:(r + 1) * R],
                                   U(s, 8 * k, 8 * k + 8), start=(k == 0), stop=(k == KB - 1))
            mm.then_inc(bank_filled[b], 1)

        def dve_expert(v, c, weight, freed):
            for r in range(NT):
                p = (c.bank - 5) % 4
                b = await_bank(v, c)
                if r == NT - 1:
                    for s in freed:
                        release(v, s)
                if r == 0:
                    for q in range(4):
                        k = c.k.get(bank_drained[q].name, 0) - (q == b)
                        v.wait_ge(bank_drained[q], c.at(bank_drained[q], k))
                anchor(v)
                v.scalar_tensor_tensor(out=Xr[0:R, r, :], in0=PS[0:R, 4 + b, :], scalar=weight(r),
                                       in1=Xr[0:R, r, :], op0=ALU.mult, op1=ALU.add).then_inc(bank_drained[b], 1)

        def dve_gated(v, c, blocks, freed):
            for o in blocks:
                g = c.slot % 2
                pass_slots(c, 1)
                v.wait_ge(drained[g], c.now(drained[g]))
                s = await_slot(v, c)
                if o == blocks[-1]:
                    for f in freed:
                        release(v, f)
                v.tensor_tensor(halves(HT)(o), slot_ap(s), halves(HT)(o), ALU.mult).then_inc(drained[s], 1)

        def dve_embedding(v, c, s):
            def settle(ins):
                ins.then_inc(dve_step, 1)
                v.wait_ge(dve_step, c.next(dve_step))

            e, turns = emb[0:64, :], TMP[0:64, 0, :]
            shift = U(s, 35, 36, 64)
            settle(v.memset(emb[0:64, N:NP], 0.0))
            settle(v.tensor_scalar(e, e, U(s, 34, 35, 64), None, ALU.mult))
            settle(v.tensor_scalar(turns, e, shift, 1.0 / TAU, ALU.add, ALU.mult))
            settle(v.tensor_scalar(turns, turns, ROUND, None, ALU.add))
            settle(v.tensor_scalar(turns, turns, -ROUND, None, ALU.add))
            for part in (TAU_A, TAU_B, TAU_C):
                settle(v.scalar_tensor_tensor(out=e, in0=turns, scalar=-part, in1=e, op0=ALU.mult, op1=ALU.add))
            settle(v.tensor_scalar(e, e, shift, 3.1415925, ALU.add, ALU.min))
            v.tensor_scalar(e, e, -3.1415925, None, ALU.max).then_inc(elu_neg, 1)
            c.next(elu_neg)

        def dve_attend_top(v, c, heads, dh, scale):
            total = NT * heads

            def settle(ins):
                ins.then_inc(dve_step, 1)
                v.wait_ge(dve_step, c.next(dve_step))

            def score(i):
                s = await_slot(v, c)
                scores, rest, most = scores_ap(s), left[0:R, i % 3, 0:N], top[0:R, i % 2 * 16:i % 2 * 16 + 16]
                settle(v.max(most[:, 0:8], scores))
                settle(v.match_replace(rest, most[:, 0:8], scores, LEAST))
                v.tensor_scalar(nm[0:R, i % 4:i % 4 + 1], most[:, 0:1], -scale, None, ALU.mult).then_inc(max_ready, 1)
                settle(v.max(most[:, 8:16], rest))
                settle(v.match_replace(rest, most[:, 8:16], rest, LEAST))
                return s, c.now(drained[s])

            def select(i):
                r, h = divmod(i, heads)
                s, k = ahead.pop(i)
                v.wait_ge(drained[s], k)
                v.scalar_tensor_tensor(out=P3[0:R, i % 3, 0:N], in0=left[0:R, i % 3, 0:N], scalar=0.5 * LEAST,
                                       in1=P3[0:R, i % 3, 0:N], op0=ALU.is_lt, op1=ALU.mult,
                                       accum_out=Z[0:R, r % 2 * 8 + h:r % 2 * 8 + h + 1]).then_inc(masked, 1)
                c.next(masked)

            ahead = {}
            for i in range(-2, total):
                if i >= 0:
                    select(i)
                if i + 2 < total:
                    ahead[i + 2] = score(i + 2)
                if i >= 0:
                    pass_slots(c, 1)
                    if i % heads == 0 and i > 0:
                        norm_heads(v, c, i // heads - 1, heads, dh)
            v.wait_ge(masked, c.now(masked))
            norm_heads(v, c, NT - 1, heads, dh)

        def quantise_order():
            done = 0
            for n in range(2 * FB):
                for _ in range(done, min(SUMS, 5 + n * (SUMS - 4) // (2 * FB - 2))):
                    yield "sum", done
                    done += 1
                yield "block", n
            for i in range(done, SUMS):
                yield "sum", i

        def pool_quantise(g, c):
            i = 0
            us = [x % RING for x in range(c.unit - 9, c.unit)]
            for u, s in enumerate(us):
                for k in range(KB if u < 8 else 3):
                    i += 1
                    g.wait_ge(scaled, i)
                    at = i % 2 * 512
                    g.tensor_tensor(U(s, k * D, (k + 1) * D), SG[:, at:at + 512], QZ[:, at:at + 512],
                                    ALU.mult).then_inc(quantised, 1)

        def window_range(e, w):
            first, past, off = (e.value_load(ranges[0:1, bass.ds(w + k * NW, 1)], min_val=lo, max_val=hi)
                                for k, lo, hi in ((0, 0, NG - 1), (1, 1, NG), (2, FAR - NG, FAR + NW * NG)))
            return first, past, off

        combv = comb[:, 0:8 * NT].rearrange("p (r e) -> p r e", e=8)
        AB, SG = G[:, 0:1024], G[:, 1024:2048]
        SC, QZ = A0[:, 0:1024], A0[:, 1024:2048]

        def load_order(l):
            return (2, 3, 0, 1) if l % 2 else (0, 1, 2, 3)

        block = ctx.enter_context(nc.Block())

        @block.sync
        def _(sp):
            for dst, src in ((ident[:, :], t["ident"]), (iota[0:R, :], t["iota"]), (iota8[:, :], t["iota8"]),
                             (edges_i[0:R, :], t["edges"]), (Xr[0:R, :, :], t["x"].rearrange("(r p) d -> p r d", p=R)),
                             (emb[0:64, 0:N], t["noise"]), (spans[:, :], t["spans"])):
                sp.dma_start(dst, src).then_inc(consts_landed, 16)
            for s in range(RING):
                sp.dma_start(U(s), t["units"][s]).then_inc(unit_full[s], 16)
            c = Counts()
            sp.wait_ge(arrived, 4)
            for b in range(3):
                sp.dma_start(FE[0:R, b, :], t["feats"][b]).then_inc(feat_landed[b], 16)
                c.next(fe_used[b])
            with repeat(sp, c, "feature", NCH // FPI - 1) as i:
                for b in range(3):
                    sp.wait_ge(fe_used[b], c.next(fe_used[b]))
                    sp.dma_start(FE[0:R, b, :], t["feats"][i * 3 + (3 + b)]).then_inc(feat_landed[b], 16)
            with sp.Fori(1, n_units // RING) as i:
                for s in range(RING):
                    sp.wait_ge(unit_free[s], i)
                    sp.dma_start(U(s), t["units"][i * RING + s]).then_inc(unit_full[s], 16)
            for s in range(n_units % RING):
                sp.wait_ge(unit_free[s], n_units // RING)
                sp.dma_start(U(s), t["units"][n_units // RING * RING + s]).then_inc(unit_full[s], 16)
            sp.wait_ge(out_stored, 16)

        @block.gpsimd
        def _(g):
            c = Counts()
            g.memset(XT[:, :], 0.0)
            g.memset(arena[:, 2 * TB:], 0.0)
            g.wait_ge(consts_landed, CONSTS)
            meet(g, c)
            for buf in (P, PT, KV, AGT):
                g.memset(buf[:, :], 0.0)
            g.memset(ones[:, :], 1.0)
            g.memset(cond[:, :], 1.0)
            g.memset(hf[:, :], -0.5)
            for b in range(2):
                g.sem_inc(window_added[b], 1)
                c.next(window_added[b])
                c.next(window_read[b])
            with repeat(g, c, "window", NW // 2) as i:
                for b in range(2):
                    g.wait_ge(window_read[b], c.next(window_read[b]))
                    anchor(g)
                    dst = TOTW[0:R, :, bass.ds((i * 2 + b) * WD, WD)]
                    for k in range(1, NREL):
                        ins = g.tensor_tensor(dst, stage[0:R, b, :, 0, :] if k == 1 else dst,
                                              stage[0:R, b, :, k, :], ALU.add)
                        if k < NREL - 1:
                            ins.then_inc(pool_step, 1)
                            g.wait_ge(pool_step, c.next(pool_step))
                            anchor(g)
                    ins.then_inc(window_added[b], 1)
                    c.next(window_added[b])
            meet(g, c)
            g.sem_inc(feat_split, 1)
            c.next(feat_split)
            with repeat(g, c, "feature", NCH // FPI):
                for b in range(3):
                    g.wait_ge(feat_first, c.next(feat_first))
                    g.wait_ge(feat_split, c.now(feat_split))
                    c.next(feat_split)
                    anchor(g)
                    g.tensor_tensor(left_over, FE[0:R, b, :].rearrange("p (j e) -> p j e", j=CPI),
                                    FP[0:R, b, :, 0, :], ALU.subtract).then_inc(feat_left, 1)
                    c.next(feat_left)
            meet(g, c)
            g.memset(B0[0:R, :, N:NP], MASKED)
            meet(g, c)
            meet(g, c)

            def ones_column():
                g.memset(V[0:R, :, :].rearrange("p r (h d) -> p (r h) d", d=65)[:, :, 64:65], 1.0)

            def settle(ins):
                ins.then_inc(pool_step, 1)
                g.wait_ge(pool_step, c.next(pool_step))

            def add_rows(dst, row):
                for r in range(NT):
                    ins = g.tensor_tensor(dst[0:R, r, :], dst[0:R, r, :], row(r), ALU.add)
                settle(ins)

            def linear_mix(more=()):
                ones_column()
                for row in more:
                    add_rows(Xr, row)
                meet(g, c)
                meet(g, c)
                meet(g, c)
                meet(g, c)

            pool_rstd(g, c)
            meet(g, c)
            pass_units(c, 2)
            meet(g, c)
            meet(g, c)
            pool_rstd(g, c)
            pool_rstd(g, c)
            meet(g, c)
            pass_units(c, 4)
            s = unit(g, c)
            meet(g, c)
            linear_mix([lambda r: U(s, 512, 1024, R)])
            pass_units(c, 4)
            pool_rstd(g, c)
            meet(g, c)
            meet(g, c)
            pass_units(c, 17)
            meet(g, c)
            meet(g, c)
            pool_rstd(g, c)
            meet(g, c)
            pass_units(c, 1)
            meet(g, c)
            with repeat(g, c, "block", NBLK):
                s = unit(g, c)
                pass_units(c, 7)
                pool_rstd(g, c)
                meet(g, c)
                meet(g, c)
                for r in range(NT):
                    g.tensor_tensor(Gr[0:R, r, :], Gr[0:R, r, :], U(s, 0, 512, R), ALU.add)
                meet(g, c)
                pool_rstd(g, c)
                meet(g, c)
                for r in range(NT):
                    g.tensor_tensor(Gr[0:R, r, :], Gr[0:R, r, :], U(s, 512, 1024, R), ALU.add)
                meet(g, c)
                meet(g, c)
            meet(g, c)
            pool_rstd(g, c)
            pass_units(c, 1)
            s = unit(g, c)
            pass_units(c, 4)
            linear_mix([lambda r: U(s, 0, 512, R), lambda r: XNr[0:R, r, :]])
            pool_rstd(g, c)
            meet(g, c)
            meet(g, c)
            pass_units(c, 39)
            meet(g, c)
            pool_rstd(g, c)
            meet(g, c)
            s = unit(g, c)
            for row in (lambda r: XNr[0:R, r, :], lambda r: U(s, 512, 1024, R), lambda r: U(s, 1024, 1536, R)):
                add_rows(Xr, row)
            meet(g, c)
            meet(g, c)
            pass_units(c, 6)
            linear_mix()
            pool_rstd(g, c)
            meet(g, c)
            pass_units(c, 9)
            pool_quantise(g, c)
            meet(g, c)
            pool_rstd(g, c)
            meet(g, c)
            pass_units(c, 2)
            s = unit(g, c)
            pass_units(c, 5)
            add_rows(Xr, lambda r: U(s, 512, 1024, R))
            meet(g, c)
            meet(g, c)
            linear_mix()
            pool_rstd(g, c)
            s = unit(g, c)
            pass_units(c, 4)
            meet(g, c)
            add_rows(Xr, lambda r: U(s, 0, 512, R))
            meet(g, c)
            meet(g, c)
            meet(g, c)
            meet(g, c)

        @block.tensor
        def _(pe):
            c = Counts()
            pe.wait_ge(consts_landed, CONSTS)
            meet(pe, c)
            zeros = XT[:, :].bitcast(BF16)

            pe.wait_ge(spans_ready, 1)
            for j in range(GC):
                mm = pe.transpose(PS[0:NG, 0, j * R:(j + 1) * R],
                                  edges_f[0:R, 1, :].rearrange("p (g j) -> p j g", j=GC)[:, j, :], ident[0:R, 0:R])
            mm.then_inc(spans_turned, 1)
            pe.wait_ge(spans_ready, 2)
            pe.transpose(PS[0:NW, 1, 0:NG], found[0:NG, 0:NW], ident[0:NG, 0:NG]).then_inc(spans_turned, 1)
            pe.wait_ge(spans_ready, 3)
            for k, rhs in enumerate((ident[0:NW, 0:NW], ident[0:NW, 0:NW], spans[0:NW, NW:2 * NW])):
                mm = pe.matmul(PS[0:1, 2, k * NW:(k + 1) * NW], found[0:NW, 140 + k:141 + k], rhs, start=True, stop=True)
            mm.then_inc(spans_turned, 1)
            pe.wait_ge(spans_ready, 4)
            for j in range(GC):
                pe.sem_inc(onehot_used[j], FAR + 1)
            for b in range(2):
                c.next(window_read[b])
            with repeat(pe, c, "window", NW // 2) as i:
                for b in range(2):
                    pe.wait_ge(window_read[b], c.now(window_read[b]))
                    c.next(window_read[b])
                    for q in range(3):
                        pe.matmul(PS[0:R, 3 * b + q, 0:2 * WC], zeros[0:R, 0:R], zeros[0:R, 0:2 * WC],
                                  start=True, stop=True)
                    first, past, off = window_range(pe, i * 2 + b)
                    with pe.Fori(first, past) as group:
                        for j in range(GC):
                            pe.wait_ge(onehot_ready, (group + off) * GC + (j + 1))
                            for q in range(NT):
                                mm = pe.matmul(PS[0:R, 3 * b + q // 2, q % 2 * WC:q % 2 * WC + WC],
                                               OH[0:R, j, q * R:(q + 1) * R], OK[0:R, j, :], start=False, stop=False,
                                               skip_group_check=True)
                            mm.then_inc(onehot_used[j], 1)
                    pe.drain().then_inc(window_filled[b], 1)
                    c.next(window_filled[b])
            meet(pe, c)

            for q in range(NT):
                pe.matmul(PS[0:R, q, 0:3 * EF], zeros[0:R, 0:R], zeros[0:R, 0:3 * EF], start=True, stop=True)
            for used in feat_used[0:CPI - 1] + fe_used:
                pe.sem_inc(used, 1)
                c.next(used)
            c.next(feat_split)
            with repeat(pe, c, "feature", NCH // FPI):
                for b in range(3):
                    pe.wait_ge(feat_split, c.next(feat_split))
                    for j in range(CPI):
                        pe.wait_ge(feat_onehot_ready, c.next(feat_onehot_ready))
                        for q in range(NT):
                            mm = pe.matmul(PS[0:R, q, 0:3 * EF], OHF[0:R, j, q * R:(q + 1) * R],
                                           FP[0:R, b, j, :, :].rearrange("p a e -> p (a e)"), start=False, stop=False,
                                           skip_group_check=True)
                        used = feat_used[j] if j < CPI - 1 else fe_used[b]
                        mm.then_inc(used, 1)
                        c.next(used)
            meet(pe, c)
            meet(pe, c)
            b = take_slot(pe, c)
            for j in range(NT):
                mm = pe.transpose(PS[0:EF, 2 * b + j // 3, j % 3 * R:(j % 3 + 1) * R], rest[0:R, j * EF:(j + 1) * EF],
                                  ident[0:R, 0:R])
            mm.then_inc(filled[b], 1)
            for r in range(NT):
                b = take_slot(pe, c)
                for j in range(NT):
                    mm = pe.transpose(PS[0:R, 2 * b + j // 3, j % 3 * R:(j % 3 + 1) * R],
                                      CNT[0:R, j, r * R:(r + 1) * R], ident[0:R, 0:R])
                mm.then_inc(filled[b], 1)
            meet(pe, c)

            def norm_T(src=XNr):
                pe_transpose_rows(pe, c, src)

            def linear_mix(krows):
                meet(pe, c)
                pe_linear_attend(pe, c, krows)
                meet(pe, c)
                pe_transpose_rows(pe, c, Ar, signalled=False)
                await_own_banks(pe, c)
                s = unit(pe, c)
                pe_project_rows(pe, c, [(s, KB)], YT)
                meet(pe, c)

            def qkv(src, krow):
                s = unit(pe, c)
                pe_project_T(pe, c, s, src, D, KB)
                s = unit(pe, c)
                if krow:
                    pe_project_rows(pe, c, [(s, KB)], src)
                else:
                    pe_project_T(pe, c, s, src, D, KB)
                s = unit(pe, c)
                pe_project_rows(pe, c, [(s, KB)], src)
                meet(pe, c)

            norm_T()
            meet(pe, c)
            sa, sbb = unit(pe, c), unit(pe, c)
            qkv(XTt, False)
            pe_attend(pe, c, 8, 64)
            meet(pe, c)
            pe_transpose_rows(pe, c, Ar, signalled=False)
            await_own_banks(pe, c)
            s = unit(pe, c)
            pe_project_rows(pe, c, [(s, KB)], YT)
            pe_transpose_rows(pe, c, Ar)
            await_own_banks(pe, c)
            pe_project_T(pe, c, sbb, YT, 128, 1, wo=516)
            await_own_slots(pe, c)
            pe_project_rows(pe, c, [(sbb, 1)], KT, wo=1028)
            meet(pe, c)
            release(pe, sa)
            release(pe, sbb)
            sc = unit(pe, c)
            meet(pe, c)
            qkv(XTt, False)
            for j in range(KB):
                for g in range(2):
                    b = take_slot(pe, c)
                    for h in range(2):
                        mm = pe.matmul(PS[:, 2 * b + h, 0:HALF], U(sc, 1036 + 128 * g, 1164 + 128 * g),
                                       QT[:, j, h * HALF:(h + 1) * HALF], start=True, stop=True)
                    mm.then_inc(filled[b], 1)
            for r in range(NT):
                for g in range(2, 4):
                    b = take_bank(pe, c)
                    for j in range(KB):
                        mm = pe.matmul(PS[0:R, 4 + b, j * 128:(j + 1) * 128], KT[:, j, r * R:(r + 1) * R],
                                       U(sc, 1036 + 128 * g, 1164 + 128 * g), start=True, stop=True)
                    mm.then_inc(bank_filled[b], 1)
            linear_mix(Gr)
            release(pe, sc)
            norm_T()
            meet(pe, c)
            sd = unit(pe, c)
            pe_gate(pe, c, sd)
            meet(pe, c)
            b = take_slot(pe, c)
            for r in range(NT):
                mm = pe.matmul(PS[0:8, 2 * b + r // 3, r % 3 * R:(r % 3 + 1) * R], combv[0:R, r, :],
                               ident[0:R, 0:R], start=True, stop=True)
            mm.then_inc(filled[b], 1)
            await_own_slots(pe, c)
            for r in range(NT):
                b = take_bank(pe, c)
                pe.matmul(PS[0:R, 4 + b, :], Pv[0:8, 0, r * R:(r + 1) * R], U(sd, 72, 584, 8),
                          start=True, stop=True).then_inc(bank_filled[b], 1)
            meet(pe, c)
            release(pe, sd)
            with repeat(pe, c, "expert0", 2):
                for e in range(4):
                    s = unit(pe, c)
                    pe_project_T(pe, c, s, XTt, D, KB)
                    await_own_slots(pe, c)
                    s = unit(pe, c)
                    pe_project_rows(pe, c, [(s, KB)], HT)
            meet(pe, c)
            norm_T()
            meet(pe, c)
            se = unit(pe, c)
            pe.wait_ge(z_ready, c.next(z_ready))
            b = take_slot(pe, c)
            for h in range(2):
                mm = pe.matmul(PS[0:16, 2 * b + h, 0:HALF], U(se, 0, 16, 64), emb[0:64, h * HALF:(h + 1) * HALF],
                               start=True, stop=True)
            mm.then_inc(filled[b], 1)
            await_own_slots(pe, c)
            b = take_slot(pe, c)
            for h in range(2):
                mm = pe.matmul(PS[0:16, 2 * b + h, 0:HALF], U(se, 16, 32, 16), Pv[0:16, 0, h * HALF:(h + 1) * HALF],
                               start=True, stop=True)
            mm.then_inc(filled[b], 1)
            meet(pe, c)
            release(pe, se)
            with repeat(pe, c, "block", NBLK):
                sf, sg = unit(pe, c), unit(pe, c)

                def condition(a):
                    for r in range(NT):
                        b = take_slot(pe, c)
                        for h in range(2):
                            mm = pe.matmul(PS[0:R, 2 * b + h, :], cond[0:17, r * R:(r + 1) * R],
                                           U(sg, (a + h) * D, (a + h + 1) * D, 17), start=True, stop=True)
                        mm.then_inc(filled[b], 1)
                    meet(pe, c)
                    pe_transpose_rows(pe, c, Ar, signalled=False)
                    await_own_banks(pe, c)

                condition(0)
                qkv(YT, False)
                pe_attend(pe, c, 4, 128)
                meet(pe, c)
                pe_transpose_rows(pe, c, Ar, signalled=False)
                await_own_banks(pe, c)
                s = unit(pe, c)
                pe_project_rows(pe, c, [(s, KB)], YT)
                condition(2)
                s = unit(pe, c)
                pe_project_T(pe, c, s, YT, D, KB)
                meet(pe, c)
                s = unit(pe, c)
                pe_project_rows(pe, c, [(s, KB)], QT)
                b = take_bank(pe, c)
                pe.sem_inc(bank_filled[b], 1)
                meet(pe, c)
                release(pe, sf)
                release(pe, sg)
            meet(pe, c)
            norm_T(Ar)
            await_own_banks(pe, c)
            sg, sh = unit(pe, c), unit(pe, c)
            qkv(YT, True)
            linear_mix(Kr)
            release(pe, sg)
            release(pe, sh)
            norm_T()
            meet(pe, c)
            si = unit(pe, c)
            pe_gate(pe, c, si)
            meet(pe, c)
            release(pe, si)
            with repeat(pe, c, "expert1", 2):
                for e in range(4):
                    for half in range(2):
                        s = unit(pe, c)
                        pe_project_T(pe, c, s, XTt, D, KB)
                    await_own_slots(pe, c)
                    s, s2 = unit(pe, c), unit(pe, c)
                    pe_project_rows(pe, c, [(s, KB), (s2, KB)], HT)
            for half in range(2):
                s, s2 = unit(pe, c), unit(pe, c)
                for o in range(KB):
                    pe_project_T(pe, c, s, XTt, D, 1, wo=o * 128)
                    pe_project_T(pe, c, s2, XTt, D, 1, wo=o * 128)
            await_own_slots(pe, c)
            s, s2 = unit(pe, c), unit(pe, c)
            pe_project_rows(pe, c, [(s, KB), (s2, KB)], HT)
            meet(pe, c)
            norm_T()
            meet(pe, c)
            sj = unit(pe, c)
            meet(pe, c)
            for o in range(KB):
                b = take_slot(pe, c)
                for h in range(2):
                    mm = pe.matmul(PS[:, 2 * b + h, 0:HALF], U(sj, o * 128, o * 128 + 128, EF),
                                   AGT[0:EF, h * HALF:(h + 1) * HALF], start=True, stop=True)
                mm.then_inc(filled[b], 1)
            await_own_slots(pe, c)
            s = unit(pe, c)
            pe_project_T(pe, c, s, YT, D, KB)
            await_own_slots(pe, c)
            s = unit(pe, c)
            pe_project_rows(pe, c, [(s, KB)], QT)
            meet(pe, c)
            release(pe, sj)
            qkv(XTt, True)
            linear_mix(Kr)
            norm_T()
            meet(pe, c)
            us = []
            for what, i in quantise_order():
                if what == "sum":
                    if i % KB == 0:
                        us.append(unit(pe, c))
                    pe.wait_ge(abs_ready, i + 1)
                    b = take_bank(pe, c)
                    at = (i + 1) % 2 * 512
                    pe.matmul(PS[:, 4 + b, :], ones[:, :], AB[:, at:at + 512], start=True,
                              stop=True).then_inc(bank_filled[b], 1)
                    continue
                u, o = divmod(i, 4)
                if o == 0:
                    pe.wait_ge(quantised, 4 * (u + 1))
                pe_project_T(pe, c, us[u], XTt, D, 1, wo=o % 2 * 256 + o // 2 * 128)
            pe.wait_ge(quantised, SUMS)
            await_own_slots(pe, c)
            pe_project_rows(pe, c, [(us[6], KB), (us[7], KB), (us[8], 3)], HT)
            meet(pe, c)
            norm_T()
            meet(pe, c)
            sa, sbb, sc = unit(pe, c), unit(pe, c), unit(pe, c)
            meet(pe, c)
            pe_project_T(pe, c, sa, XTt, 128, 1)
            for l in range(3):
                await_own_slots(pe, c)
                su, at = ((sa, 512), (sa, 1280), (sbb, 0))[l]
                for j in range(NT):
                    b = take_slot(pe, c)
                    for h in range(2):
                        mm = pe.matmul(PS[0:R, 2 * b + h, 0:384], YT[:, 0, j * R:(j + 1) * R],
                                       U(su, at + 384 * h, at + 384 * h + 384), start=True, stop=True)
                    mm.then_inc(filled[b], 1)
                await_own_slots(pe, c)
                for n, q in enumerate(load_order(l)):
                    if l == 0 or n >= 2:
                        pe.wait_ge(rel_landed[q % 2], c.next(rel_landed[q % 2], 16))
                    b = take_bank(pe, c)
                    for k in range(NREL):
                        for j in range(NT):
                            mm = pe.matmul(PS[:, 4 + b, 0:GW * WD].rearrange("p (w d) -> p w d", d=WD),
                                           REL[0:R, j, k * 128:(k + 1) * 128], CR[q % 2][0:R, :, j, k, :],
                                           start=(k == 0 and j == 0), stop=(k == NREL - 1 and j == NT - 1))
                    mm.then_inc(bank_filled[b], 1)
                for b in range(4):
                    pe.wait_ge(bank_drained[b], c.now(bank_drained[b]))
            await_own_slots(pe, c)
            pe_project_rows(pe, c, [(sbb, 1)], YT, nk=1, wo=768)
            s = unit(pe, c)
            pe_project_rows(pe, c, [(s, KB)], XTt)
            meet(pe, c)
            release(pe, sa)
            release(pe, sbb)
            release(pe, sc)
            qkv(XTt, True)
            linear_mix(Kr)
            norm_T()
            sd = unit(pe, c)
            meet(pe, c)
            meet(pe, c)
            qkv(YT, False)
            pe_attend_top(pe, c, 8, 64)
            meet(pe, c)
            pe_transpose_rows(pe, c, Ar, signalled=False)
            await_own_banks(pe, c)
            s = unit(pe, c)
            pe_project_rows(pe, c, [(s, KB)], YT)
            meet(pe, c)

        @block.scalar
        def _(act):
            c = Counts()
            act.wait_ge(consts_landed, CONSTS)
            meet(act, c)
            for b in range(2):
                act.sem_inc(window_read[b], 1)
                act.sem_inc(window_stored[b], 16)
                c.next(window_read[b])
                c.next(window_stored[b], 16)
                c.next(window_added[b])
            with repeat(act, c, "window", NW // 2) as i:
                for b in range(2):
                    act.wait_ge(window_stored[b], c.now(window_stored[b]))
                    act.wait_ge(window_added[b], c.now(window_added[b]))
                    act.wait_ge(window_filled[b], c.next(window_filled[b]))
                    c.next(window_added[b])
                    for q in range(3):
                        n = min(2, NT - 2 * q)
                        ins = act.activation(
                            stage[0:R, b, 2 * q:2 * q + n, :, :].rearrange("p q t d -> p q d t"),
                            PS[0:R, 3 * b + q, 0:n * WC].rearrange("p (q d t) -> p q d t", q=n, t=NREL), ACT.Copy)
                    ins.then_inc(window_read[b], 1)
                    act.wait_ge(window_read[b], c.next(window_read[b]))
                    act.dma_start(rel_dram[bass.ds(i * 2 + b, 1)].rearrange("w p c -> p (w c)"),
                                  biases[0:R, b * WS:(b + 1) * WS]).then_inc(window_stored[b], 16)
                    c.next(window_stored[b], 16)
            meet(act, c)
            with repeat(act, c, "feature", NCH // FPI):
                for b in range(3):
                    act.wait_ge(feat_left, c.next(feat_left))
                    act.activation(FP[0:R, b, :, 1, :], left_over, ACT.Copy).then_inc(feat_second, 1)
                    c.next(feat_second)
            for b in range(2):
                act.wait_ge(window_stored[b], c.now(window_stored[b]))
            meet(act, c)
            act.wait_ge(elu_neg, c.next(elu_neg))
            act.activation(CNT[0:R, :, :], CNT[0:R, :, :], ACT.Ln).then_inc(elu_exp, 1)
            c.next(elu_exp)
            meet(act, c)
            s = await_slot(act, c)
            act.activation(AGT[0:EF, 0:3 * R], PS[0:EF, 2 * s, 0:3 * R], ACT.Copy)
            act.activation(AGT[0:EF, 3 * R:N], PS[0:EF, 2 * s + 1, 0:2 * R], ACT.Copy).then_inc(drained[s], 1)
            for r in range(NT):
                s = await_slot(act, c)
                act.activation(B0[0:R, r, 0:3 * R], PS[0:R, 2 * s, 0:3 * R], ACT.Copy)
                act.activation(B0[0:R, r, 3 * R:N], PS[0:R, 2 * s + 1, 0:2 * R], ACT.Copy).then_inc(drained[s], 1)
            meet(act, c)

            def norm_T(dst=XTt):
                act_drain_transposed(act, c, dst)

            def column(s, at):
                return lambda o: U(s, at + o, at + o + 1)

            def qkv(krow, qbias=None, kbias=None, scale=(None, None)):
                f = ACT.Copy if qbias is None else ACT.Identity
                s = unit(act, c)
                act_drain_T(act, c, halves(QT), f, KB, bias=qbias, scale=scale[0], freed=s)
                s = unit(act, c)
                if krow:
                    pass_banks(c, NT)
                else:
                    act_drain_T(act, c, halves(KT), f, KB, bias=kbias, scale=scale[1], freed=s)
                pass_units(c, 1)
                pass_banks(c, NT)
                meet(act, c)

            def linear_mix(scale=1.0):
                meet(act, c)
                act_linear_attend(act, c, scale)
                meet(act, c)
                act_drain_transposed(act, c, YT)
                pass_units(c, 1)
                pass_banks(c, NT)
                meet(act, c)

            def elu_maps():
                act_elu(act, c, Y0[:, 0:KB * NP])
                act_elu(act, c, A0[0:R, 0:NT * D])

            norm_T()
            meet(act, c)
            sa, sbb = unit(act, c), unit(act, c)
            qkv(False)
            act_attend(act, c, 8)
            pass_banks(c, NT)
            meet(act, c)
            act_drain_transposed(act, c, YT)
            pass_units(c, 1)
            pass_banks(c, NT)
            act_drain_transposed(act, c, YT)
            act_drain_T(act, c, halves(KT), ACT.Relu, 1, bias=column(sbb, 512))
            pass_banks(c, NT)
            meet(act, c)
            sc = unit(act, c)
            meet(act, c)
            qkv(False, qbias=lambda o: wts[:, o:o + 1], kbias=lambda o: wts[:, 4 + o:5 + o],
                scale=(U(sc, 1032, 1033), U(sc, 1034, 1035)))
            for j in range(KB):
                s = await_slot(act, c)
                act.activation(TMP[:, j % 2, :].rearrange("p (h n) -> p h n", h=2), slot_ap(s),
                               ACT.Copy).then_inc(drained[s], 1)
                pass_slots(c, 1)
                act.wait_ge(drained[1 - s], c.now(drained[1 - s]))
                act.activation(QT[:, j, :], YT[:, j, :], ACT.Square, scale=0.125)
            for r in range(NT):
                b = await_bank(act, c)
                act.activation(TMP[0:R, r % 2, 0:D], PS[0:R, 4 + b, :], ACT.Copy).then_inc(bank_drained[b], 1)
                pass_banks(c, 1)
                act.wait_ge(bank_drained[(b + 1) % 4], c.now(bank_drained[(b + 1) % 4]))
                act.activation(Gr[0:R, r, :], Ar[0:R, r, :], ACT.Square, scale=0.125)
            linear_mix()
            norm_T()
            meet(act, c)
            sd = unit(act, c)
            pass_banks(c, 1)
            act.activation(kept[:, 0:32], U(sd, 40, 72), ACT.Copy)
            act_gate(act, c)
            meet(act, c)
            s = await_slot(act, c)
            act.activation(Pv[0:8, 0, 0:3 * R], PS[0:8, 2 * s, 0:3 * R], ACT.Copy)
            act.activation(Pv[0:8, 0, 3 * R:N], PS[0:8, 2 * s + 1, 0:2 * R], ACT.Copy).then_inc(drained[s], 1)
            pass_banks(c, NT)
            meet(act, c)
            with repeat(act, c, "expert0", 2) as i:
                for e in range(4):
                    s = unit(act, c)
                    act_drain_T(act, c, halves(HT), ACT.Gelu, KB, freed=s,
                                bias=lambda o: kept[:, bass.ds(i * 16 + (e * 4 + o), 1)])
                    pass_units(c, 1)
                    pass_banks(c, NT)
            meet(act, c)
            norm_T()
            meet(act, c)
            se = unit(act, c)
            act.wait_ge(elu_neg, c.next(elu_neg))
            act.activation(emb[0:64, :], emb[0:64, :], ACT.Sin).then_inc(z_ready, 1)
            c.next(z_ready)
            s = await_slot(act, c)
            act.activation(Pv[0:16, 0, :].rearrange("p (h n) -> p h n", h=2), slot_ap(s, 16), ACT.Silu,
                           bias=U(se, 32, 33, 16)).then_inc(drained[s], 1)
            s = await_slot(act, c)
            act.activation(cond[0:16, :].rearrange("p (h n) -> p h n", h=2), slot_ap(s, 16), ACT.Identity,
                           bias=U(se, 33, 34, 16)).then_inc(drained[s], 1)
            meet(act, c)
            with repeat(act, c, "block", NBLK):
                sf, sg = unit(act, c), unit(act, c)
                pass_slots(c, NT)
                meet(act, c)
                act_drain_transposed(act, c, YT)
                qkv(False, qbias=column(sf, 1536), kbias=column(sf, 1540))
                act_attend(act, c, 4)
                pass_banks(c, NT)
                meet(act, c)
                act_drain_transposed(act, c, YT)
                pass_units(c, 1)
                pass_banks(c, NT)
                pass_slots(c, NT)
                meet(act, c)
                act_drain_transposed(act, c, YT)
                s = unit(act, c)
                act_drain_T(act, c, halves(QT), ACT.Relu, KB, bias=column(sf, 1544), freed=s)
                meet(act, c)
                pass_units(c, 1)
                pass_banks(c, NT)
                b = await_bank(act, c)
                act.sem_inc(bank_drained[b], 1)
                meet(act, c)
            meet(act, c)
            act_drain_transposed(act, c, YT)
            sg, sh = unit(act, c), unit(act, c)
            qkv(True, qbias=column(sh, 512))
            elu_maps()
            linear_mix()
            norm_T()
            meet(act, c)
            pass_units(c, 1)
            pass_banks(c, 1)
            act_gate(act, c)
            meet(act, c)
            with repeat(act, c, "expert1", 2):
                for e in range(4):
                    for half in range(2):
                        s = unit(act, c)
                        act_drain_T(act, c, lambda o: halves(HT)(4 * half + o), ACT.Silu, KB, freed=s)
                    pass_units(c, 2)
                    pass_banks(c, NT)
            for o in range(2 * KB):
                s = await_slot(act, c)
                act.activation(halves(HT)(o), slot_ap(s), ACT.Silu).then_inc(drained[s], 1)
                pass_slots(c, 1)
            pass_units(c, 6)
            pass_banks(c, NT)
            meet(act, c)
            norm_T()
            meet(act, c)
            sj = unit(act, c)
            meet(act, c)
            act_drain_T(act, c, halves(YT), ACT.Copy, KB)
            s = unit(act, c)
            act_drain_T(act, c, halves(QT), ACT.Relu, KB, bias=column(sj, 1536), freed=s)
            pass_units(c, 1)
            pass_banks(c, NT)
            meet(act, c)
            qkv(True)
            elu_maps()
            linear_mix(0.125)
            norm_T()
            meet(act, c)

            for what, i in quantise_order():
                if what == "sum":
                    if i % KB == 0:
                        s = unit(act, c)
                    if i >= 2:
                        act.wait_ge(quantised, i - 1)
                    k = i % KB
                    w, at = U(s, k * D, (k + 1) * D), (i + 1) % 2 * 512
                    act.activation(SG[:, at:at + 512], w, ACT.Sign)
                    act.activation(AB[:, at:at + 512], w, ACT.Abs).then_inc(abs_ready, 1)
                    pass_banks(c, 1)
                elif i % 2 == 0:
                    b = await_slot(act, c)
                    act.activation(halves(HT)(i // 2), slot_ap(b), ACT.Silu).then_inc(drained[b], 1)
                else:
                    pass_slots(c, 1)
            pass_banks(c, NT)
            meet(act, c)
            norm_T()
            meet(act, c)
            sa, sbb, sc = unit(act, c), unit(act, c), unit(act, c)
            meet(act, c)
            act_drain_T(act, c, halves(YT), ACT.Relu, 1, bias=column(sbb, 1792))
            def load(q):
                act.dma_start(loads[q % 2][0:R, :].rearrange("p (w c) -> p w c", w=GW),
                              rel_dram[q * GW:(q + 1) * GW].rearrange("w p c -> p w c")
                              ).then_inc(rel_landed[q % 2], 16)

            for l in range(3):
                if l == 0:
                    load(0)
                    load(1)
                for j in range(NT):
                    s = await_slot(act, c)
                    act.activation(REL[0:R, j, :].rearrange("p (h n) -> p h n", h=2),
                                   PS[0:R, 2 * s:2 * s + 2, 0:384], ACT.Copy).then_inc(drained[s], 1)
                for n, q in enumerate(load_order(l)):
                    b = await_bank(act, c)
                    if n < 2:
                        load((q + 2) % 4)
                    cols = min(GW * WD, NP - q * GW * WD)
                    act.activation(YT[:, 0, q * GW * WD:q * GW * WD + cols], PS[:, 4 + b, 0:cols], ACT.Relu,
                                   bias=column(sbb, 1793 + l)(0)).then_inc(bank_drained[b], 1)
            pass_banks(c, NT)
            pass_units(c, 1)
            pass_banks(c, NT)
            meet(act, c)
            qkv(True)
            elu_maps()
            linear_mix()
            norm_T()
            sd = unit(act, c)
            meet(act, c)
            meet(act, c)
            qkv(False, qbias=column(sd, 528), kbias=column(sd, 532))
            act_attend_top(act, c, 8, 512.0 ** -0.5)
            pass_banks(c, NT)
            meet(act, c)
            act_drain_transposed(act, c, YT, bias=column(sd, 536))
            pass_units(c, 1)
            pass_banks(c, NT)
            meet(act, c)
            act.dma_start(out.rearrange("(r p) d -> p r d", p=R), Xr[0:R, :, :]).then_inc(out_stored, 16)
            act.wait_ge(out_stored, 16)

        @block.vector
        def _(v):
            c = Counts()
            v.memset(arena[:, 0:2 * TB], 0.0)
            v.wait_ge(consts_landed, CONSTS)
            for a in range(3):
                v.tensor_copy(edges_f[0:R, a, :], edges_i[0:R, a * NCH:(a + 1) * NCH])
            meet(v, c)

            def step(ins):
                ins.then_inc(dve_step, 1)
                v.wait_ge(dve_step, c.next(dve_step))

            v.scalar_tensor_tensor(out=edges_f[0:R, 2, :], in0=edges_f[0:R, 1, :], scalar=float(NREL),
                                   in1=edges_f[0:R, 2, :], op0=ALU.mult, op1=ALU.add).then_inc(spans_ready, 1)
            v.wait_ge(spans_turned, 1)
            most, least, both = found[0:NG, 120:121], found[0:NG, 121:122], found[0:NG, 0:NW]
            step(v.tensor_reduce(most, PS[0:NG, 0, 0:GC * R], AX.X, ALU.max))
            step(v.tensor_reduce(least, PS[0:NG, 0, 0:GC * R], AX.X, ALU.min))
            step(v.tensor_scalar(found[0:NG, 40:40 + NW], spans[0:NG, 0:NW], most, None, ALU.is_le))
            step(v.tensor_scalar(both, spans[0:NG, 0:NW], float(WD - 1), least, ALU.add, ALU.is_ge))
            v.tensor_tensor(both, both, found[0:NG, 40:40 + NW], ALU.mult).then_inc(spans_ready, 1)
            v.wait_ge(spans_turned, 2)
            ends = found[0:NW, 64:64 + NG]
            first, past, steps = (found[0:NW, k:k + 1] for k in (140, 141, 142))
            step(v.scalar_tensor_tensor(out=ends, in0=iota[0:NW, 0:NG], scalar=-float(NG), in1=PS[0:NW, 1, 0:NG],
                                        op0=ALU.add, op1=ALU.mult))
            step(v.tensor_reduce(first, ends, AX.X, ALU.min))
            step(v.tensor_scalar(first, first, float(NG), float(NG - 1), ALU.add, ALU.min))
            step(v.scalar_tensor_tensor(out=ends, in0=iota[0:NW, 0:NG], scalar=1.0, in1=PS[0:NW, 1, 0:NG],
                                        op0=ALU.add, op1=ALU.mult))
            step(v.tensor_reduce(past, ends, AX.X, ALU.max))
            step(v.scalar_tensor_tensor(out=past, in0=first, scalar=1.0, in1=past, op0=ALU.add, op1=ALU.max))
            v.tensor_tensor(steps, past, first, ALU.subtract).then_inc(spans_ready, 1)
            v.wait_ge(spans_turned, 3)
            row = found[0:1, 0:3 * NW]
            step(v.tensor_copy(row, PS[0:1, 2, 0:3 * NW]))
            step(v.scalar_tensor_tensor(out=row[:, 2 * NW:3 * NW], in0=row[:, 2 * NW:3 * NW], scalar=float(FAR),
                                        in1=row[:, 0:NW], op0=ALU.add, op1=ALU.subtract))
            v.tensor_copy(ranges[0:1, :], row).then_inc(spans_ready, 1)
            v.wait_ge(spans_ready, 4)
            v.sem_inc(onehot_ready, GC * FAR)
            with repeat(v, c, "window", NW // 2) as i:
                for b in range(2):
                    anchor(v)
                    v.tensor_scalar(wkey[0:R, b, :], edges_f[0:R, 2, :], spans[0:R, bass.ds(2 * NW + i * 2 + b, 1)],
                                    None, ALU.subtract).then_inc(key_ready, 1)
                    v.wait_ge(key_ready, c.next(key_ready))
                    anchor(v)
                    first, past, off = window_range(v, i * 2 + b)
                    with v.Fori(first, past) as group:
                        for j in range(GC):
                            v.wait_ge(onehot_used[j], group + off + 1)
                            anchor(v)
                            v.tensor_scalar(OH[0:R, j, :], iota[0:R, :], edges_f[0:R, 0, bass.ds(group * GC + j, 1)],
                                            None, ALU.is_equal)
                            v.tensor_scalar(OK[0:R, j, :], iota[0:R, 0:WC], wkey[0:R, b, bass.ds(group * GC + j, 1)],
                                            None, ALU.is_equal).then_inc(onehot_ready, 1)
            anchor(v)
            meet(v, c)
            for used in feat_used[0:CPI - 1] + fe_used:
                c.next(used)
            with repeat(v, c, "feature", NCH // FPI) as i:
                for b in range(3):
                    v.wait_ge(feat_landed[b], c.next(feat_landed[b], 16))
                    anchor(v)
                    v.tensor_copy(FP[0:R, b, :, 0, :], FE[0:R, b, :].rearrange("p (j e) -> p j e", j=CPI)
                                  ).then_inc(feat_first, 1)
                    c.next(feat_first)
                    for j in range(CPI):
                        if j == 2:
                            v.wait_ge(feat_second, c.next(feat_second))
                            anchor(v)
                            v.tensor_tensor(FP[0:R, b, :, 2, :], left_over, FP[0:R, b, :, 1, :],
                                            ALU.subtract).then_inc(feat_split, 1)
                            c.next(feat_split)
                        if j < CPI - 1:
                            v.wait_ge(feat_used[j], c.now(feat_used[j]))
                            c.next(feat_used[j])
                        else:
                            p = fe_used[(b - 1) % 3]
                            v.wait_ge(p, c.at(p, c.k.get(p.name, 0)))
                            c.next(fe_used[b])
                        anchor(v)
                        v.tensor_scalar(OHF[0:R, j, :], iota[0:R, :], edges_f[0:R, 0, bass.ds(i * FPI + (b * CPI + j), 1)],
                                        None, ALU.is_equal).then_inc(feat_onehot_ready, 1)
                        c.next(feat_onehot_ready)
            meet(v, c)
            v.tensor_reduce(rest[0:R, :].rearrange("p (q e) -> p q e", q=NT),
                            PS[0:R, 0:NT, 0:3 * EF].rearrange("p q (a e) -> p q e a", a=3), AX.X, ALU.add)
            v.tensor_scalar(CNT[0:R, :, :], TOT[0:R, :, :], 1.0, None, ALU.max).then_inc(elu_neg, 1)
            c.next(elu_neg)
            v.tensor_scalar(TOT[0:R, :, :], TOT[0:R, :, :], 1.0, -MASKED, ALU.min, ALU.mult).then_inc(dve_step, 1)
            v.wait_ge(dve_step, c.next(dve_step))
            v.tensor_scalar(TOT[0:R, :, :], TOT[0:R, :, :], MASKED, None, ALU.add).then_inc(dve_step, 1)
            v.wait_ge(dve_step, c.next(dve_step))
            v.wait_ge(elu_exp, c.next(elu_exp))
            v.scalar_tensor_tensor(out=B1[0:R, :, :], in0=CNT[0:R, :, :], scalar=float(np.sqrt(128.0)),
                                   in1=TOT[0:R, :, :], op0=ALU.mult, op1=ALU.add)
            v.scalar_tensor_tensor(out=CNT[0:R, :, :], in0=CNT[0:R, :, :], scalar=8.0,
                                   in1=TOT[0:R, :, :], op0=ALU.mult, op1=ALU.add)
            meet(v, c)
            pass_slots(c, NT + 1)
            meet(v, c)

            def norm_X(stats=False):
                dve_norm(v, c, Xr, XNr, stats=stats)
                pass_banks(c, NT)

            def qkv_tail(krow, kbias=None, vbias=None, values=True):
                pass_units(c, 1)
                pass_slots(c, KB)
                s = unit(v, c)
                if krow:
                    row = None if kbias is None else (lambda r: kbias)
                    dve_drain_rows(v, c, lambda r: Kr[0:R, r, :], row=row, freed=(s,))
                else:
                    pass_slots(c, KB)
                s = unit(v, c)
                if values:
                    dve_values(v, c, s, bias=vbias)
                else:
                    row = None if vbias is None else (lambda r: vbias)
                    dve_drain_rows(v, c, lambda r: V[0:R, r, 0:D], row=row, freed=(s,))
                meet(v, c)

            def linear_mix(guard):
                meet(v, c)
                dve_linear_attend(v, c, guard)
                meet(v, c)
                pass_banks(c, NT)
                s = unit(v, c)
                dve_accumulate(v, c, Xr, (s,), stats=True)
                meet(v, c)

            def elu_maps():
                dve_elu(v, c, Q0[:, 0:KB * NP], Y0[:, 0:KB * NP], 128)
                dve_elu(v, c, K0[0:R, 0:NT * D], A0[0:R, 0:NT * D], R)

            norm_X(stats=True)
            meet(v, c)
            sa, sbb = unit(v, c), unit(v, c)
            qkv_tail(False, values=False)
            dve_attend(v, c, 8, 64, B0, 0.125)
            meet(v, c)
            pass_banks(c, NT)
            s = unit(v, c)
            dve_accumulate(v, c, Ar, (s,), row=XNr, stats=True)
            await_own_banks(v, c)
            dve_norm(v, c, Ar, Ar, gain=U(sa, 0, 512, R), shift=U(sa, 512, 1024, R), stats=False, signal=rows_ready)
            pass_banks(c, NT)
            await_own_banks(v, c)
            for r in range(NT):
                v.tensor_tensor(Ar[0:R, r, :], Ar[0:R, r, :], U(sbb, 0, 512, R), ALU.add).then_inc(dve_step, 1)
                c.next(dve_step)
            v.wait_ge(dve_step, c.now(dve_step))
            pass_slots(c, 1)
            dve_accumulate(v, c, Ar, (), stats=True)
            await_own_banks(v, c)
            dve_norm(v, c, Ar, Ar, gain=U(sa, 1024, 1536, R), shift=U(sa, 1536, 2048, R), stats=False,
                     signal=dve_step)
            v.wait_ge(dve_step, c.now(dve_step))
            for r in range(NT):
                v.tensor_tensor(Xr[0:R, r, :], Xr[0:R, r, :], Ar[0:R, r, :], ALU.add)
            meet(v, c)
            sc = unit(v, c)
            for a in range(2):
                v.tensor_scalar(wts[:, 4 * a:4 * a + 4], U(sc, 1024 + 4 * a, 1028 + 4 * a),
                                U(sc, 1032 + 2 * a, 1033 + 2 * a), U(sc, 1033 + 2 * a, 1034 + 2 * a),
                                ALU.mult, ALU.add)
            meet(v, c)
            qkv_tail(False, vbias=U(sc, 0, 512, R))
            for j in range(KB):
                b = c.slot % 2
                pass_slots(c, 1)
                v.wait_ge(drained[b], c.now(drained[b]))
                s = await_slot(v, c)
                v.tensor_tensor(halves(YT)(j), slot_ap(s), TMP[:, j % 2, :].rearrange("p (h n) -> p h n", h=2),
                                ALU.mult).then_inc(drained[s], 1)
            for r in range(NT):
                b = c.bank % 4
                pass_banks(c, 1)
                v.wait_ge(bank_drained[b], c.now(bank_drained[b]))
                b = await_bank(v, c)
                v.tensor_tensor(Ar[0:R, r, :], PS[0:R, 4 + b, :], TMP[0:R, r % 2, 0:D],
                                ALU.mult).then_inc(bank_drained[b], 1)
            linear_mix((ALU.add, 1.0e-6))
            norm_X()
            meet(v, c)
            sd = unit(v, c)
            dve_gate(v, c, row=U(sd, 32, 40, R))
            meet(v, c)
            pass_slots(c, 1)
            dve_accumulate(v, c, Xr, ())
            meet(v, c)
            with repeat(v, c, "expert0", 2) as i:
                for e in range(4):
                    pass_units(c, 1)
                    pass_slots(c, KB)
                    s = unit(v, c)
                    dve_expert(v, c, lambda r: combv[0:R, r, bass.ds(i * 4 + e, 1)], (s,))
            meet(v, c)
            norm_X(stats=True)
            meet(v, c)
            se = unit(v, c)
            dve_embedding(v, c, se)
            for r in range(NT):
                v.tensor_copy(Gr[0:R, r, :], XNr[0:R, r, :])
            pass_slots(c, 2)
            meet(v, c)
            with repeat(v, c, "block", NBLK):
                sf, sg = unit(v, c), unit(v, c)
                dve_norm(v, c, Gr, Ar, cond=True)
                meet(v, c)
                pass_banks(c, NT)
                qkv_tail(False, vbias=U(sf, 1024, 1536, R), values=False)
                dve_attend(v, c, 4, 128, B1, 128.0 ** -0.5)
                meet(v, c)
                pass_banks(c, NT)
                s = unit(v, c)
                dve_accumulate(v, c, Gr, (s,), stats=True)
                await_own_banks(v, c)
                dve_norm(v, c, Gr, Ar, cond=True, stats=False)
                meet(v, c)
                pass_banks(c, NT)
                pass_units(c, 1)
                pass_slots(c, KB)
                meet(v, c)
                s = unit(v, c)
                dve_accumulate(v, c, Gr, (s,))
                pass_banks(c, 1)
                meet(v, c)
            for r in range(NT):
                v.tensor_tensor(Xr[0:R, r, :], Xr[0:R, r, :], Gr[0:R, r, :], ALU.add)
            meet(v, c)
            sg, sh = unit(v, c), unit(v, c)
            dve_norm(v, c, XNr, Ar, gain=U(sg, 0, 512, R), shift=U(sg, 512, 1024, R), signal=rows_ready)
            pass_banks(c, NT)
            qkv_tail(True, kbias=U(sg, 1024, 1536, R), vbias=U(sg, 1536, 2048, R))
            elu_maps()
            linear_mix((ALU.add, 1.0e-8))
            norm_X()
            meet(v, c)
            pass_units(c, 1)
            dve_gate(v, c)
            meet(v, c)
            with repeat(v, c, "expert1", 2) as i:
                for e in range(4):
                    pass_units(c, 2)
                    pass_slots(c, 2 * KB)
                    s, s2 = unit(v, c), unit(v, c)
                    dve_expert(v, c, lambda r: combv[0:R, r, bass.ds(i * 4 + e, 1)], (s, s2))
            for half in range(2):
                s, s2 = unit(v, c), unit(v, c)
                dve_gated(v, c, range(4 * half, 4 * half + 4), (s, s2))
            s, s2 = unit(v, c), unit(v, c)
            dve_accumulate(v, c, Xr, (s, s2), stats=True)
            meet(v, c)
            norm_X()
            meet(v, c)
            pass_units(c, 1)
            meet(v, c)
            pass_slots(c, 2 * KB)
            pass_units(c, 1)
            s = unit(v, c)
            dve_accumulate(v, c, Xr, (s,))
            meet(v, c)
            qkv_tail(True)
            elu_maps()
            linear_mix(None)
            norm_X()
            meet(v, c)
            us = []
            for what, i in quantise_order():
                if what == "sum":
                    if i % KB == 0:
                        us.append(unit(v, c))
                    b = await_bank(v, c)
                    at = (i + 1) % 2 * 512
                    if i >= 2:
                        v.wait_ge(quantised, i - 1)
                    sc, q = SC[:, at:at + 512], QZ[:, at:at + 512]
                    v.tensor_scalar(sc, PS[:, 4 + b, :], 1.0 / 128, 1.0e-5, ALU.mult,
                                    ALU.add).then_inc(bank_drained[b], 1)
                    v.wait_ge(bank_drained[b], c.now(bank_drained[b]))
                    v.scalar_tensor_tensor(out=q, in0=sc, scalar=0.5, in1=AB[:, at:at + 512], op0=ALU.mult,
                                           op1=ALU.is_lt).then_inc(dve_step, 1)
                    v.wait_ge(dve_step, c.next(dve_step))
                    v.tensor_tensor(q, q, sc, ALU.mult).then_inc(scaled, 1)
                elif i % 2 == 1:
                    dve_gated(v, c, (i // 2,), (us[i // 4],) if i % 4 == 3 or i == 2 * FB - 1 else ())
            dve_accumulate(v, c, Xr, (us[6], us[7], us[8]), stats=True)
            meet(v, c)
            norm_X()
            meet(v, c)
            sa, sbb, sc = unit(v, c), unit(v, c), unit(v, c)
            meet(v, c)
            pass_slots(c, 1 + 3 * NT)
            pass_banks(c, 3 * NW // GW)
            for row, free in ((U(sbb, 1280, 1792, R), False), (U(sc, 0, 512, R), True)):
                s = unit(v, c) if free else None
                for r in range(NT):
                    b = await_bank(v, c)
                    if free and r == NT - 1:
                        release(v, s)
                    tmp = P[0:R, r % 2 * 512:r % 2 * 512 + 512]
                    v.tensor_tensor(tmp, PS[0:R, 4 + b, :], row, ALU.add).then_inc(bank_drained[b], 1)
                    v.wait_ge(bank_drained[b], c.now(bank_drained[b]))
                    v.scalar_tensor_tensor(out=Xr[0:R, r, :], in0=tmp, scalar=0.0, in1=Xr[0:R, r, :],
                                           op0=ALU.max, op1=ALU.add).then_inc(dve_step, 1)
                    c.next(dve_step)
                v.wait_ge(dve_step, c.now(dve_step))
            meet(v, c)
            qkv_tail(True)
            elu_maps()
            linear_mix((ALU.max, 1.0e-4))
            norm_X()
            sd = unit(v, c)
            meet(v, c)
            for k in range(KB):
                y, x = YT[:, k, 0:N], XTt[:, k, 0:N]
                w = [U(sd, 512 + 3 * k + j, 513 + 3 * k + j) for j in range(3)]

                def settle(ins):
                    ins.then_inc(dve_step, 1)
                    v.wait_ge(dve_step, c.next(dve_step))

                settle(v.tensor_scalar(y, x, w[1], U(sd, 524 + k, 525 + k), ALU.mult, ALU.add))
                settle(v.scalar_tensor_tensor(out=y[:, 1:N], in0=x[:, 0:N - 1], scalar=w[0], in1=y[:, 1:N],
                                              op0=ALU.mult, op1=ALU.add))
                settle(v.scalar_tensor_tensor(out=y[:, 0:N - 1], in0=x[:, 1:N], scalar=w[2], in1=y[:, 0:N - 1],
                                              op0=ALU.mult, op1=ALU.add))
                v.tensor_tensor(y, y, x, ALU.add)
            meet(v, c)
            qkv_tail(False, values=False)
            dve_attend_top(v, c, 8, 64, 512.0 ** -0.5)
            meet(v, c)
            pass_banks(c, NT)
            s = unit(v, c)
            dve_accumulate(v, c, Xr, (s,))
            meet(v, c)


UNITS = {"edges": 0, "l0a": 11, "l0f": 17, "l1a": 39, "l1f": 39, "l2a": 7, "l2f": 9, "l3a": 8, "l3f": 5}


def blocks_of(w, k=None):
    w = np.asarray(w)
    return w.reshape(-1, 128, w.shape[1]).transpose(1, 0, 2).reshape(128, -1)


def columns_of(b):
    return np.asarray(b).reshape(-1, 128).T


def row_of(b):
    return np.broadcast_to(np.asarray(b).reshape(1, -1), (128, np.asarray(b).size))


def below(*parts):
    parts = [np.asarray(p) for p in parts]
    u = np.zeros((128, parts[0].shape[1]), np.float32)
    at = 0
    for p in parts:
        u[at:at + len(p)] = p
        at += len(p)
    return u


def diagonal(g):
    u = np.zeros((128, 128), np.float32)
    u[0:64, 0:64] = g
    u[64:128, 64:128] = g
    return u


def units_of(a):
    out = []

    def put(*parts):
        u = np.zeros((128, UC), np.float32)
        at = 0
        for p in parts:
            u[:, at:at + p.shape[1]] = p
            at += p.shape[1]
        assert at <= UC
        out.append(u)

    def mats(*ws):
        for w in ws:
            put(blocks_of(w))

    g = lambda layer: (lambda n: np.asarray(a[f"{layer}_{n}"]))
    w = g("L0_gnn")
    put(row_of(w("ln1_g")), row_of(w("ln1_b")), row_of(w("ln2_g")), row_of(w("ln2_b")))
    put(row_of(w("b2")), columns_of(w("b1")), np.zeros((128, 3), np.float32), blocks_of(w("W1")), blocks_of(w("W2")))
    mats(w("Wq"), w("Wk"), w("Wv"), w("Wo"))
    w = g("L0_mix")
    put(row_of(w("bv")), row_of(w("bp")), columns_of(w("bq")), columns_of(w("bk")), row_of(w("gamma_q")),
        row_of(w("beta_q")), row_of(w("gamma_k")), row_of(w("beta_k")),
        diagonal(w("qG1")), diagonal(w("qG2")), diagonal(w("kG1")), diagonal(w("kG2")))
    mats(w("Wq"), w("Wk"), w("Wv"), w("Wp"))
    w = g("L0_ffn")
    put(blocks_of(w("Wg")), row_of(w("bg")), columns_of(w("b1")), below(w("b2")))
    for e in range(NEXP):
        mats(w("W1")[e], w("W2")[e])
    w = g("L1_gnn")
    freqs = np.arange(1, 33, dtype=np.float32) * np.float32(2.0 * np.pi / 16)
    turn = np.zeros((64, 1), np.float32)
    turn[32:] = np.float32(np.pi / 2)
    put(below(w("f_w1")), below(w("f_w2")), below(w("f_b1")[:, None]), below(w("f_b2")[:, None]),
        below(freqs[:, None], freqs[:, None]), below(turn))
    for i in range(NBLK):
        put(row_of(w("bo")[i]), row_of(w("m_b2")[i]), row_of(w("bv")[i]), columns_of(w("bq")[i]),
            columns_of(w("bk")[i]), columns_of(w("m_b1")[i]))
        put(*[below(w(f"{n}_w")[i], w(f"{n}_b")[i][None]) for n in ("s1", "b1", "s2", "b2")])
        mats(*[w(n)[i] for n in ("wq", "wk", "wv", "wo", "m_w1", "m_w2")])
    w = g("L1_mix")
    qkv, b = w("qkv_w").T, w("qkv_b")
    put(row_of(w("ln_gamma")), row_of(w("ln_beta")), row_of(b[D:2 * D]), row_of(b[2 * D:]))
    put(row_of(w("out_b")), columns_of(b[0:D]))
    mats(qkv[:, 0:D], qkv[:, D:2 * D], qkv[:, 2 * D:], w("out_w").T)
    w = g("L1_ffn")
    put(blocks_of(w("gate_w").T))
    for e in range(NEXP):
        w1, w2 = w("w1")[e].T, w("w2")[e].T
        mats(w1[:, 0:D], w1[:, D:], w2[0:D], w2[D:])
    for h in range(2):
        mats(w("sg_gate").T[:, h * D:(h + 1) * D], w("sg_up").T[:, h * D:(h + 1) * D])
    mats(w("sg_down").T[0:D], w("sg_down").T[D:])
    w = g("L2_gnn")
    put(below(w("W_edge"), w("b_edge")[None]), row_of(w("b2")), row_of(a["L2_mix_b_proj"]), columns_of(w("b1")))
    mats(w("W1"), w("W2"))
    w = g("L2_mix")
    qkv = w("w_qkv").T
    mats(qkv[:, 0:D], qkv[:, D:2 * D], qkv[:, 2 * D:], w("w_proj").T)
    w = g("L2_ffn")
    wg, wu, wd = w("w_gate").T, w("w_up").T, w("w_down").T
    for u in range(6):
        m = np.zeros((D, 512), np.float32)
        n = 256 if u < 5 else 128
        m[:, 0:n] = wg[:, u * 256:u * 256 + n]
        m[:, 256:256 + n] = wu[:, u * 256:u * 256 + n]
        mats(m)
    mats(wd[0:D], wd[D:2 * D], wd[2 * D:])
    w = g("L3_gnn")
    rel = lambda n: w(n).transpose(1, 0, 2).reshape(128, NREL * 128)
    put(blocks_of(w("W_lower")), rel("W1"), rel("W2"))
    put(rel("W3"), w("W_upper"), row_of(w("b_upper")), *[columns_of(w(n)) for n in ("b_lower", "b1", "b2", "b3")])
    put(row_of(w("b_skip")), row_of(a["L3_mix_b_out"]))
    mats(w("W_skip"))
    w = g("L3_mix")
    qkv = w("W_qkv").T
    mats(qkv[:, 0:D], qkv[:, D:2 * D], qkv[:, 2 * D:], w("W_out").T)
    w = g("L3_ffn")
    b = w("qkv_b")
    put(row_of(w("wo_b")), w("pos_w").reshape(KB, 128, 3).transpose(1, 0, 2).reshape(128, 3 * KB),
        columns_of(w("pos_b")), columns_of(b[0:D]), columns_of(b[D:2 * D]), columns_of(b[2 * D:]))
    qkv = w("qkv_w").T
    mats(qkv[:, 0:D], qkv[:, D:2 * D], qkv[:, 2 * D:], w("wo_w").T)
    assert len(out) == sum(UNITS.values())
    return np.stack(out)


def arrays_of(a):
    ids = np.stack([np.asarray(a[n]).reshape(NCH, R).T for n in ("src", "dst", "edge_type_6")], 1)
    feats = np.ones((E, EF), np.float32)
    feats[:, 0:64] = np.asarray(a["edge_attr_64"])
    feats[:, 64:96] = np.asarray(a["edge_attr_32"])
    window = np.arange(NW, dtype=np.float32)
    spans = np.zeros((128, 3, NW), np.float32)
    spans[:, 0], spans[:, 2] = WD * window, WC * window
    spans[0:NW, 1] = np.triu(np.ones((NW, NW)), 1)
    spans = spans.reshape(128, 3 * NW)
    return {
        "x": np.asarray(a["x"]),
        "edges": np.ascontiguousarray(ids.reshape(R, 3 * NCH)),
        "feats": np.ascontiguousarray(feats.reshape(NCH // CPI, CPI, R, EF).transpose(0, 2, 1, 3)
                                      .reshape(NCH // CPI, R, CPI * EF)),
        "noise": np.ascontiguousarray(np.broadcast_to(np.asarray(a["node_vec1"]).reshape(1, N), (64, N))),
        "units": units_of(a),
        "ident": np.eye(128, dtype=np.float32),
        "iota": np.ascontiguousarray(np.broadcast_to(np.arange(NP, dtype=np.float16), (R, NP))),
        "iota8": np.ascontiguousarray(np.broadcast_to(np.arange(8, dtype=np.float32), (128, 8))),
        "spans": spans,
    }


def kernel(**inputs):
    import concourse.bacc as bacc
    from concourse.bass_utils import run_bass_kernel_spmd

    arrays = arrays_of(inputs)
    nc = bacc.Bacc("TRN2", target_bir_lowering=False, num_devices=1)
    t = {n: nc.dram_tensor(f"in_{n}", x.shape, mybir.dt.from_np(x.dtype), kind="ExternalInput").ap()
         for n, x in arrays.items()}
    out = nc.dram_tensor("out", (N, D), F32, kind="ExternalOutput").ap()
    gps_network(nc, t, out, sum(UNITS.values()))
    r = run_bass_kernel_spmd(nc, [{f"in_{n}": x for n, x in arrays.items()}], core_ids=[0])
    return r.results[0]["out"]
```
